# Optimizing a Trainium2 kernel written in Bass

```python
import numpy as np
import jax
import jax.numpy as jnp

def _softmax(x, axis=-1):
    return jax.nn.softmax(x, axis=axis)

def _gelu(x):
    return jax.nn.gelu(x, approximate=True)

def _silu(x):
    return jax.nn.silu(x)

def _sigmoid(x):
    return jax.nn.sigmoid(x)

def _layernorm(x, axis=-1, eps=1e-05):
    m = jnp.mean(x, axis=axis, keepdims=True)
    v = jnp.var(x, axis=axis, keepdims=True)
    return (x - m) / jnp.sqrt(v + eps)

def _scatter_add(tgt, idx, src, axis=0):
    return tgt.at[idx].add(src)

def _segment_sum(src, seg, n):
    return jax.ops.segment_sum(src, seg, n)
kernel_name = 'mk_lm_tower_d2_tok_ids256_r4_3a710b'

def setup_inputs(seed: int=0):
    np.random.seed(seed)
    _w = jnp.asarray

    def _rec_inputs():
        import jax
        import jax.numpy as jnp
        _rk = jax.random.key(seed)
        x = jax.random.randint(jax.random.fold_in(_rk, 1), (4, 1024), 0, 64, jnp.int32)
        fside_BS_continuous_positions = jax.random.uniform(jax.random.fold_in(_rk, 21), (4, 1024), jnp.float32, 0.0, 0.999927)
        return (x, fside_BS_continuous_positions)
    x, fside_BS_continuous_positions = _rec_inputs()

    def _L0_tok_setup():
        import jax, jax.numpy as jnp
        import numpy as np
        N_SCALES = 4

        def _conv1d(x, w, b, pad):
            y = jax.lax.conv_general_dilated(x, w, window_strides=(1,), padding=[(pad, pad)], dimension_numbers=('NCH', 'OIH', 'NCH'))
            return y + b[None, :, None]
        key = jax.random.key(seed)
        ks = jax.random.split(key, 12)
        B, S, P, D = (8, 512, 512, 64)
        byte_sequence = jax.random.randint(ks[0], (B, S), 0, 64, dtype=jnp.int64)
        continuous_positions = jax.random.uniform(ks[1], (B, P), dtype=jnp.float32)
        emb = jax.random.normal(ks[2], (64, D), dtype=jnp.float32)
        locality_shapes = jax.random.normal(ks[3], (64, 4), dtype=jnp.float32)
        w1 = jax.random.normal(ks[4], (128, 64, 7), dtype=jnp.float32) * 0.02
        b1 = jnp.zeros((128,), dtype=jnp.float32)
        w2 = jax.random.normal(ks[5], (64, 128, 5), dtype=jnp.float32) * 0.02
        b2 = jnp.zeros((64,), dtype=jnp.float32)
        w3 = jax.random.normal(ks[6], (1, 64, 3), dtype=jnp.float32) * 0.02
        b3 = jnp.zeros((1,), dtype=jnp.float32)
        multiscale_widths = jnp.array([0.01, 0.02, 0.05, 0.1], dtype=jnp.float32)
        scale_weights = jnp.ones((4,), dtype=jnp.float32)
        return {'byte_sequence': byte_sequence, 'continuous_positions': continuous_positions, 'emb': emb, 'locality_shapes': locality_shapes, 'w1': w1, 'b1': b1, 'w2': w2, 'b2': b2, 'w3': w3, 'b3': b3, 'multiscale_widths': multiscale_widths, 'scale_weights': scale_weights}
    _L0_tok_all = _L0_tok_setup()
    _L0_tok_in = {k: v for k, v in _L0_tok_all.items() if k in ('emb', 'locality_shapes', 'w1', 'b1', 'w2', 'b2', 'w3', 'b3', 'multiscale_widths', 'scale_weights')}
    del _L0_tok_all

    def _L0_attn_setup():
        import jax, jax.numpy as jnp
        import numpy as np
        import math
        N_SEQ, L_RES, D_MODEL = (128, 96, 64)
        N_HEAD, C_HEAD = (8, 32)
        EPS = 1e-05
        key = jax.random.key(seed)
        ks = jax.random.split(key, 8)
        s = 1.0 / math.sqrt(D_MODEL)
        return {'m': jax.random.normal(ks[0], (N_SEQ, L_RES, D_MODEL), jnp.float32), 'gamma': jnp.ones((D_MODEL,), jnp.float32), 'beta': jnp.zeros((D_MODEL,), jnp.float32), 'Wq': jax.random.normal(ks[1], (D_MODEL, N_HEAD * C_HEAD), jnp.float32) * s, 'Wk': jax.random.normal(ks[2], (D_MODEL, N_HEAD * C_HEAD), jnp.float32) * s, 'Wv': jax.random.normal(ks[3], (D_MODEL, N_HEAD * C_HEAD), jnp.float32) * s, 'Wg': jax.random.normal(ks[4], (D_MODEL, N_HEAD * C_HEAD), jnp.float32) * s, 'bg': jnp.zeros((N_HEAD * C_HEAD,), jnp.float32), 'Wo': jax.random.normal(ks[5], (N_HEAD * C_HEAD, D_MODEL), jnp.float32) * s, 'bo': jnp.zeros((D_MODEL,), jnp.float32)}
    _L0_attn_all = _L0_attn_setup()
    _L0_attn_in = {k: v for k, v in _L0_attn_all.items() if k in ('gamma', 'beta', 'Wq', 'Wk', 'Wv', 'Wg', 'bg', 'Wo', 'bo')}
    del _L0_attn_all

    def _L0_ffn_setup():
        import jax, jax.numpy as jnp
        import numpy as np
        B, K, D = (128, 16, 64)
        E = 32
        H = int(D * 0.25)
        key = jax.random.key(seed)
        ks = jax.random.split(key, 7)
        d_rs = D ** (-0.5)
        h_rs = H ** (-0.5)
        x = jax.random.normal(ks[0], (B, K, D), dtype=jnp.float32)
        router_w = jax.random.uniform(ks[1], (E, D), jnp.float32, -d_rs, d_rs)
        router_b = jax.random.uniform(ks[2], (E,), jnp.float32, -d_rs, d_rs)
        W1 = jax.random.uniform(ks[3], (E, D, H), jnp.float32, -h_rs, h_rs)
        b1 = jax.random.uniform(ks[4], (E, H), jnp.float32, -h_rs, h_rs)
        W2 = jax.random.uniform(ks[5], (E, H, D), jnp.float32, -d_rs, d_rs)
        b2 = jax.random.uniform(ks[6], (E, D), jnp.float32, -d_rs, d_rs)
        return {'x': x, 'router_w': router_w, 'router_b': router_b, 'W1': W1, 'b1': b1, 'W2': W2, 'b2': b2}
    _L0_ffn_all = _L0_ffn_setup()
    _L0_ffn_in = {k: v for k, v in _L0_ffn_all.items() if k in ('router_w', 'router_b', 'W1', 'b1', 'W2', 'b2')}
    del _L0_ffn_all

    def _L1_attn_setup():
        import jax, jax.numpy as jnp
        import numpy as np
        B, L, H, N, NLAYERS = (16, 512, 64, 64, 4)
        PRENORM = True

        def layer_norm(z, scale, bias, eps=1e-05):
            mu = jnp.mean(z, axis=-1, keepdims=True)
            var = jnp.var(z, axis=-1, keepdims=True)
            return (z - mu) * jax.lax.rsqrt(var + eps) * scale + bias

        def s4_block(u, log_dt, Alog, Aim, Cre, Cim, D, Wout, bout):
            Lq = u.shape[-1]
            dt = jnp.exp(log_dt)[:, None]
            A = -jnp.exp(Alog) + 1j * Aim
            C = Cre + 1j * Cim
            dtA = A * dt
            Cd = C * (jnp.exp(dtA) - 1.0) / A
            vand = jnp.exp(dtA[:, :, None] * jnp.arange(Lq))
            K = 2.0 * jnp.real(jnp.einsum('hn,hnl->hl', Cd, vand))
            n = 2 * Lq
            y = jnp.fft.irfft(jnp.fft.rfft(u, n=n) * jnp.fft.rfft(K, n=n), n=n)[..., :Lq]
            y = y + D[:, None] * u
            y = jax.nn.gelu(y)
            z = jnp.einsum('oh,bhl->bol', Wout, y) + bout[None, :, None]
            z1, z2 = jnp.split(z, 2, axis=1)
            return z1 * jax.nn.sigmoid(z2)
        key = jax.random.key(seed)
        ks = jax.random.split(key, 8)
        x = jax.random.normal(ks[0], (B, L, H), jnp.float32)
        log_dt = jnp.log(10.0 ** jax.random.uniform(ks[1], (NLAYERS, H), minval=-3.0, maxval=-1.0)).astype(jnp.float32)
        Alog = jnp.log(0.5 * jnp.ones((NLAYERS, H, N), jnp.float32))
        Aim = jnp.broadcast_to(np.pi * jnp.arange(N, dtype=jnp.float32), (NLAYERS, H, N)).copy()
        Cre = jax.random.normal(ks[2], (NLAYERS, H, N), jnp.float32) * 0.5 ** 0.5
        Cim = jax.random.normal(ks[3], (NLAYERS, H, N), jnp.float32) * 0.5 ** 0.5
        D = jax.random.normal(ks[4], (NLAYERS, H), jnp.float32)
        Wout = jax.random.normal(ks[5], (NLAYERS, 2 * H, H), jnp.float32) / jnp.sqrt(jnp.float32(H))
        bout = jnp.zeros((NLAYERS, 2 * H), jnp.float32)
        ln_scale = jnp.ones((NLAYERS, H), jnp.float32)
        ln_bias = jnp.zeros((NLAYERS, H), jnp.float32)
        return dict(x=x, log_dt=log_dt, Alog=Alog, Aim=Aim, Cre=Cre, Cim=Cim, D=D, Wout=Wout, bout=bout, ln_scale=ln_scale, ln_bias=ln_bias)
    _L1_attn_all = _L1_attn_setup()
    _L1_attn_in = {k: v for k, v in _L1_attn_all.items() if k in ('log_dt', 'Alog', 'Aim', 'Cre', 'Cim', 'D', 'Wout', 'bout', 'ln_scale', 'ln_bias')}
    del _L1_attn_all

    def _L1_ffn_setup():
        import jax, jax.numpy as jnp
        import numpy as np
        D_MODEL = 64
        EXPERT_DIM = 128
        NUM_EXPERTS = 8
        TOP_K = 2
        SEQ_LEN = 512
        BATCH = 2
        key = jax.random.key(seed)
        ks = jax.random.split(key, 8)
        s = 0.02
        x = jax.random.normal(ks[0], (SEQ_LEN, BATCH, D_MODEL), dtype=jnp.float32)
        Wg = jax.random.normal(ks[1], (D_MODEL, NUM_EXPERTS), dtype=jnp.float32) * s
        bg = jax.random.normal(ks[2], (NUM_EXPERTS,), dtype=jnp.float32) * s
        bias = jnp.zeros((NUM_EXPERTS,), dtype=jnp.float32)
        W1 = jax.random.normal(ks[3], (NUM_EXPERTS, D_MODEL, EXPERT_DIM), dtype=jnp.float32) * s
        b1 = jax.random.normal(ks[4], (NUM_EXPERTS, EXPERT_DIM), dtype=jnp.float32) * s
        W2 = jax.random.normal(ks[5], (NUM_EXPERTS, EXPERT_DIM, D_MODEL), dtype=jnp.float32) * s
        b2 = jax.random.normal(ks[6], (NUM_EXPERTS, D_MODEL), dtype=jnp.float32) * s
        return {'x': x, 'Wg': Wg, 'bg': bg, 'bias': bias, 'W1': W1, 'b1': b1, 'W2': W2, 'b2': b2}
    _L1_ffn_all = _L1_ffn_setup()
    _L1_ffn_in = {k: v for k, v in _L1_ffn_all.items() if k in ('Wg', 'bg', 'bias', 'W1', 'b1', 'W2', 'b2')}
    del _L1_ffn_all
    return {'x': x, 'fside_BS_continuous_positions': fside_BS_continuous_positions, 'L0_tok_emb': _L0_tok_in['emb'], 'L0_tok_locality_shapes': _L0_tok_in['locality_shapes'], 'L0_tok_w1': _L0_tok_in['w1'], 'L0_tok_b1': _L0_tok_in['b1'], 'L0_tok_w2': _L0_tok_in['w2'], 'L0_tok_b2': _L0_tok_in['b2'], 'L0_tok_w3': _L0_tok_in['w3'], 'L0_tok_b3': _L0_tok_in['b3'], 'L0_tok_multiscale_widths': _L0_tok_in['multiscale_widths'], 'L0_tok_scale_weights': _L0_tok_in['scale_weights'], 'L0_attn_gamma': _L0_attn_in['gamma'], 'L0_attn_beta': _L0_attn_in['beta'], 'L0_attn_Wq': _L0_attn_in['Wq'], 'L0_attn_Wk': _L0_attn_in['Wk'], 'L0_attn_Wv': _L0_attn_in['Wv'], 'L0_attn_Wg': _L0_attn_in['Wg'], 'L0_attn_bg': _L0_attn_in['bg'], 'L0_attn_Wo': _L0_attn_in['Wo'], 'L0_attn_bo': _L0_attn_in['bo'], 'L0_ffn_router_w': _L0_ffn_in['router_w'], 'L0_ffn_router_b': _L0_ffn_in['router_b'], 'L0_ffn_W1': _L0_ffn_in['W1'], 'L0_ffn_b1': _L0_ffn_in['b1'], 'L0_ffn_W2': _L0_ffn_in['W2'], 'L0_ffn_b2': _L0_ffn_in['b2'], 'L1_attn_log_dt': _L1_attn_in['log_dt'], 'L1_attn_Alog': _L1_attn_in['Alog'], 'L1_attn_Aim': _L1_attn_in['Aim'], 'L1_attn_Cre': _L1_attn_in['Cre'], 'L1_attn_Cim': _L1_attn_in['Cim'], 'L1_attn_D': _L1_attn_in['D'], 'L1_attn_Wout': _L1_attn_in['Wout'], 'L1_attn_bout': _L1_attn_in['bout'], 'L1_attn_ln_scale': _L1_attn_in['ln_scale'], 'L1_attn_ln_bias': _L1_attn_in['ln_bias'], 'L1_ffn_Wg': _L1_ffn_in['Wg'], 'L1_ffn_bg': _L1_ffn_in['bg'], 'L1_ffn_bias': _L1_ffn_in['bias'], 'L1_ffn_W1': _L1_ffn_in['W1'], 'L1_ffn_b1': _L1_ffn_in['b1'], 'L1_ffn_W2': _L1_ffn_in['W2'], 'L1_ffn_b2': _L1_ffn_in['b2']}

def reference(x, fside_BS_continuous_positions, L0_tok_emb, L0_tok_locality_shapes, L0_tok_w1, L0_tok_b1, L0_tok_w2, L0_tok_b2, L0_tok_w3, L0_tok_b3, L0_tok_multiscale_widths, L0_tok_scale_weights, L0_attn_gamma, L0_attn_beta, L0_attn_Wq, L0_attn_Wk, L0_attn_Wv, L0_attn_Wg, L0_attn_bg, L0_attn_Wo, L0_attn_bo, L0_ffn_router_w, L0_ffn_router_b, L0_ffn_W1, L0_ffn_b1, L0_ffn_W2, L0_ffn_b2, L1_attn_log_dt, L1_attn_Alog, L1_attn_Aim, L1_attn_Cre, L1_attn_Cim, L1_attn_D, L1_attn_Wout, L1_attn_bout, L1_attn_ln_scale, L1_attn_ln_bias, L1_ffn_Wg, L1_ffn_bg, L1_ffn_bias, L1_ffn_W1, L1_ffn_b1, L1_ffn_W2, L1_ffn_b2):
    import jax
    import jax.numpy as jnp

    def _L0_tok_ref(byte_sequence, continuous_positions, emb, locality_shapes, w1, b1, w2, b2, w3, b3, multiscale_widths, scale_weights):
        import jax, jax.numpy as jnp
        import numpy as np
        N_SCALES = 4

        def _conv1d(x, w, b, pad):
            y = jax.lax.conv_general_dilated(x, w, window_strides=(1,), padding=[(pad, pad)], dimension_numbers=('NCH', 'OIH', 'NCH'))
            return y + b[None, :, None]
        B, S = byte_sequence.shape
        P = continuous_positions.shape[1]
        amps = emb[byte_sequence]
        onehot = jax.nn.one_hot(byte_sequence, 64, dtype=jnp.float32)
        onehot = jnp.transpose(onehot, (0, 2, 1))
        h = jax.nn.gelu(_conv1d(onehot, w1, b1, 3), approximate=False)
        h = jax.nn.gelu(_conv1d(h, w2, b2, 2), approximate=False)
        ctx = jax.nn.sigmoid(_conv1d(h, w3, b3, 1))[:, 0, :]
        amps = amps * ctx[:, :, None]
        lp = locality_shapes[byte_sequence]
        byte_pos = jnp.linspace(0.0, 1.0, S, dtype=jnp.float32)
        center = byte_pos[None, :] + lp[..., 0] * 0.05
        xd = continuous_positions[:, None, :] - center[..., None]
        amp_scale = jax.nn.sigmoid(lp[..., 2])
        phase = lp[..., 3] * jnp.pi
        abs_w = jnp.abs(lp[..., 1])
        TWO_PI = 2.0 * jnp.pi
        basis_total = jnp.zeros((B, S, P), dtype=jnp.float32)
        for s in range(N_SCALES):
            width = abs_w * multiscale_widths[s] + 1e-05
            z = xd / width[..., None]
            basis = jnp.exp(-0.5 * z * z) * jnp.cos(phase[..., None] + TWO_PI * z)
            basis_total = basis_total + basis * (amp_scale[..., None] * scale_weights[s] ** 2)
        semantic_field = jnp.einsum('bsp,bsd->bpd', basis_total, amps)
        return semantic_field

    def _L0_attn_ref(m, gamma, beta, Wq, Wk, Wv, Wg, bg, Wo, bo):
        import jax, jax.numpy as jnp
        import numpy as np
        import math
        N_SEQ, L_RES, D_MODEL = (128, 96, 64)
        N_HEAD, C_HEAD = (8, 32)
        EPS = 1e-05
        N, L, D = m.shape
        H, C = (N_HEAD, C_HEAD)
        mu = jnp.mean(m, axis=-1, keepdims=True)
        var = jnp.mean(jnp.square(m - mu), axis=-1, keepdims=True)
        mn = (m - mu) * jax.lax.rsqrt(var + EPS) * gamma + beta
        q = (mn @ Wq).reshape(N, L, H, C)
        k = (mn @ Wk).reshape(N, L, H, C)
        v = (mn @ Wv).reshape(N, L, H, C)
        g = jax.nn.sigmoid(mn @ Wg + bg).reshape(N, L, H, C)
        scale = 1.0 / math.sqrt(C) / math.sqrt(L)
        att = jnp.einsum('slhc,tlhc->sth', q, k) * scale
        att = jax.nn.softmax(att, axis=1)
        o = jnp.einsum('sth,tlhc->slhc', att, v) * g
        return o.reshape(N, L, H * C) @ Wo + bo

    def _L0_ffn_ref(x, router_w, router_b, W1, b1, W2, b2):
        import jax, jax.numpy as jnp
        import numpy as np
        B, K, D = (128, 16, 64)
        E = 32
        H = int(D * 0.25)
        xf = x.reshape(-1, D)
        logits = xf @ router_w.T + router_b
        idx = jnp.argmax(logits, axis=-1)
        w1t = jnp.take(W1, idx, axis=0)
        h = jnp.einsum('nd,ndh->nh', xf, w1t) + jnp.take(b1, idx, axis=0)
        h = jax.nn.relu(h)
        w2t = jnp.take(W2, idx, axis=0)
        out = jnp.einsum('nh,nhd->nd', h, w2t) + jnp.take(b2, idx, axis=0)
        out = jax.nn.relu(out)
        return out.reshape(x.shape)

    def _L1_attn_ref(x, log_dt, Alog, Aim, Cre, Cim, D, Wout, bout, ln_scale, ln_bias):
        import jax, jax.numpy as jnp
        import numpy as np
        B, L, H, N, NLAYERS = (16, 512, 64, 64, 4)
        PRENORM = True

        def layer_norm(z, scale, bias, eps=1e-05):
            mu = jnp.mean(z, axis=-1, keepdims=True)
            var = jnp.var(z, axis=-1, keepdims=True)
            return (z - mu) * jax.lax.rsqrt(var + eps) * scale + bias

        def s4_block(u, log_dt, Alog, Aim, Cre, Cim, D, Wout, bout):
            Lq = u.shape[-1]
            dt = jnp.exp(log_dt)[:, None]
            A = -jnp.exp(Alog) + 1j * Aim
            C = Cre + 1j * Cim
            dtA = A * dt
            Cd = C * (jnp.exp(dtA) - 1.0) / A
            vand = jnp.exp(dtA[:, :, None] * jnp.arange(Lq))
            K = 2.0 * jnp.real(jnp.einsum('hn,hnl->hl', Cd, vand))
            n = 2 * Lq
            y = jnp.fft.irfft(jnp.fft.rfft(u, n=n) * jnp.fft.rfft(K, n=n), n=n)[..., :Lq]
            y = y + D[:, None] * u
            y = jax.nn.gelu(y)
            z = jnp.einsum('oh,bhl->bol', Wout, y) + bout[None, :, None]
            z1, z2 = jnp.split(z, 2, axis=1)
            return z1 * jax.nn.sigmoid(z2)
        h = jnp.swapaxes(x, -1, -2)
        for i in range(NLAYERS):
            z = h
            if PRENORM:
                z = jnp.swapaxes(layer_norm(jnp.swapaxes(z, -1, -2), ln_scale[i], ln_bias[i]), -1, -2)
            z = s4_block(z, log_dt[i], Alog[i], Aim[i], Cre[i], Cim[i], D[i], Wout[i], bout[i])
            h = z + h
            if not PRENORM:
                h = jnp.swapaxes(layer_norm(jnp.swapaxes(h, -1, -2), ln_scale[i], ln_bias[i]), -1, -2)
        return jnp.swapaxes(h, -1, -2)

    def _L1_ffn_ref(x, Wg, bg, bias, W1, b1, W2, b2):
        import jax, jax.numpy as jnp
        import numpy as np
        D_MODEL = 64
        EXPERT_DIM = 128
        NUM_EXPERTS = 8
        TOP_K = 2
        SEQ_LEN = 512
        BATCH = 2
        x_flat = x.reshape(-1, D_MODEL)
        gate_logits = x_flat @ Wg + bg + bias
        topk_vals, topk_idx = jax.lax.top_k(gate_logits, TOP_K)
        topk_w = jax.nn.softmax(topk_vals, axis=-1)
        combine = (jax.nn.one_hot(topk_idx, NUM_EXPERTS, dtype=x.dtype) * topk_w[..., None]).sum(axis=1)
        h = jax.nn.relu(jnp.einsum('td,edh->teh', x_flat, W1) + b1)
        y = jnp.einsum('teh,ehd->ted', h, W2) + b2
        out = jnp.einsum('ted,te->td', y, combine)
        return out.reshape(x.shape)
    h = _L0_tok_ref(x, fside_BS_continuous_positions, L0_tok_emb, L0_tok_locality_shapes, L0_tok_w1, L0_tok_b1, L0_tok_w2, L0_tok_b2, L0_tok_w3, L0_tok_b3, L0_tok_multiscale_widths, L0_tok_scale_weights)
    h = h + _L0_attn_ref(_layernorm(h, axis=-1), L0_attn_gamma, L0_attn_beta, L0_attn_Wq, L0_attn_Wk, L0_attn_Wv, L0_attn_Wg, L0_attn_bg, L0_attn_Wo, L0_attn_bo)
    h = h + _L0_ffn_ref(_layernorm(h, axis=-1), L0_ffn_router_w, L0_ffn_router_b, L0_ffn_W1, L0_ffn_b1, L0_ffn_W2, L0_ffn_b2)
    h = h + _L1_attn_ref(_layernorm(h, axis=-1), L1_attn_log_dt, L1_attn_Alog, L1_attn_Aim, L1_attn_Cre, L1_attn_Cim, L1_attn_D, L1_attn_Wout, L1_attn_bout, L1_attn_ln_scale, L1_attn_ln_bias)
    h = h + _L1_ffn_ref(_layernorm(h, axis=-1), L1_ffn_Wg, L1_ffn_bg, L1_ffn_bias, L1_ffn_W1, L1_ffn_b1, L1_ffn_W2, L1_ffn_b2)
    return h

_drawn_inputs = setup_inputs


def setup_inputs(seed=0):
    import zlib

    import numpy as np

    out = dict(_drawn_inputs(seed))
    spreads = {'L0_tok_b1': (0.0, 0.8),
     'L0_tok_b2': (0.0, 0.8),
     'L0_tok_scale_weights': (1.0, 0.2),
     'L0_attn_gamma': (1.0, 0.2),
     'L0_attn_beta': (0.0, 0.1),
     'L0_attn_bg': (0.0, 0.696),
     'L0_attn_bo': (0.0, 0.1),
     'L1_attn_Alog': (-0.6931471824645996, 0.6),
     'L1_attn_bout': (0.0, 0.1),
     'L1_attn_ln_scale': (1.0, 0.2),
     'L1_attn_ln_bias': (0.0, 0.1),
     'L1_ffn_bias': (0.0, 0.8)}
    factors = {'L0_tok_w1': 8.0,
     'L0_tok_w2': 8.0,
     'L0_tok_w3': 8.0,
     'L0_ffn_router_b': 2.984,
     'L0_ffn_b1': 8.0,
     'L0_ffn_b2': 4.19,
     'L1_ffn_Wg': 8.0,
     'L1_ffn_bg': 8.0,
     'L1_ffn_W1': 8.0,
     'L1_ffn_b1': 8.0,
     'L1_ffn_W2': 8.0,
     'L1_ffn_b2': 8.0}
    for name, (base, spread) in spreads.items():
        noise = np.random.default_rng([zlib.crc32(name.encode()), seed]).standard_normal(out[name].shape)
        drawn = base * np.exp(spread * noise) if base else spread * noise
        out[name] = jnp.asarray(drawn.astype(out[name].dtype))
    for name, factor in factors.items():
        out[name] = (out[name] * factor).astype(out[name].dtype)
    return out
```

```python
from contextlib import ExitStack

import concourse.bass as bass
from concourse import mybir

F32 = mybir.dt.float32
I32 = mybir.dt.int32
ALU = mybir.AluOpType
ACT = mybir.ActivationFunctionType
AX = mybir.AxisListType

P = 128
B, L, D = 4, 1024, 64
NT = L // P
SC = 4
NH, CH = 8, 32
HC = NH * CH
E0, H0 = 32, 16
NL, N = 4, 64
E1, H1 = 8, 128
EPS = 1e-5
MANT = 23
ONE_BITS = 0x3F800000
ROUND = 1.5 * 2.0 ** 23
BIG = 2.0 ** 100
CHUNKS = 4
HCH = D // CHUNKS

C_ID, C_T, C_BP, C_PC, C_DESC, C_PH, C_LO, C_HI, C_BIG, C_N3PI = 0, 128, 256, 264, 265, 297, 298, 426, 554, 586
C_ALL = 588
C_J = C_ALL


def tower_kernel(nc, a):
    ctx = ExitStack()
    with ctx:
        def sb(name, shape, dt=F32):
            return ctx.enter_context(nc.sbuf_tensor(name, shape, dt))

        def sem(name):
            return ctx.enter_context(nc.semaphore(name))

        def dram(ap, offset, pattern):
            return bass.AP(tensor=ap.tensor, offset=ap.offset + offset, ap=pattern)

        p_dram = nc.dram_tensor("mode_tables", [NL, P, D * P], F32, kind="Internal").ap()
        v_dram = nc.dram_tensor("mode_tables_t", [NL, P, D * P], F32, kind="Internal").ap()
        k_dram = nc.dram_tensor("taps", [NL, 2 * P, D], F32, kind="Internal").ap()

        y_dram = nc.dram_tensor("conv_out", [D, 32, P], F32, kind="Internal").ap()

        big = sb("big", [P, 4 * 8192])
        cst = sb("cst", [P, C_ALL])
        ht = sb("ht", [P, NT, B, D])
        amp = sb("amp", [P, B * NT, 68])
        pos = sb("pos", [P, B, L])
        xd = sb("xd", [P, 2, 2, L])
        xq = sb("xq", [P, 2, 2, L])
        ampw = sb("ampw", [P, 2, 2, SC, D])
        prm = sb("prm", [P, B, NT, 17])
        prb = sb("prb", [P, 2, NT, 17])
        ctxp = sb("ctxp", [P, B * NT])
        la = sb("la", [P, 4, NL, 32])
        lnw = sb("lnw", [P, 6, 32])

        def cut(off, *shape, parts=P, dt=F32):
            n = 1
            for s in shape:
                n *= s
            v = big[0:parts, off:off + n]
            if dt is not F32:
                v = v.bitcast(dt)
            if len(shape) == 1:
                return v
            names = "abcde"[:len(shape)]
            return v.rearrange(f"p ({' '.join(names)}) -> p {' '.join(names)}",
                               **{k: s for k, s in zip(names[1:], shape[1:])})

        ident = cst[:, C_ID:C_ID + P]
        trow = cst[:, C_T:C_T + P]
        n3pi = cst[:, C_N3PI:C_N3PI + 1]

        pe_t = cut(0, D, P)
        ph_t = cut(8192, D, P)
        ph_i = cut(8192, D * P, dt=I32)
        o = 16384
        xb = cut(o, 1032, dt=I32); o += 1032
        oh = cut(o, 1032); o += 1032
        h1 = cut(o, 1028); o += 1028
        h2 = cut(o, 1026, parts=64); o += 1026
        w1r = cut(o, 448); o += 448
        w2r = cut(o, 640, parts=64); o += 640
        w3r = cut(o, 192, parts=1); o += 192
        w1t = cut(o, 4, P); o += 512
        w2t = cut(o, 5, D); o += 320
        w3t = cut(o, 3, parts=64); o += 4
        el = cut(o, 68, parts=64); o += 68
        b1c = cut(o, 1); o += 1
        b2c = cut(o, 1); o += 1
        b3c = cut(o, 1); o += 1
        msc = cut(o, SC); o += SC
        swc = cut(o, SC); o += SC
        ldt = cut(o, 2); o += 2
        dtc = cut(o, 2); o += 2
        row = cut(o, 26, 2, N); o += 26 * 2 * N
        tin = cut(o, 7, 2, 2, N); o += 7 * 4 * N
        rt = cut(o, 3, NL, D); o += 3 * NL * D
        rs = cut(o, 3, D); o += 3 * D
        kt = cut(o, D); o += D
        post = cut(o, 16, B * NT, SC); o += 16 * 32 * SC
        zk = cut(o, D); o += D
        drow = cut(o, NL, D, parts=1); o += NL * D
        assert o <= 32768, o

        eb = [cut(0, 2, SC, L), cut(8192, 2, SC, L)]
        qb = [cut(16384, 2, SC, L), cut(24576, 2, SC, L)]
        qi = [cut(16384, 8 * L, dt=I32), cut(24576, 8 * L, dt=I32)]
        accs = sb("accs", [P, 512])

        mn = cut(0, NT, B, D)
        mnt = cut(2048, 2, L)
        xc = cut(4096, 32, D)
        sq = cut(6144, 32, D)
        gr = cut(8192, 2, HC)
        wqkvg = cut(8704, 4, HC)
        rr = cut(9728, 8, HC)
        r2 = cut(11776, 8, NH)
        att = cut(11840, 2, 2, 2, 2, NH)
        amx = cut(11968, 4, 32); 
        wvs = cut(12288, 2, 2, 2, HC)
        gt = cut(16384, 2, B, L)
        wo = cut(24576, 2, D)
        bgc = cut(24704, 2)
        gbc = cut(24706, 3, D)

        xn = cut(0, 32, D)
        x96 = cut(8192, 32, P)
        oht = cut(12288, 32, P, parts=32)
        hm = cut(16384, 2, 4, 512)
        f0 = cut(20480, 512)
        lg = cut(21000, 32, E0)
        o1 = cut(22024, 32, E0)
        o2 = cut(23048, 32, E0)
        rwr = cut(26000, D, parts=32)
        rwt = cut(24960, E0, parts=64)
        rbb = cut(24992, E0)
        w1x = cut(25024, 4, P, parts=96)
        b1x = cut(25536, 4)
        w2x = cut(25540, 4, D)
        b2x = cut(25796, D, parts=32)

        vt = cut(0, D, P)
        pt = cut(8192, D, P)
        t0 = cut(16384, P, D)
        w4 = 24576
        uu = cut(w4, 32, D); 
        us = amp[:, :, :].rearrange("p t c -> p (t c)")[:, 0:2048].rearrange("p (t d) -> p t d", d=D)
        xa = cut(w4 + 2048, 2, 7, 32, B)
        m4 = cut(w4 + 2048 + 1792, 4, 7 * 32 * B)
        sbt = pos[:, :, :].rearrange("p a b -> p (a b)")[:, 0:2048].rearrange("p (h c) -> p h c", h=D)
        yg = pos[:, :, :].rearrange("p a b -> p (a b)")[:, 2048:4096].rearrange("p (g t) -> p g t", g=16)
        yt = xd[0:65, :, :, :].rearrange("p a b c -> p (a b c)").rearrange("p (i b t) -> p i b t", i=NT, b=B)
        sg = xq[:, 0, :, :].rearrange("p a b -> p (a b)").rearrange("p (t d) -> p t d", d=D)
        gl = xq[:, 1, :, :].rearrange("p a b -> p (a b)").rearrange("p (t d) -> p t d", d=D)
        xc4 = sg
        sq4 = gl
        late = ampw[:, :, :, :, :].rearrange("p a b s d -> p (a b s d)")
        wo4 = late[0:65, 512:1024].rearrange("p (l o) -> p l o", l=NL)
        wor = prm[:, :, :, :].rearrange("p b t c -> p (b t c)")[:, 0:NL * D].rearrange("p (l d) -> p l d", l=NL)
        lsb = late[:, 0:512].rearrange("p (l k d) -> p l k d", l=NL, k=2)
        w4l = sb("w4l", [65, P])
        lax = cut(32000, 4, 128)

        y8 = cut(0, 2, E1, D)
        x65 = cut(8192, 32, P, parts=65)
        h8 = [cut(16384, E1, 512), cut(20480, E1, 512)]
        w1e = cut(24576, E1, P, parts=64)
        w2e = cut(25600, E1, D)
        b1e = cut(26112, E1)
        wgx = cut(26120, E1, parts=65)
        bgx = cut(26128, 2, E1, parts=65)
        b2d = cut(26144, 16, D)
        cmb = cut(27168, 32, E1)
        cm2 = cut(27424, 32, E1)
        cm3 = cut(27680, 32, E1)
        cmt = cut(27936, 2, P)
        xn1 = cut(28192, 32, D)
        f1 = cut(30240, 32, D)

        turn = cut(32512, P)

        ps = ctx.enter_context(nc.psum_tensor("ps", [P, 8, 512], F32))

        names = """const_in w_in row_in x_in pos_in oh_ready oh_used wt_ps wt_out rt_ps rt_out row_exp row_act row_dve
            gat_ps amp_out c1_ps h1_ready c2_ps h2_ready c3_ps ctx_out arg_ready exp_done phase_ready sin_done
            p_ready v_ps v_out_dve v_out_act k_ps k_out k_stored zk_ready zk_stored d_order f_order p_order sig_in sig_out
            prm_ready m_order prb_ready acc_out acc_ps htr_ps ht_out ln_var ln_sd ln_out
            a_in mnt_ps mnt_out g_ps g_out u_ps r_ready lsum_ps amax_ready att_exp att_ready wvs_ready gate_ps gate_out
            pv_ps og_ready o_ps ht_att
            e_in rw_ps rw_out x_ps x_out lg_ps oh0_ready oht_ps oht_out hx_ps hm_ready f0_ps f0_out f0t_ps ht_ffn
            s_in vt_in pt_in t0_in turn_ps lt_ps lt_out xm_ps xm_out st_ready y_ps yg_ready yt_in yd_in z_ps sig_done us_out xm_done ht_s4
            s_order mask_ready
            m_in x65_ps x65_out gl_ps gexp_in gexp_out cmb_ready cmt_ps cmt_out hh_ps hh_out_a hh_out_d yy_ps yy_out b2_ps b2d_in out_ready stored
            m0_order""".split()
        s = {n: sem(n) for n in names}
        par = {n: [sem(f"{n}_{j}") for j in range(2)] for n in
               ("xq_ready", "ph_ready", "e_done", "s_done", "mul_dve", "mul_pool", "aw_ready", "field_ps", "hm_used")}
        p_stored = [sem(f"p_stored_{c}") for c in range(CHUNKS)]
        v_stored = [sem(f"v_stored_{c}") for c in range(CHUNKS)]
        chunk_used = [sem(f"chunk_used_{c}") for c in range(CHUNKS)]

        def back(x):
            step = x.ap[-1][0]
            return bass.AP(tensor=x.tensor, offset=x.offset + step * (P - 1), ap=[list(x.ap[0]), [-step, P]])

        def past(i):
            return not isinstance(i, int) or i > 0

        class Order:

            def __init__(self, eng, sm, base=0):
                self.eng, self.sm, self.n, self.base = eng, sm, 0, base

            def __call__(self, ins):
                self.n += 1
                ins.then_inc(self.sm, 1)
                self.eng.wait_ge(self.sm, self.base + self.n)

        ln_no = {"attn": 1, "ffn0": 2, "s4in": 3, "s4": 4, "ffn1": 8}
        block = ctx.enter_context(nc.Block())
        col = lambda ap, n: ap.rearrange("(p a) -> p a", a=1) if n else ap
        TWO_PI = 6.2831845
        W_IN = 11 * 16
        ROW_IN = 6 * 16

        @block.sync
        def _(sp):
            def load(dst, src, sm):
                sp.dma_start(dst, src, allow_slow_non_contiguous=True).then_inc(sm, 16)

            load(cst[:, :], a["shape_constants"][:, 0:C_ALL], s["const_in"])
            load(w1r, a["L0_tok_w1"].rearrange("o c k -> o (c k)"), s["w_in"])
            load(w2r, a["L0_tok_w2"].rearrange("o c k -> o (c k)"), s["w_in"])
            load(el[:, 0:D], a["L0_tok_emb"], s["w_in"])
            load(el[:, D:68], a["L0_tok_locality_shapes"], s["w_in"])
            load(w3t, a["L0_tok_w3"].rearrange("o c k -> c (o k)"), s["w_in"])
            load(b1c, col(a["L0_tok_b1"], 1), s["w_in"])
            load(b2c[0:64], col(a["L0_tok_b2"], 1), s["w_in"])
            load(b2c[64:128], col(a["L0_tok_b2"], 1), s["w_in"])
            load(b3c, dram(a["L0_tok_b3"], 0, [[0, P], [1, 1]]), s["w_in"])
            load(msc, dram(a["L0_tok_multiscale_widths"], 0, [[0, P], [1, SC]]), s["w_in"])
            load(swc, dram(a["L0_tok_scale_weights"], 0, [[0, P], [1, SC]]), s["w_in"])
            for j, n in enumerate(("Alog", "Aim", "Cre", "Cim")):
                load(row[:, j], a["L1_attn_" + n].rearrange("(q r) h n -> (r h) q n", r=2), s["row_in"])
            load(ldt, a["L1_attn_log_dt"].rearrange("(q r) h -> (r h) q", r=2), s["row_in"])
            load(drow[:, :, :], dram(a["L1_attn_D"], 0, [[NL * D, 1], [D, NL], [1, D]]), s["row_in"])
            load(pos[:, :, :], dram(a["fside_BS_continuous_positions"], 0, [[0, P], [L, B], [1, L]]), s["pos_in"])
            sp.wait_ge(s["zk_ready"], 2)
            sp.wait_ge(s["mask_ready"], 1)
            for l in range(NL):
                load(k_dram[l, 0:P], zk, s["zk_stored"])
            for i in range(B):
                if i:
                    sp.wait_ge(s["oh_ready"], i)
                load(xb[0:64, 3:1027], dram(a["x"], i * L, [[0, 64], [1, L]]), s["x_in"])
                load(xb[64:128, 2:1026], dram(a["x"], i * L, [[0, 64], [1, L]]), s["x_in"])
                for c in range(CHUNKS):
                    sp.wait_ge(s["p_ready"], i * CHUNKS + c + 1)
                    load(p_dram[i][:, c * HCH * P:(c + 1) * HCH * P], pe_t[:, c * HCH:(c + 1) * HCH, :], p_stored[c])
                for c in range(CHUNKS):
                    sp.wait_ge(s["v_out_dve"], i * 8 + 2 * c + 2)
                    sp.wait_ge(s["v_out_act"], i * 8 + 2 * c + 2)
                    load(v_dram[i][:, c * HCH * P:(c + 1) * HCH * P], ph_t[:, c * HCH:(c + 1) * HCH, :], v_stored[c])
                sp.wait_ge(s["k_out"], i + 1)
                load(k_dram[i, P:2 * P], kt, s["k_stored"])
            sp.wait_ge(s["ht_out"], B)
            for j, n in enumerate(("Wq", "Wk", "Wv", "Wg")):
                load(wqkvg[0:64, j], a["L0_attn_" + n], s["a_in"])
                load(wqkvg[64:128, j], a["L0_attn_" + n], s["a_in"])
            load(wo, a["L0_attn_Wo"].rearrange("(g p) d -> p g d", p=P), s["a_in"])
            load(bgc, a["L0_attn_bg"].rearrange("(g p) -> p g", p=P), s["a_in"])
            for j, n in enumerate(("gamma", "beta", "bo")):
                load(gbc[:, j], dram(a["L0_attn_" + n], 0, [[0, P], [1, D]]), s["a_in"])
            load(rwr, a["L0_ffn_router_w"], s["e_in"])
            load(rbb, dram(a["L0_ffn_router_b"], 0, [[0, P], [1, E0]]), s["e_in"])
            for g in range(4):
                load(w1x[0:64, g, :].rearrange("d (e h) -> d e h", e=8),
                     a["L0_ffn_W1"][8 * g:8 * g + 8].rearrange("e d h -> d e h"), s["e_in"])
            load(b1x, a["L0_ffn_b1"].rearrange("(g e) h -> (e h) g", g=4), s["e_in"])
            load(w2x, a["L0_ffn_W2"].rearrange("(g e) h d -> (e h) g d", g=4), s["e_in"])
            load(b2x, a["L0_ffn_b2"], s["e_in"])
            load(wor, a["L1_attn_Wout"].rearrange("l o h -> o l h"), s["s_in"])
            load(wo4[64:65, :, :], dram(a["L1_attn_bout"], 0, [[NL * P, 1], [P, NL], [1, P]]), s["s_in"])
            load(turn, a["shape_constants"][:, C_J:C_J + P], s["s_in"])
            load(lsb[:, :, 0], dram(a["L1_attn_ln_scale"], 0, [[0, P], [D, NL], [1, D]]), s["s_in"])
            load(lsb[:, :, 1], dram(a["L1_attn_ln_bias"], 0, [[0, P], [D, NL], [1, D]]), s["s_in"])
            for c in range(CHUNKS):
                sp.wait_ge(p_stored[c], 16 * NL)
                sp.wait_ge(v_stored[c], 16 * NL)
            sp.wait_ge(s["k_stored"], 16 * NL)
            sp.wait_ge(s["zk_stored"], 16 * NL)
            sp.wait_ge(s["ht_ffn"], 4)
            for l in range(NL):
                if l:
                    sp.wait_ge(s["xm_done"], l)
                load(vt.rearrange("p h t -> p (h t)"), v_dram[l], s["vt_in"])
                if l:
                    sp.wait_ge(s["y_ps"], 4 * l)
                load(pt.rearrange("p h t -> p (h t)"), p_dram[l], s["pt_in"])
                load(t0.rearrange("p t h -> p (t h)"),
                     dram(k_dram, l * 2 * P * D + D, [[D, P], [1, P * D]]), s["t0_in"])
                sp.wait_ge(s["z_ps"], 8 * l)
                sp.wait_ge(s["yg_ready"], 4 * l + 4)
                for hq in range(4):
                    load(y_dram[16 * hq:16 * hq + 16].rearrange("h c t -> c h t"), yg[32 * hq:32 * hq + 32, :, :],
                         s["yd_in"])
                sp.wait_ge(s["yd_in"], 64 * (l + 1))
                load(yt[0:64].rearrange("h i b t -> h (i b t)"), y_dram.rearrange("h c t -> h (c t)"), s["yt_in"])
            sp.wait_ge(s["us_out"], NL)
            load(w1e, a["L1_ffn_W1"].rearrange("e d f -> d e f"), s["m_in"])
            load(w2e, a["L1_ffn_W2"].rearrange("e f d -> f e d"), s["m_in"])
            load(b1e, a["L1_ffn_b1"].rearrange("e f -> f e"), s["m_in"])
            load(wgx[0:64], a["L1_ffn_Wg"], s["m_in"])
            load(bgx[64:65, 0], dram(a["L1_ffn_bg"], 0, [[E1, 1], [1, E1]]), s["m_in"])
            load(bgx[64:65, 1], dram(a["L1_ffn_bias"], 0, [[E1, 1], [1, E1]]), s["m_in"])
            sp.wait_ge(s["zk_ready"], 3)
            for t in range(16):
                load(b2d[8 * t:8 * t + 8, t, :], a["L1_ffn_b2"], s["b2d_in"])
            sp.wait_ge(s["out_ready"], 1)
            for b in range(B):
                load(a["out"][b].rearrange("(i p) d -> p i d", p=P), ht[:, :, b, :], s["stored"])
            sp.wait_ge(s["stored"], 16 * B)

        @block.gpsimd
        def _(pool):
            pool.memset(zk, 0.0).then_inc(s["zk_ready"], 1)
            pool.memset(h1, 0.0).then_inc(s["zk_ready"], 1)
            pool.wait_ge(s["rt_out"], 1)
            def step(l):
                for c in range(CHUNKS):
                    pool.wait_ge(s["oh_ready"], l + 1)
                    if past(l):
                        pool.wait_ge(p_stored[c], l * 16)
                    if past(l):
                        pool.wait_ge(chunk_used[c], l)
                    hs = slice(c * HCH, (c + 1) * HCH)
                    pool.tensor_tensor(pe_t[:, hs, :],
                                       rs[:, 0, hs].rearrange("p (h a) -> p h a", a=1).broadcast_to([P, HCH, P]),
                                       trow.rearrange("p (a t) -> p a t", a=1).broadcast_to([P, HCH, P]),
                                       ALU.mult).then_inc(s["arg_ready"], 1)
            step(0)
            with pool.Fori(1, NL) as l:
                step(l)
            for it in range(2):
                for g in range(8):
                    p, bp, st = g % 2, g // 4, 2 * (g % 4)
                    pool.wait_ge(s["prb_ready"], it * 2 + bp + 1)
                    pool.wait_ge(par["field_ps"][p], it * 4 + g // 2)
                    for j in range(2):
                        rows = amp[:, bass.ds(it * 16 + bp * 8 + st + j, 1), 0:D].broadcast_to([P, SC, D])
                        ins = pool.tensor_tensor(ampw[:, p, j], rows,
                                                 prb[:, bp, st + j, 13:17].rearrange("p (s a) -> p s a", a=1)
                                                 .broadcast_to([P, SC, D]), ALU.mult)
                    ins.then_inc(par["aw_ready"][p], 1)
                    pool.wait_ge(par["e_done"][p], it * 4 + g // 2 + 1)
                    pool.wait_ge(par["s_done"][p], it * 4 + g // 2 + 1)
                    pool.tensor_tensor(eb[p][:, 1], eb[p][:, 1], qb[p][:, 1], ALU.mult)\
                        .then_inc(par["mul_pool"][p], 1)
            pool.wait_ge(s["us_out"], NL)
            pool.memset(b2d, 0.0).then_inc(s["zk_ready"], 1)

        @block.scalar
        def _(act):
            A = act.activation
            act.wait_ge(s["row_in"], ROW_IN)
            A(dtc, ldt, ACT.Exp).then_inc(s["row_act"], 1)
            A(row[:, 4], row[:, 0], ACT.Exp).then_inc(s["row_act"], 1)
            act.wait_ge(s["row_dve"], 1)
            A(row[:, 8], row[:, 5], ACT.Tanh, scale=0.5).then_inc(s["row_act"], 1)
            A(row[:, 9], row[:, 5], ACT.Exp).then_inc(s["row_act"], 1)
            A(row[:, 10], row[:, 5], ACT.Exp, scale=128.0).then_inc(s["row_act"], 1)
            act.wait_ge(s["row_dve"], 2)
            A(row[:, 16:21], row[:, 11:16], ACT.Sin, scale=TWO_PI).then_inc(s["row_act"], 1)
            def step(i):
                for c in range(CHUNKS):
                    hs = slice(c * HCH, (c + 1) * HCH)
                    act.wait_ge(s["arg_ready"], i * 4 + c + 1)
                    A(pe_t[:, hs, :], pe_t[:, hs, :], ACT.Exp).then_inc(s["exp_done"], 1)
                for j in range(2):
                    act.wait_ge(s["c1_ps"], i * 2 + j + 1)
                    act.wait_ge(s["zk_ready"], 2)
                    if past(i):
                        act.wait_ge(s["c2_ps"], i)
                    A(h1[:, 2 + 512 * j:514 + 512 * j], ps[:, j, :], ACT.Gelu, bias=b1c).then_inc(s["h1_ready"], 1)
                act.wait_ge(s["c2_ps"], i + 1)
                act.wait_ge(s["mask_ready"], 1)
                if past(i):
                    act.wait_ge(s["ctx_out"], i)
                for j in range(2):
                    A(h2[:, 1 + 512 * j:513 + 512 * j], ps[64 * j:64 * j + 64, 2, :], ACT.Gelu,
                      bias=b2c[64 * j:64 * j + 64]).then_inc(s["h2_ready"], 1)
                for c in range(CHUNKS):
                    hs = slice(c * HCH, (c + 1) * HCH)
                    act.wait_ge(s["phase_ready"], i * 4 + c + 1)
                    A(ph_t[:, hs, :], ph_t[:, hs, :], ACT.Sin, scale=TWO_PI, bias=n3pi).then_inc(s["sin_done"], 1)
                act.wait_ge(s["c3_ps"], i + 1)
                A(ctxp[:, bass.ds(i * 8, 8)], ps[:, 2, 0:8], ACT.Copy).then_inc(s["ctx_out"], 1)
                for g in range(8):
                    act.wait_ge(s["v_ps"], i * 16 + 2 * g + 2)
                    A(ph_t[:, 8 * g + 4:8 * g + 8, :], ps[:, 6, :], ACT.Copy).then_inc(s["v_out_act"], 1)
            step(0)
            with act.Fori(1, NL) as i:
                step(i)
            act.wait_ge(s["sig_in"], 1)
            act.wait_ge(s["ctx_out"], B)
            A(post[:, 2, :, 0], ctxp[:, :], ACT.Sigmoid, bias=b3c).then_inc(s["sig_out"], 1)
            A(post[:, 3, :, 0], amp[:, :, 66], ACT.Sigmoid).then_inc(s["sig_out"], 1)
            for it in range(2):
                def gauss(g):
                    p, bp, st, k = g % 2, g // 4, 2 * (g % 4), g // 2
                    act.wait_ge(par["xq_ready"][p], it * 4 + k + 1)
                    act.wait_ge(par["field_ps"][p], it * 4 + k)
                    for j in range(2):
                        for sc in range(SC):
                            ins = A(eb[p][:, j, sc], xq[:, p, j], ACT.Exp,
                                    scale=prb[:, bp, st + j, 9 + sc:10 + sc])
                    ins.then_inc(par["e_done"][p], 1)

                def wave(g):
                    p, k = g % 2, g // 2
                    act.wait_ge(par["ph_ready"][p], it * 4 + k + 1)
                    A(qb[p], qb[p], ACT.Sin, scale=TWO_PI, bias=n3pi).then_inc(par["s_done"][p], 1)

                def field_out(bp):
                    act.wait_ge(s["acc_ps"], it * 2 + bp + 1)
                    act.wait_ge(s["htr_ps"], it * 2 + bp)
                    A(accs[:, :], ps[:, bp, :], ACT.Copy).then_inc(s["acc_out"], 1)

                for g in range(8):
                    (gauss if g % 2 == 0 else wave)(g)
                    (wave if g % 2 == 0 else gauss)(g)
                    if g == 4:
                        field_out(0)
                field_out(1)

            def sqrt(k):
                act.wait_ge(s["ln_var"], k)
                A(lnw[:, 3], lnw[:, 2], ACT.Sqrt).then_inc(s["ln_sd"], 1)

            sqrt(1)
            act.wait_ge(s["ln_var"], 2)
            A(lnw[:, 3], lnw[:, 2], ACT.Sqrt).then_inc(s["ln_sd"], 1)
            for j in range(2):
                act.wait_ge(s["mnt_ps"], 3 + j)
                A(mnt[:, 1, 512 * j:512 * j + 512], ps[:, 2 + j, :], ACT.Copy).then_inc(s["mnt_out"], 1)
            act.wait_ge(s["amax_ready"], 1)
            A(att.rearrange("p a b c d e -> p (a b c d e)"), amx.rearrange("p a b -> p (a b)"), ACT.Exp)\
                .then_inc(s["att_exp"], 1)
            act.wait_ge(s["a_in"], 16 * 13)
            for u in range(16):
                act.wait_ge(s["gate_ps"], u + 1)
                g, b, j = u % 2, u // 4, (u // 2) % 2
                A(gt[:, g, b, 512 * j:512 * j + 512], ps[:, 4 + u % 2, :], ACT.Sigmoid, bias=bgc[:, g:g + 1])\
                    .then_inc(s["gate_out"], 1)
            sqrt(3)
            for k in range(4):
                act.wait_ge(s["x_ps"], 2 * k + 2)
                A(x96[0:64, 8 * k + 4:8 * k + 8, :], ps[0:64, 1, :], ACT.Copy).then_inc(s["x_out"], 1)
            for k in range(4):
                for j in range(2):
                    for g in range(4):
                        u = 8 * k + 4 * j + g
                        if u % 2:
                            continue
                        act.wait_ge(s["hx_ps"], u + 1)
                        if k:
                            act.wait_ge(s["f0_ps"], k)
                        A(hm[:, j, g], ps[:, 2 + u % 4, :], ACT.Relu, bias=b1x[:, g:g + 1]).then_inc(s["hm_ready"], 1)
                act.wait_ge(s["f0_ps"], k + 1)
                if k:
                    act.wait_ge(s["f0t_ps"], k)
                A(f0, ps[:, 6, :], ACT.Relu).then_inc(s["f0_out"], 1)
            sqrt(4)
            def step(l):
                act.wait_ge(s["ln_var"], l + 5)
                A(lnw[:, 3], lnw[:, 2], ACT.Sqrt).then_inc(s["ln_sd"], 1)
                for g in range(4):
                    act.wait_ge(s["y_ps"], l * 4 + g + 1)
                    if past(l):
                        act.wait_ge(s["yd_in"], l * 64)
                    A(yg[:, 4 * g:4 * g + 4, :], ps[:, 4 + g, :].rearrange("p (g t) -> p g t", g=4),
                      ACT.Gelu_apprx_tanh).then_inc(s["yg_ready"], 1)
                for g in range(8):
                    act.wait_ge(s["z_ps"], l * 8 + g + 1)
                    A(sg[:, 4 * g:4 * g + 4, :], ps[:, g, :].rearrange("p (t d) -> p t d", t=4)[:, :, D:P],
                      ACT.Sigmoid).then_inc(s["sig_done"], 1)
            step(0)
            with act.Fori(1, NL) as l:
                step(l)
            sqrt(9)
            for k in range(4):
                act.wait_ge(s["x65_ps"], 2 * k + 2)
                A(x65[0:64, 8 * k + 4:8 * k + 8, :], ps[0:64, 1, :], ACT.Copy).then_inc(s["x65_out"], 1)
            act.wait_ge(s["gexp_in"], 1)
            A(lnw[:, 5], lnw[:, 4], ACT.Exp).then_inc(s["gexp_out"], 1)
            act.wait_ge(s["m_in"], 96)
            for c in range(8):
                for e in range(0, E1, 2):
                    u = 8 * c + e
                    act.wait_ge(s["hh_ps"], u + 1)
                    if c >= 2:
                        act.wait_ge(s["yy_ps"], 4 * (c - 1))
                    A(h8[c % 2][:, e, :], ps[:, 2 + u % 4, :], ACT.Relu, bias=b1e[:, e:e + 1])\
                        .then_inc(s["hh_out_a"], 1)

        @block.tensor
        def _(pe):
            def mm(out, lhsT, rhs, start=True, stop=True):
                return pe.matmul(out, lhsT, rhs, start=start, stop=stop)

            pe.wait_ge(s["const_in"], 16)
            pe.wait_ge(s["w_in"], W_IN)
            w1v = w1r.rearrange("o (c k) -> o k c", k=7)
            w2v = w2r.rearrange("o (c k) -> o k c", k=5)
            for j in range(3):
                for r in range(2):
                    mm(ps[64 * r:64 * r + 64, 0, P * j:P * j + P], w1v[:, 2 * j + r], ident)
            mm(ps[0:64, 0, 3 * P:4 * P], w1v[:, 6], ident).then_inc(s["wt_ps"], 1)
            for k in range(5):
                ins = mm(ps[:, 1, D * k:D * k + D], w2v[:, k], ident[0:64, 0:64])
            ins.then_inc(s["wt_ps"], 1)
            pe.wait_ge(s["row_dve"], 3)
            for q in range(7):
                for r in range(2):
                    k = 2 * q + r
                    ins = pe.transpose(ps[:, 2 + k // 4, P * (k % 4):P * (k % 4) + P],
                                       tin[:, q, r].rearrange("p a n -> p (a n)"), ident)
            ins.then_inc(s["rt_ps"], 1)
            pe.wait_ge(s["wt_out"], 2)
            pe.wait_ge(s["rt_out"], 1)
            def step(i):
                pe.wait_ge(s["oh_ready"], i + 1)
                if past(i):
                    pe.wait_ge(s["amp_out"], i * 2)
                for t in range(NT):
                    ins = mm(ps[:, 3 + t // 4, 68 * (t % 4):68 * (t % 4) + 68], oh[0:64, 3 + P * t:3 + P * t + P], el)
                ins.then_inc(s["gat_ps"], 1)
                if past(i):
                    pe.wait_ge(s["h1_ready"], i * 2)
                for j in range(2):
                    for k in range(3):
                        mm(ps[:, j, :], w1t[:, k], oh[:, 2 * k + 512 * j:2 * k + 512 * j + 512], k == 0, False)
                    ins = mm(ps[:, j, :], w1t[0:64, 3], oh[0:64, 6 + 512 * j:518 + 512 * j], False, True)
                    ins.then_inc(s["c1_ps"], 1)
                pe.wait_ge(s["c1_ps"], i * 2 + 2)
                pe.nop().then_inc(s["oh_used"], 1)
                pe.wait_ge(s["h1_ready"], i * 2 + 2)
                if past(i):
                    pe.wait_ge(s["ctx_out"], i)
                for k in range(5):
                    for j in range(2):
                        ins = mm(ps[64 * j:64 * j + 64, 2, :], w2t[:, k], h1[:, k + 512 * j:k + 512 * j + 512],
                                 k == 0, k == 4)
                ins.then_inc(s["c2_ps"], 1)
                pe.wait_ge(s["h2_ready"], i * 2 + 2)
                for t in range(NT):
                    for k in range(3):
                        ins = mm(ps[:, 2, t:t + 1], h2[:, P * t + k:P * t + k + P], w3t[:, k:k + 1], k == 0, k == 2)
                ins.then_inc(s["c3_ps"], 1)
                if past(i):
                    pe.wait_ge(s["k_out"], i)
                for c in range(CHUNKS):
                    pe.wait_ge(s["p_ready"], i * 4 + c + 1)
                    for g in range(4):
                        gg = 4 * c + g
                        bank = 5 + gg % 2
                        if gg >= 2:
                            pe.wait_ge(s["v_out_act"] if gg % 2 else s["v_out_dve"], i * 8 + gg // 2)
                        else:
                            if past(i):
                                pe.wait_ge(s["v_out_act"] if gg % 2 else s["v_out_dve"], i * 8)
                        for q in range(4):
                            ins = pe.transpose(ps[:, bank, P * q:P * q + P], pe_t[:, 4 * gg + q, :], ident)
                        ins.then_inc(s["v_ps"], 1)
                    for h in range(c * HCH, (c + 1) * HCH):
                        ins = mm(ps[:, 7, h:h + 1], pe_t[:, h, :], rs[:, 2, h:h + 1])
                    ins.then_inc(chunk_used[c], 1)
                pe.wait_ge(chunk_used[CHUNKS - 1], i + 1)
                pe.nop().then_inc(s["k_ps"], 1)
            step(0)
            with pe.Fori(1, NL) as i:
                step(i)
            for it in range(2):
                def turn_out(bp):
                    pe.wait_ge(s["acc_out"], it * 2 + bp + 1)
                    pe.wait_ge(s["ht_out"], it * 2 + bp)
                    for c in range(4):
                        ins = pe.transpose(ps[:, 2, P * c:P * c + P], accs[:, P * c:P * c + P], ident)
                    ins.then_inc(s["htr_ps"], 1)

                for g in range(8):
                    p, bp, k = g % 2, g // 4, g // 2
                    pe.wait_ge(par["aw_ready"][p], it * 4 + k + 1)
                    if g % 4 == 0:
                        pe.wait_ge(s["acc_out"], it * 2)
                    for j in range(2):
                        pe.wait_ge(par["mul_pool" if j else "mul_dve"][p], it * 4 + k + 1)
                        for sc in range(SC):
                            for hf in range(2):
                                ins = mm(ps[64 * hf:64 * hf + 64, bp, :], ampw[:, p, j, sc],
                                         eb[p][:, j, sc, 512 * hf:512 * hf + 512],
                                         g % 4 == 0 and j == 0 and sc == 0, g % 4 == 3 and j == 1 and sc == SC - 1)
                    ins.then_inc(par["field_ps"][p], 1)
                    if g % 4 == 3:
                        pe.wait_ge(par["field_ps"][p], it * 4 + k + 1)
                        pe.nop().then_inc(s["acc_ps"], 1)
                    if g == 4:
                        turn_out(0)
                turn_out(1)
            pe.wait_ge(s["ln_out"], 1)
            for bp in range(2):
                for i in range(NT):
                    ins = pe.transpose(ps[:, 2 * bp + i // 4, P * (i % 4):P * (i % 4) + P],
                                       mn[:, i, 2 * bp:2 * bp + 2, :].rearrange("p b d -> p (b d)"), ident)
                    if i % 4 == 3:
                        ins.then_inc(s["mnt_ps"], 1)
            for sp_ in range(2):
                for i in range(NT):
                    ins = mm(ps[:, 4, 256 * sp_:256 * sp_ + 256],
                             mn[:, i, 2 * sp_:2 * sp_ + 2, :].rearrange("p b d -> p (b d)"),
                             mn[:, i].rearrange("p b d -> p (b d)"), i == 0, i == NT - 1)
            ins.then_inc(s["g_ps"], 1)
            pe.wait_ge(s["g_out"], 1)
            pe.wait_ge(s["a_in"], 16 * 13)
            pe.wait_ge(s["mnt_out"], 4)
            for tp in range(2):
                for sp_ in range(2):
                    for t2 in range(2):
                        ins = mm(ps[:, 2 * t2 + tp, 256 * sp_:256 * sp_ + 256],
                                 gr[64 * t2:64 * t2 + 64, tp, 128 * sp_:128 * sp_ + 128],
                                 wqkvg[64 * t2:64 * t2 + 64, 1])
            ins.then_inc(s["u_ps"], 1)
            pe.wait_ge(s["r_ready"], 1)
            r2f = r2.rearrange("p a h -> p (a h)")
            mm(ps[:, 4, 0:64], cst[:, C_LO:C_LO + P], r2f)
            mm(ps[:, 4, 64:128], cst[:, C_HI:C_HI + P], r2f).then_inc(s["lsum_ps"], 1)
            pe.wait_ge(s["amax_ready"], 1)
            pe.wait_ge(s["wvs_ready"], 1)
            for u in range(16):
                g, b, j = u % 2, u // 4, (u // 2) % 2
                rows = slice(64 * (b % 2), 64 * (b % 2) + 64)
                if u >= 2:
                    pe.wait_ge(s["gate_out"], u - 1)
                    pe.wait_ge(s["gate_ps"], u)
                mm(ps[:, 4 + u % 2, :], wqkvg[rows, 3, P * g:P * g + P], mnt[rows, b // 2, 512 * j:512 * j + 512])\
                    .then_inc(s["gate_ps"], 1)
                if u >= 2:
                    pe.wait_ge(s["og_ready"], u - 1)
                for tp in range(2):
                    ins = mm(ps[:, 6 + u % 2, :], wvs[:, b // 2, b % 2, tp, P * g:P * g + P],
                             mnt[:, tp, 512 * j:512 * j + 512], tp == 0, tp == 1)
                ins.then_inc(s["pv_ps"], 1)
            pe.wait_ge(s["og_ready"], 16)
            for t in range(32):
                i, b = t // 4, t % 4
                for g in range(2):
                    ins = mm(ps[:, t // 8, D * (t % 8):D * (t % 8) + D], gt[:, g, b, P * i:P * i + P], wo[:, g],
                             g == 0, g == 1)
                if t % 8 == 7:
                    ins.then_inc(s["o_ps"], 1)
            pe.wait_ge(s["e_in"], 16 * 9)
            pe.wait_ge(s["ht_att"], 4)
            pe.transpose(ps[0:64, 7, 0:E0], rwr, ident[0:32, 0:32]).then_inc(s["rw_ps"], 1)
            pe.wait_ge(s["ln_out"], 2)
            for k in range(8):
                if k >= 2:
                    pe.wait_ge(s["x_out"] if k % 2 else s["rw_out"], k // 2 if k % 2 else k // 2 + 1)
                for t in range(4):
                    ins = pe.transpose(ps[0:64, k % 2, P * t:P * t + P], xn[:, 4 * k + t], ident)
                ins.then_inc(s["x_ps"], 1)
            pe.wait_ge(s["rw_out"], 5)
            pe.wait_ge(s["x_out"], 4)
            for t in range(32):
                ins = mm(ps[:, 2 + t // 16, E0 * (t % 16):E0 * (t % 16) + E0], x96[0:64, t], rwt)
            ins.then_inc(s["lg_ps"], 1)
            for k in range(8):
                pe.wait_ge(s["oh0_ready"], 1)
                pe.wait_ge(s["oht_out"], 2 * max(k - 1, 0))
                for t in range(4):
                    ins = pe.transpose(ps[0:32, k % 2, P * t:P * t + P], o2[:, 4 * k + t], ident)
                ins.then_inc(s["oht_ps"], 1)
            pe.wait_ge(s["oht_out"], 16)
            pe.wait_ge(s["mask_ready"], 2)
            for k in range(4):
                for j in range(2):
                    c = 2 * k + j
                    for g in range(4):
                        u = 8 * k + 4 * j + g
                        if u >= 4:
                            pe.wait_ge(s["hm_ready"] if u % 2 == 0 else par["hm_used"][0], (u - 4) // 2 + 1)
                        mm(ps[:, 2 + u % 4, :], w1x[:, g],
                           x96[0:96, 4 * c:4 * c + 4, :].rearrange("p t q -> p (t q)")).then_inc(s["hx_ps"], 1)
                pe.wait_ge(s["hm_ready"], 4 * k + 4)
                pe.wait_ge(par["hm_used"][0], 4 * k + 4)
                if k:
                    pe.wait_ge(s["f0_out"], k)
                for g in range(4):
                    for j in range(2):
                        mm(ps[64 * j:64 * j + 64, 6, :], w2x[:, g], hm[:, j, g], g == 0, False)
                for j in range(2):
                    c = 2 * k + j
                    ins = mm(ps[64 * j:64 * j + 64, 6, :], b2x,
                             oht[:, 4 * c:4 * c + 4, :].rearrange("p t q -> p (t q)"), False, True)
                ins.then_inc(s["f0_ps"], 1)
                pe.wait_ge(s["f0_out"], k + 1)
                if k:
                    pe.wait_ge(s["ht_ffn"], k)
                for b in range(B):
                    ins = pe.transpose(ps[:, 7, P * b:P * b + P], f0[:, P * b:P * b + P], ident)
                ins.then_inc(s["f0t_ps"], 1)
            pe.wait_ge(s["s_in"], 80)
            for l in range(NL):
                ins = pe.transpose(ps[0:64, 0, P * l:P * l + P], wor[:, l, :], ident)
            ins.then_inc(s["lt_ps"], 1)
            pe.wait_ge(s["lt_out"], 2)
            pe.wait_ge(s["ln_out"], 3)
            for k in range(4):
                ins = mm(ps[:, 4 + k, :], turn, uu[:, 8 * k:8 * k + 8, :].rearrange("p t d -> p (t d)"))
                ins.then_inc(s["turn_ps"], 1)
            def step(l):
                pe.wait_ge(s["ln_out"], l + 4)
                pe.wait_ge(s["vt_in"], l * 16 + 16)
                if past(l):
                    pe.wait_ge(s["us_out"], l)
                for h in range(D):
                    ins = mm(ps[:, h // 16, 32 * (h % 16):32 * (h % 16) + 28], vt[:, h, :], uu[:, 0:28, h])
                    if h % 16 == 15:
                        ins.then_inc(s["xm_ps"], 1)
                pe.wait_ge(s["xm_ps"], l * 4 + 4)
                pe.nop().then_inc(s["xm_done"], 1)
                pe.wait_ge(s["t0_in"], l * 16 + 16)
                pe.wait_ge(s["pt_in"], l * 16 + 16)
                pe.wait_ge(s["st_ready"], l + 1)
                for g in range(16):
                    for hq in range(4):
                        h = 16 * hq + g
                        mm(ps[32 * hq:32 * hq + 32, 4 + g // 4, P * (g % 4):P * (g % 4) + P], uu[:, :, h],
                           back(t0[:, :, h]), True, False)
                    for hq in range(4):
                        h = 16 * hq + g
                        ins = mm(ps[32 * hq:32 * hq + 32, 4 + g // 4, P * (g % 4):P * (g % 4) + P], sbt[:, h, :],
                                 back(pt[:, h, :]), False, True)
                    if g % 4 == 3:
                        ins.then_inc(s["y_ps"], 1)
                pe.wait_ge(s["yt_in"], l * 16 + 16)
                pe.wait_ge(s["yg_ready"], l * 4 + 4)
                for t in range(32):
                    ins = mm(ps[:, t // 4, P * (t % 4):P * (t % 4) + P], yt[:, t // 4, t % 4, :],
                             w4l[:, :])
                    if t % 4 == 3:
                        ins.then_inc(s["z_ps"], 1)
            step(0)
            with pe.Fori(1, NL) as l:
                step(l)
            for k in range(4):
                pe.wait_ge(s["us_out"], NL)
                mm(ps[:, k, :], turn, us[:, 8 * k:8 * k + 8, :].rearrange("p t d -> p (t d)"))\
                    .then_inc(s["turn_ps"], 1)
            pe.wait_ge(s["ln_out"], 8)
            pe.wait_ge(s["us_out"], NL)
            for k in range(8):
                if k >= 2:
                    pe.wait_ge(s["x65_out"] if k % 2 else s["rw_out"], k // 2 if k % 2 else 5 + k // 2)
                for t in range(4):
                    ins = pe.transpose(ps[0:64, k % 2, P * t:P * t + P], xn1[:, 4 * k + t], ident)
                ins.then_inc(s["x65_ps"], 1)
            pe.wait_ge(s["rw_out"], 9)
            pe.wait_ge(s["x65_out"], 4)
            pe.wait_ge(s["mask_ready"], 4)
            pe.wait_ge(s["m_in"], 96)
            for t in range(32):
                ins = mm(ps[:, 6, E1 * t:E1 * t + E1], x65[0:65, t], wgx)
            ins.then_inc(s["gl_ps"], 1)
            pe.wait_ge(s["b2d_in"], 256)
            pe.wait_ge(s["cmb_ready"], 1)
            for r in range(2):
                ins = pe.transpose(ps[:, 7, P * r:P * r + P],
                                   cmb[:, 16 * r:16 * r + 16, :].rearrange("p t e -> p (t e)"), ident)
            ins.then_inc(s["cmt_ps"], 1)
            pe.wait_ge(s["cmt_out"], 1)
            for r in range(2):
                for q in range(2):
                    k = 2 * r + q
                    ins = mm(ps[:, [6, 7, 0, 1][k], :], cmt[:, r],
                             b2d[:, 8 * q:8 * q + 8, :].rearrange("p t d -> p (t d)"))
            ins.then_inc(s["b2_ps"], 1)
            pe.wait_ge(s["cmt_out"], 2)
            for c in range(9):
                if c < 8:
                    for e in range(E1):
                        u = 8 * c + e
                        if u >= 4:
                            pe.wait_ge(s["hh_out_d"] if u % 2 else s["hh_out_a"], (u - 4) // 2 + 1)
                        mm(ps[:, 2 + u % 4, :], w1e[:, e],
                           x65[0:64, 4 * c:4 * c + 4, :].rearrange("p t q -> p (t q)")).then_inc(s["hh_ps"], 1)
                if c >= 1:
                    cc = c - 1
                    pe.wait_ge(s["hh_out_a"], 4 * cc + 4)
                    pe.wait_ge(s["hh_out_d"], 4 * cc + 4)
                    for t in range(4):
                        u = 4 * cc + t
                        if u >= 2:
                            pe.wait_ge(s["yy_out"], u - 1)
                        for e in range(E1):
                            ins = mm(ps[:, 6 + u % 2, D * e:D * e + D], h8[cc % 2][:, e, P * t:P * t + P], w2e[:, e])
                        ins.then_inc(s["yy_ps"], 1)

        @block.vector
        def _(v):
            TT, TS, TC = v.tensor_tensor, v.tensor_scalar, v.tensor_copy

            def bc(ap, n):
                return ap.rearrange("p (k a) -> p k a", a=1).broadcast_to([ap.shape[0], ap.shape[1], n])

            def bcr(ap, n):
                return ap.rearrange("p (a k) -> p a k", a=1).broadcast_to([ap.shape[0], n, ap.shape[1]])

            od = Order(v, s["d_order"])
            od(v.memset(xb, -1))
            v.memset(h2, 0.0).then_inc(s["mask_ready"], 1)
            R = lambda j: row[:, j].rearrange("p q n -> p (q n)")
            v.wait_ge(s["row_act"], 2)
            for q in range(2):
                od(TS(row[:, 5, q], row[:, 4, q], dtc[:, q:q + 1], -1.0, ALU.mult, ALU.mult))
                od(TS(row[:, 6, q], row[:, 1, q], dtc[:, q:q + 1], 1.0 / 6.283185307179586, ALU.mult, ALU.mult))
            v.nop().then_inc(s["row_dve"], 1)

            def whole(dst, src, tmp):
                od(TS(tmp, src, ROUND, ROUND, ALU.add, ALU.subtract))
                od(TT(dst, src, tmp, ALU.subtract))

            whole(R(7), R(6), R(21))
            od(TC(R(11), R(7)))
            od(TS(R(22), R(7), 0.25, None, ALU.add))
            whole(R(12), R(22), R(21))
            od(TS(R(13), R(7), 0.5, None, ALU.mult))
            od(TS(R(22), R(7), 128.0, None, ALU.mult))
            whole(R(14), R(22), R(21))
            od(TS(R(22), R(14), 0.25, None, ALU.add))
            whole(R(15), R(22), R(21))
            v.nop().then_inc(s["row_dve"], 1)
            v.wait_ge(s["row_act"], 6)
            od(TS(R(21), R(8), -1.0, 1.0, ALU.mult, ALU.add))
            od(v.reciprocal(R(22), R(21)))
            od(TT(R(21), R(8), R(22), ALU.mult))
            od(TS(R(21), R(21), 2.0, None, ALU.mult))
            od(TT(R(21), R(21), R(17), ALU.mult))
            od(TT(R(22), R(18), R(18), ALU.mult))
            od(TS(R(22), R(22), -2.0, None, ALU.mult))
            od(TT(R(21), R(21), R(22), ALU.add))
            od(TT(R(22), R(9), R(16), ALU.mult))
            od(TT(R(23), R(4), R(4), ALU.mult))
            od(TT(R(24), R(1), R(1), ALU.mult))
            od(TT(R(23), R(23), R(24), ALU.add))
            od(v.reciprocal(R(23), R(23)))
            od(TT(R(24), R(22), R(1), ALU.mult))
            od(TT(R(25), R(21), R(4), ALU.mult))
            od(TT(R(24), R(24), R(25), ALU.subtract))
            od(TT(R(24), R(24), R(23), ALU.mult))
            od(TT(R(25), R(22), R(4), ALU.mult))
            od(TT(R(21), R(21), R(1), ALU.mult))
            od(TT(R(25), R(25), R(21), ALU.add))
            od(TT(R(25), R(25), R(23), ALU.mult))
            od(TS(R(25), R(25), -1.0, None, ALU.mult))
            od(TT(R(21), R(2), R(24), ALU.mult))
            od(TT(R(22), R(3), R(25), ALU.mult))
            od(TT(R(21), R(21), R(22), ALU.subtract))
            od(TT(R(22), R(2), R(25), ALU.mult))
            od(TT(R(23), R(3), R(24), ALU.mult))
            od(TT(R(22), R(22), R(23), ALU.add))
            od(TS(tin[:, 2, :, 0], row[:, 21], 2.0, None, ALU.mult))
            od(TS(tin[:, 2, :, 1], row[:, 22], -2.0, None, ALU.mult))
            od(TT(R(23), R(9), R(17), ALU.mult))
            od(TT(R(24), R(9), R(16), ALU.mult))
            od(TT(R(25), R(21), R(23), ALU.mult))
            od(TT(R(11), R(22), R(24), ALU.mult))
            od(TT(R(25), R(25), R(11), ALU.subtract))
            od(TT(R(21), R(21), R(24), ALU.mult))
            od(TT(R(22), R(22), R(23), ALU.mult))
            od(TT(R(21), R(21), R(22), ALU.add))
            for r in range(2):
                od(TC(tin[:, 0, :, r], row[:, 5]))
                od(TS(tin[:, 1, :, r], row[:, 7], 2.0 ** MANT, None, ALU.mult))
                od(TT(tin[:, 3, :, r], row[:, 10], row[:, 20], ALU.mult))
                od(TT(tin[:, 4, :, r], row[:, 10], row[:, 19], ALU.mult))
                od(TS(tin[:, 5, :, r], row[:, 25], 2.0, None, ALU.mult))
                od(TS(tin[:, 6, :, r], row[:, 21], 2.0, None, ALU.mult))
            v.nop().then_inc(s["row_dve"], 1)
            v.wait_ge(s["wt_ps"], 2)
            TC(w1t[:, 0:3].rearrange("p a b -> p (a b)"), ps[:, 0, 0:384])
            TC(w1t[0:64, 3], ps[0:64, 0, 384:512]).then_inc(s["wt_out"], 1)
            TC(w2t.rearrange("p a b -> p (a b)"), ps[:, 1, 0:320]).then_inc(s["wt_out"], 1)
            v.wait_ge(s["rt_ps"], 1)
            for q in range(3):
                od(TC(rt[:, q].rearrange("p l h -> p (l h)"),
                      ps[:, 2 + q // 2, 256 * (q % 2):256 * (q % 2) + 256]))
            for q in range(4):
                k = 3 + q
                src = ps[:, 2 + k // 2, 256 * (k % 2):256 * (k % 2) + 256].rearrange("p (l h) -> p l h", l=NL)
                for hf in range(2):
                    od(TC(la[64 * hf:64 * hf + 64, q], src[64 * hf:64 * hf + 64, :, 32 * hf:32 * hf + 32]))
            v.nop().then_inc(s["rt_out"], 1)
            OT = 64 + 20
            def step(i):
                ot = Order(v, s["f_order"], i * 8)
                if past(i):
                    v.wait_ge(s["k_ps"], i)
                if past(i):
                    v.wait_ge(s["arg_ready"], i * 4)
                ot(TC(rs, rt[:, :, bass.ds(i, 1), :].rearrange("p q a h -> p q (a h)")))
                v.wait_ge(s["x_in"], i * 32 + 32)
                if past(i):
                    v.wait_ge(s["oh_used"], i)
                TS(oh, xb, cst[:, C_PC:C_PC + 1], None, ALU.is_equal).then_inc(s["oh_ready"], 1)
                for c in range(CHUNKS):
                    if past(i):
                        v.wait_ge(v_stored[c], i * 16)
                    for h in range(c * HCH, (c + 1) * HCH):
                        ins = TS(ph_i[:, h * P:(h + 1) * P], trow, rs[:, 1, h:h + 1], cst[:, C_PH:C_PH + 1],
                                 ALU.mult, ALU.add)
                    ot(ins)
                    w = ph_i[:, c * HCH * P:(c + 1) * HCH * P]
                    TS(w, w, (1 << MANT) - 1, ONE_BITS, ALU.bitwise_and, ALU.bitwise_or)\
                        .then_inc(s["phase_ready"], 1)
                v.wait_ge(s["gat_ps"], i + 1)
                for j in range(2):
                    TC(amp[:, bass.ds(i * 8 + 4 * j, 4), :], ps[:, 3 + j, 0:272].rearrange("p (t c) -> p t c", t=4))\
                        .then_inc(s["amp_out"], 1)
                for c in range(CHUNKS):
                    hs = slice(c * HCH, (c + 1) * HCH)
                    v.wait_ge(s["exp_done"], i * 4 + c + 1)
                    v.wait_ge(s["sin_done"], i * 4 + c + 1)
                    TT(pe_t[:, hs, :], pe_t[:, hs, :], ph_t[:, hs, :], ALU.mult).then_inc(s["p_ready"], 1)
                for g in range(8):
                    v.wait_ge(s["v_ps"], i * 16 + 2 * g + 1)
                    TC(ph_t[:, 8 * g:8 * g + 4, :].rearrange("p h t -> p (h t)"), ps[:, 5, :])\
                        .then_inc(s["v_out_dve"], 1)
                v.wait_ge(s["k_ps"], i + 1)
                if past(i):
                    v.wait_ge(s["k_stored"], i * 16)
                ot(TC(kt, ps[:, 7, 0:D]))
                TT(kt[0:1], kt[0:1], drow[0:1, bass.ds(i, 1), :].rearrange("p a h -> p (a h)"), ALU.add)\
                    .then_inc(s["k_out"], 1)
                assert ot.n == 6
                v.nop().then_inc(s["f_order"], 2)
            step(0)
            with v.Fori(1, NL) as i:
                step(i)
            v.wait_ge(s["amp_out"], 2 * B)
            v.nop().then_inc(s["sig_in"], 1)
            lp = lambda j: amp[:, :, 64 + j]
            prf = prm[:, :, :, :].rearrange("p b t c -> p (b t) c")
            od(TS(post[:, 0, :, 0], lp(0), 0.05, None, ALU.mult))
            for b in range(B):
                od(TT(prf[:, 8 * b:8 * b + 8, 0], post[:, 0, 8 * b:8 * b + 8, 0], cst[:, C_BP:C_BP + NT], ALU.add))
            od(TS(post[:, 10, :, 0], lp(1), -1.0, None, ALU.mult))
            od(TT(post[:, 1, :, 0], post[:, 10, :, 0], lp(1), ALU.max))
            od(TT(post[:, 4], bc(post[:, 1, :, 0], SC), bcr(msc, 32), ALU.mult))
            od(TS(post[:, 4], post[:, 4], 1e-5, None, ALU.add))
            od(v.reciprocal(post[:, 5], post[:, 4]))
            od(TS(prf[:, :, 1:5], post[:, 5], 2.0 ** MANT, None, ALU.mult))
            od(TT(post[:, 6], post[:, 5], post[:, 5], ALU.mult))
            od(TS(prf[:, :, 9:13], post[:, 6], -0.5, None, ALU.mult))
            od(TS(post[:, 7, :, 0], lp(3), 0.5, 0.75, ALU.mult, ALU.add))
            od(TS(post[:, 8, :, 0], post[:, 7, :, 0], ROUND, ROUND, ALU.add, ALU.subtract))
            od(TT(post[:, 7, :, 0], post[:, 7, :, 0], post[:, 8, :, 0], ALU.subtract))
            od(TS(post[:, 7, :, 0], post[:, 7, :, 0], 2.0 ** MANT, None, ALU.mult))
            od(TC(prf[:, :, 5:9], bc(post[:, 7, :, 0], SC)))
            od(TT(swc, swc, swc, ALU.mult))
            v.wait_ge(s["sig_out"], 2)
            od(TT(post[:, 9, :, 0], post[:, 2, :, 0], post[:, 3, :, 0], ALU.mult))
            od(TT(prf[:, :, 13:17], bc(post[:, 9, :, 0], SC), bcr(swc, 32), ALU.mult))
            for c in range(CHUNKS):
                v.wait_ge(p_stored[c], 16 * NL)
                v.wait_ge(v_stored[c], 16 * NL)
            v.wait_ge(s["k_stored"], 16 * NL)
            v.wait_ge(s["zk_stored"], 16 * NL)
            v.wait_ge(s["pos_in"], 16)
            for it in range(2):
                om = Order(v, s["m_order"], it * 64)

                def front(g):
                    p, bp, st, k = g % 2, g // 4, 2 * (g % 4), g // 2
                    if g % 4 == 0:
                        v.wait_ge(par["e_done"][1], it * 4)
                        v.wait_ge(par["aw_ready"][1], it * 4)
                        TC(prb[:, bp], prm[:, bass.ds(it * 2 + bp, 1)].rearrange("p a t c -> p (a t) c"))\
                            .then_inc(s["prb_ready"], 1)
                        v.wait_ge(s["prb_ready"], it * 2 + bp + 1)
                    v.wait_ge(par["mul_dve"][p], it * 4 + k)
                    v.wait_ge(par["ph_ready"][p], it * 4 + k)
                    for j in range(2):
                        ins = TS(xd[:, p, j], pos[:, bass.ds(it * 2 + bp, 1), :].rearrange("p a l -> p (a l)"),
                                 prb[:, bp, st + j, 0:1], None, ALU.subtract)
                    om(ins)
                    v.wait_ge(par["e_done"][p], it * 4 + k)
                    TT(xq[:, p], xd[:, p], xd[:, p], ALU.mult).then_inc(par["xq_ready"][p], 1)
                    v.wait_ge(par["mul_pool"][p], it * 4 + k)
                    for j in range(2):
                        for sc in range(SC):
                            w = (4 * j + sc) * L
                            ins = TS(qi[p][:, w:w + L], xd[:, p, j], prb[:, bp, st + j, 1 + sc:2 + sc],
                                     prb[:, bp, st + j, 5 + sc:6 + sc], ALU.mult, ALU.add)
                    om(ins)
                    TS(qi[p], qi[p], (1 << MANT) - 1, ONE_BITS, ALU.bitwise_and, ALU.bitwise_or)\
                        .then_inc(par["ph_ready"][p], 1)

                def product(g):
                    p, k = g % 2, g // 2
                    v.wait_ge(par["e_done"][p], it * 4 + k + 1)
                    v.wait_ge(par["s_done"][p], it * 4 + k + 1)
                    TT(eb[p][:, 0], eb[p][:, 0], qb[p][:, 0], ALU.mult).then_inc(par["mul_dve"][p], 1)

                def field_out(bp):
                    v.wait_ge(s["htr_ps"], it * 2 + bp + 1)
                    for hf in range(2):
                        dst = ht[:, 4 * hf:4 * hf + 4, bass.ds(it * 2 + bp, 1), :].rearrange("p i a d -> p i (a d)")
                        src = ps[:, 2, :].rearrange("p (c f d) -> p c f d", c=4, f=2)[:, :, hf]
                        ins = TC(dst, src)
                    ins.then_inc(s["ht_out"], 1)

                front(0)
                for g in range(1, 8):
                    front(g)
                    product(g - 1)
                    if g == 6:
                        field_out(0)
                product(7)
                field_out(1)
                assert om.n == 16
                v.nop().then_inc(s["m_order"], 48)
            v.wait_ge(s["ht_out"], B)

            neg_mean, ve = lnw[:, 0], lnw[:, 2]

            def centre(x, xc_, sq_):
                od(v.reduce_sum(lnw[:, 0], x, axis=AX.X))
                od(TS(lnw[:, 0], lnw[:, 0], -1.0 / D, None, ALU.mult))
                od(TT(xc_, x, bc(lnw[:, 0], D), ALU.add))
                od(TT(sq_, xc_, xc_, ALU.mult))
                od(v.reduce_sum(lnw[:, 1], sq_, axis=AX.X))

            def rstd(k):
                TS(lnw[:, 2], lnw[:, 1], 1.0 / D, EPS, ALU.mult, ALU.add).then_inc(s["ln_var"], 1)
                v.wait_ge(s["ln_sd"], k)
                od(v.reciprocal(lnw[:, 4], lnw[:, 3]))

            flat = lambda t: t.rearrange("p i b d -> p (i b) d")
            htf = flat(ht[:, :, :, :])
            centre(htf, xc, sq)
            rstd(1)
            od(TT(lnw[:, 5], lnw[:, 4], lnw[:, 4], ALU.mult))
            od(TT(lnw[:, 1], lnw[:, 1], lnw[:, 5], ALU.mult))
            od(TC(lnw[:, 5], lnw[:, 4]))
            rstd(2)
            od(TT(lnw[:, 4], lnw[:, 4], lnw[:, 5], ALU.mult))
            od(TT(xc, xc, bc(lnw[:, 4], D), ALU.mult))
            v.wait_ge(s["a_in"], 16 * 13)
            od(TT(xc, xc, bcr(gbc[:, 0], 32), ALU.mult))
            TT(flat(mn), xc, bcr(gbc[:, 1], 32), ALU.add).then_inc(s["ln_out"], 1)
            for j in range(2):
                v.wait_ge(s["mnt_ps"], 1 + j)
                TC(mnt[:, 0, 512 * j:512 * j + 512], ps[:, j, :]).then_inc(s["mnt_out"], 1)
            v.wait_ge(s["g_ps"], 1)
            TC(gr.rearrange("p a b -> p (a b)"), ps[:, 4, :]).then_inc(s["g_out"], 1)
            v.wait_ge(s["u_ps"], 1)
            for k in range(4):
                od(TT(rr[:, 2 * k:2 * k + 2], ps[:, k, :].rearrange("p (a c) -> p a c", a=2),
                      bcr(wqkvg[:, 0], 2), ALU.mult))
            v.reduce_sum(r2.rearrange("p a h -> p (a h)"), rr.rearrange("p a (h c) -> p (a h) c", c=CH), axis=AX.X)\
                .then_inc(s["r_ready"], 1)
            v.wait_ge(s["lsum_ps"], 1)
            sc_att = 1.0 / (CH ** 0.5) / (L ** 0.5)
            lgt = rr.rearrange("p a c -> p (a c)")[:, 0:128]
            od(TS(lgt, ps[:, 4, 0:128], sc_att, None, ALU.mult))
            by_t = lambda x: x.rearrange("p (s t k) -> p s k t", s=2, t=4)
            mx = rr.rearrange("p a c -> p (a c)")[:, 128:160]
            od(v.reduce_max(mx.rearrange("p (s k) -> p s k", s=2), by_t(lgt), axis=AX.X))
            amf = amx.rearrange("p a b -> p (a b)")
            for s2 in range(2):
                ins = TT(amf[:, 64 * s2:64 * s2 + 64].rearrange("p (t k) -> p t k", t=4),
                         lgt[:, 64 * s2:64 * s2 + 64].rearrange("p (t k) -> p t k", t=4),
                         bcr(mx[:, 16 * s2:16 * s2 + 16], 4), ALU.subtract)
            ins.then_inc(s["amax_ready"], 1)
            v.wait_ge(s["att_exp"], 1)
            atf = att.rearrange("p a b c d e -> p (a b c d e)")
            od(v.reduce_sum(mx.rearrange("p (s k) -> p s k", s=2), by_t(atf), axis=AX.X))
            od(v.reciprocal(mx, mx))
            for s2 in range(2):
                w = atf[:, 64 * s2:64 * s2 + 64].rearrange("p (t k) -> p t k", t=4)
                od(TT(w, w, bcr(mx[:, 16 * s2:16 * s2 + 16], 4), ALU.mult))
            for t2 in range(2):
                rows = slice(64 * t2, 64 * t2 + 64)
                for sp_ in range(2):
                    for s2 in range(2):
                        for tp in range(2):
                            ins = TT(wvs[rows, sp_, s2, tp].rearrange("p (h c) -> p h c", h=NH),
                                     wqkvg[rows, 2].rearrange("p (h c) -> p h c", h=NH),
                                     bc(att[rows, s2, t2, tp, sp_], CH), ALU.mult)
            ins.then_inc(s["wvs_ready"], 1)
            for u in range(16):
                g, b, j = u % 2, u // 4, (u // 2) % 2
                w = gt[:, g, b, 512 * j:512 * j + 512]
                v.wait_ge(s["gate_out"], u + 1)
                v.wait_ge(s["pv_ps"], u + 1)
                TT(w, ps[:, 6 + u % 2, :], w, ALU.mult).then_inc(s["og_ready"], 1)
            for k in range(4):
                v.wait_ge(s["o_ps"], k + 1)
                w = htf[:, 8 * k:8 * k + 8]
                od(TT(w, w, bcr(gbc[:, 2], 8), ALU.add))
                TT(w, w, ps[:, k, :].rearrange("p (t d) -> p t d", t=8), ALU.add).then_inc(s["ht_att"], 1)
            v.wait_ge(s["ht_att"], 4)
            v.wait_ge(s["e_in"], 16 * 9)
            for g in range(4):
                ins = TC(w1x[64:96, g].rearrange("p (e h) -> p e h", e=8),
                         bc(cst[64:96, C_BIG + 8 * g:C_BIG + 8 * g + 8], H0))
            ins.then_inc(s["mask_ready"], 1)
            v.wait_ge(s["rw_ps"], 1)
            TC(rwt, ps[0:64, 7, 0:E0]).then_inc(s["rw_out"], 1)
            centre(htf, xc, sq)
            rstd(3)
            TT(xn, xc, bc(lnw[:, 4], D), ALU.mult).then_inc(s["ln_out"], 1)
            for k in range(4):
                v.wait_ge(s["x_ps"], 2 * k + 1)
                TC(x96[0:64, 8 * k:8 * k + 4, :].rearrange("p t q -> p (t q)"), ps[0:64, 0, :])\
                    .then_inc(s["rw_out"], 1)
            v.wait_ge(s["lg_ps"], 1)
            for k in range(2):
                od(TT(lg[:, 16 * k:16 * k + 16], ps[:, 2 + k, :].rearrange("p (t e) -> p t e", t=16),
                      bcr(rbb, 16), ALU.add))
            od(v.reduce_max(lnw[:, 0], lg, axis=AX.X))
            od(TT(o1, lg, bc(lnw[:, 0], E0), ALU.is_equal))
            od(TT(o1, o1, bcr(cst[:, C_DESC:C_DESC + E0], 32), ALU.mult))
            od(v.reduce_max(lnw[:, 1], o1, axis=AX.X))
            TT(o2, o1, bc(lnw[:, 1], E0), ALU.is_equal).then_inc(s["oh0_ready"], 1)
            for k in range(8):
                v.wait_ge(s["oht_ps"], k + 1)
                TC(oht[:, 4 * k:4 * k + 4].rearrange("p t q -> p (t q)"), ps[0:32, k % 2, :])\
                    .then_inc(s["oht_out"], 1)
                TS(x96[64:96, 4 * k:4 * k + 4].rearrange("p t q -> p (t q)"), ps[0:32, k % 2, :], -1.0, None,
                   ALU.add).then_inc(s["oht_out"], 1)
            for k in range(4):
                for u in range(8 * k + 1, 8 * k + 8, 2):
                    j, g = (u // 4) % 2, u % 4
                    v.wait_ge(s["hx_ps"], u + 1)
                    if k:
                        v.wait_ge(s["f0_ps"], k)
                    TS(hm[:, j, g], ps[:, 2 + u % 4, :], b1x[:, g:g + 1], 0.0, ALU.add, ALU.max)\
                        .then_inc(par["hm_used"][0], 1)
                v.wait_ge(s["f0t_ps"], k + 1)
                w = ht[:, 2 * k:2 * k + 2].rearrange("p i b d -> p b i d")
                for b in range(B):
                    ins = TT(ht[:, 2 * k:2 * k + 2, b, :], ht[:, 2 * k:2 * k + 2, b, :],
                             ps[:, 7, P * b:P * b + P].rearrange("p (i d) -> p i d", i=2), ALU.add)
                ins.then_inc(s["ht_ffn"], 1)
            v.wait_ge(s["lt_ps"], 1)
            TC(wo4[0:64, :, :].rearrange("p l o -> p (l o)"), ps[0:64, 0, :]).then_inc(s["lt_out"], 1)
            v.memset(yt[64:65].rearrange("p i b t -> p (i b t)"), 1.0).then_inc(s["lt_out"], 1)
            v.wait_ge(s["ht_ffn"], 4)
            v.wait_ge(s["s_in"], 80)
            usf = us
            centre(htf, xc4, sq4)
            rstd(4)
            TT(uu, xc4, bc(lnw[:, 4], D), ALU.mult).then_inc(s["ln_out"], 1)
            for k in range(4):
                v.wait_ge(s["turn_ps"], k + 1)
                od(TC(usf[:, 8 * k:8 * k + 8, :].rearrange("p t d -> p (t d)"), ps[:, 4 + k, :]))
            od(v.memset(sbt, 0.0))
            def step(l):
                global_od = Order(v, s["s_order"], l * 128)
                O = global_od
                O(v.reduce_sum(lnw[:, 0], usf, axis=AX.X))
                O(TS(lnw[:, 0], lnw[:, 0], -1.0 / D, None, ALU.mult))
                O(TT(xc4, usf, bc(lnw[:, 0], D), ALU.add))
                O(TT(sq4, xc4, xc4, ALU.mult))
                O(v.reduce_sum(lnw[:, 1], sq4, axis=AX.X))
                TS(lnw[:, 2], lnw[:, 1], 1.0 / D, EPS, ALU.mult, ALU.add).then_inc(s["ln_var"], 1)
                v.wait_ge(s["ln_sd"], l + 5)
                O(v.reciprocal(lnw[:, 4], lnw[:, 3]))
                O(TT(xc4, xc4, bc(lnw[:, 4], D), ALU.mult))
                O(TC(w4l[:, :], wo4[:, bass.ds(l, 1), :].rearrange("p a o -> p (a o)")))
                O(TT(xc4, xc4, lsb[:, bass.ds(l, 1), 0, :].broadcast_to([P, 32, D]), ALU.mult))
                TT(uu, xc4, lsb[:, bass.ds(l, 1), 1, :].broadcast_to([P, 32, D]), ALU.add).then_inc(s["ln_out"], 1)
                for q in range(4):
                    ins = TC(lax[:, q].rearrange("p (h b) -> p h b", b=B),
                             bc(la[:, q, bass.ds(l, 1), :].rearrange("p a h -> p (a h)"), B))
                O(ins)
                for k in range(4):
                    v.wait_ge(s["xm_ps"], l * 4 + k + 1)
                    hp, hh = k // 2, 16 * (k % 2)
                    for ri in range(2):
                        src = ps[64 * ri:64 * ri + 64, k, :].rearrange("p (h c) -> p h c", h=16)[:, :, 0:28]
                        ins = TC(xa[64 * hp:64 * hp + 64, ri, :, hh:hh + 16, :],
                                 src.rearrange("p h (i b) -> p i h b", i=7))
                    O(ins)
                for i in range(1, 7):
                    last = xa[:, :, i - 1].rearrange("p r h b -> p r (h b)")
                    xi = xa[:, :, i].rearrange("p r h b -> p r (h b)")
                    TT(m4[:, 0:2, 0:128], last, bcr(lax[:, 0], 2), ALU.mult)
                    O(TT(m4[:, 2:4, 0:128], last, bcr(lax[:, 1], 2), ALU.mult))
                    O(TT(xi, xi, m4[:, 0:2, 0:128], ALU.add))
                    TT(xi[:, 0], xi[:, 0], m4[:, 3, 0:128], ALU.subtract)
                    O(TT(xi[:, 1], xi[:, 1], m4[:, 2, 0:128], ALU.add))
                for ri in range(2):
                    for gi in range(2):
                        ins = TT(m4[:, 2 * ri + gi].rearrange("p (i k) -> p i k", i=7),
                                 xa[:, ri].rearrange("p i h b -> p i (h b)"), bcr(lax[:, 2 + gi], 7), ALU.mult)
                O(ins)
                for hp in range(2):
                    rows = slice(64 * hp, 64 * hp + 64)
                    re, im = sbt[0:64, 32 * hp:32 * hp + 32, 4:32], sbt[64:128, 32 * hp:32 * hp + 32, 4:32]
                    m = lambda k: m4[rows, k].rearrange("p (i h b) -> p h i b", i=7, b=B)
                    shp = lambda w: w.rearrange("p h (i b) -> p h i b", i=7)
                    TT(shp(re), m(0), m(3), ALU.subtract)
                    O(TT(m(1), m(1), m(2), ALU.add))
                    O(TS(shp(im), m(1), -1.0, None, ALU.mult))
                v.nop().then_inc(s["st_ready"], 1)
                for g in range(8):
                    v.wait_ge(s["sig_done"], l * 8 + g + 1)
                    w = slice(4 * g, 4 * g + 4)
                    O(TT(gl[:, w], ps[:, g, :].rearrange("p (t d) -> p t d", t=4)[:, :, 0:D], sg[:, w], ALU.mult))
                TT(usf, usf, gl, ALU.add).then_inc(s["us_out"], 1)
                v.wait_ge(s["us_out"], l + 1)
                v.nop().then_inc(s["s_order"], 128 - O.n)
            step(0)
            with v.Fori(1, NL) as l:
                step(l)
            for k in range(4):
                v.wait_ge(s["turn_ps"], 5 + k)
                w = htf[:, 8 * k:8 * k + 8]
                od(TT(w, w, ps[:, k, :].rearrange("p (t d) -> p t d", t=8), ALU.add))
            centre(htf, xc4, sq4)
            rstd(9)
            TT(xn1, xc4, bc(lnw[:, 4], D), ALU.mult).then_inc(s["ln_out"], 1)
            v.wait_ge(s["m_in"], 96)
            TT(wgx[64:65], bgx[64:65, 0], bgx[64:65, 1], ALU.add).then_inc(s["mask_ready"], 1)
            v.memset(x65[64:65].rearrange("p t q -> p (t q)"), 1.0).then_inc(s["mask_ready"], 1)
            for k in range(4):
                v.wait_ge(s["x65_ps"], 2 * k + 1)
                TC(x65[0:64, 8 * k:8 * k + 4, :].rearrange("p t q -> p (t q)"), ps[0:64, 0, :])\
                    .then_inc(s["rw_out"], 1)
            v.wait_ge(s["gl_ps"], 1)
            desc = bcr(cst[:, C_DESC + E0 - E1:C_DESC + E0], 32)

            def first_max(dst, src, mxc):
                od(v.reduce_max(mxc, src, axis=AX.X))
                od(TT(cm3, src, bc(mxc, E1), ALU.is_equal))
                od(TT(cm3, cm3, desc, ALU.mult))
                od(v.reduce_max(lnw[:, 3], cm3, axis=AX.X))
                od(TT(dst, cm3, bc(lnw[:, 3], E1), ALU.is_equal))

            od(TC(cm2, ps[:, 6, 0:256].rearrange("p (t e) -> p t e", t=32)))
            first_max(cmb, cm2, lnw[:, 0])
            od(TS(f1[:, :, 0:E1], cmb, -3.0e38, None, ALU.mult))
            od(TT(cm2, cm2, f1[:, :, 0:E1], ALU.add))
            first_max(f1[:, :, 8:16], cm2, lnw[:, 1])
            TT(lnw[:, 4], lnw[:, 1], lnw[:, 0], ALU.subtract).then_inc(s["gexp_in"], 1)
            v.wait_ge(s["gexp_out"], 1)
            od(TS(lnw[:, 0], lnw[:, 5], 1.0, None, ALU.add))
            od(v.reciprocal(lnw[:, 1], lnw[:, 0]))
            od(TT(lnw[:, 2], lnw[:, 5], lnw[:, 1], ALU.mult))
            od(TT(cmb, cmb, bc(lnw[:, 1], E1), ALU.mult))
            od(TT(f1[:, :, 8:16], f1[:, :, 8:16], bc(lnw[:, 2], E1), ALU.mult))
            od(TT(cmb, cmb, f1[:, :, 8:16], ALU.add))
            v.nop().then_inc(s["cmb_ready"], 1)
            v.wait_ge(s["cmt_ps"], 1)
            TC(cmt.rearrange("p a b -> p (a b)"), ps[:, 7, 0:256]).then_inc(s["cmt_out"], 1)
            v.wait_ge(s["b2_ps"], 1)
            for k in range(4):
                w = htf[:, 8 * k:8 * k + 8]
                ins = TT(w, w, ps[:, [6, 7, 0, 1][k], :].rearrange("p (t d) -> p t d", t=8), ALU.add)
            ins.then_inc(s["cmt_out"], 1)

            def combine(cc):
                for t in range(4):
                    u = 4 * cc + t
                    v.wait_ge(s["yy_ps"], u + 1)
                    TT(y8[:, u % 2], ps[:, 6 + u % 2, :].rearrange("p (e d) -> p e d", e=E1),
                       bc(cmb[:, u], D), ALU.mult).then_inc(s["yy_out"], 1)
                    v.wait_ge(s["yy_out"], u + 1)
                    od(v.reduce_sum(f1[:, u, :], y8[:, u % 2].rearrange("p e d -> p d e"), axis=AX.X))

            for c in range(9):
                if c < 8:
                    for e in range(1, E1, 2):
                        u = 8 * c + e
                        v.wait_ge(s["hh_ps"], u + 1)
                        if c >= 2:
                            v.wait_ge(s["yy_ps"], 4 * (c - 1))
                        TS(h8[c % 2][:, e, :], ps[:, 2 + u % 4, :], b1e[:, e:e + 1], 0.0, ALU.add, ALU.max)\
                            .then_inc(s["hh_out_d"], 1)
                if c >= 1:
                    combine(c - 1)
            TT(htf, htf, f1, ALU.add).then_inc(s["out_ready"], 1)


def kernel(**inputs):
    import numpy as np
    from concourse import bacc
    from concourse.bass_utils import run_bass_kernel_spmd

    nc = bacc.Bacc("TRN2", target_bir_lowering=False, num_devices=1)
    c = np.zeros((P, C_J + P), np.float32)
    c[:, C_ID:C_ID + P] = np.eye(P)
    c[:, C_T:C_T + P] = np.arange(P)
    c[:, C_BP:C_BP + NT] = (np.arange(L, dtype=np.float32) / np.float32(L - 1)).reshape(NT, P).T
    c[:, C_PC] = np.arange(P) % 64
    c[:, C_DESC:C_DESC + E0] = E0 - np.arange(E0)
    c[:, C_PH] = np.where(np.arange(P) < 64, 0.75, 0.5) * 2.0 ** MANT
    c[:64, C_LO:C_LO + P] = 1.0
    c[64:, C_HI:C_HI + P] = 1.0
    c[64:96, C_BIG:C_BIG + E0] = np.eye(E0) * BIG
    c[:, C_J:C_J + P] = np.eye(P)[::-1]
    c[:, C_N3PI] = -9.424777
    arrays = {n: np.ascontiguousarray(x) for n, x in inputs.items()}
    arrays["shape_constants"] = c
    aps = {n: nc.dram_tensor("in_" + n, x.shape, mybir.dt.from_np(x.dtype), kind="ExternalInput").ap()
           for n, x in arrays.items()}
    aps["out"] = nc.dram_tensor("out_0", (B, L, D), F32, kind="ExternalOutput").ap()
    tower_kernel(nc, aps)
    r = run_bass_kernel_spmd(nc, [{"in_" + n: x for n, x in arrays.items()}], core_ids=[0])
    return r.results[0]["out_0"]
```

```python
from contextlib import ExitStack

import concourse.bass as bass
from concourse import mybir

F32 = mybir.dt.float32
I32 = mybir.dt.int32
BF16 = mybir.dt.bfloat16
ALU = mybir.AluOpType
ACT = mybir.ActivationFunctionType
AX = mybir.AxisListType

P = 128
B, L, D = 4, 1024, 64
NT = L // P
SC = 4
NH, CH = 8, 32
HC = NH * CH
E0, H0 = 32, 16
NL, N = 4, 64
E1, H1 = 8, 128
EPS = 1e-5
MANT = 23
ONE_BITS = 0x3F800000
ROUND = 1.5 * 2.0 ** 23
BIG = 2.0 ** 100
CHUNKS = 4
HCH = D // CHUNKS

C_ID, C_T, C_BP, C_PC, C_DESC, C_PH, C_LO, C_HI, C_BIG, C_N3PI = 0, 128, 256, 264, 265, 297, 298, 426, 554, 586
C_ALL = 588
C_J = C_ALL
C_SEL = C_J + P


def tower_kernel(nc, a):
    ctx = ExitStack()
    with ctx:
        def sb(name, shape, dt=F32):
            return ctx.enter_context(nc.sbuf_tensor(name, shape, dt))

        def sem(name):
            return ctx.enter_context(nc.semaphore(name))

        def dram(ap, offset, pattern):
            return bass.AP(tensor=ap.tensor, offset=ap.offset + offset, ap=pattern)

        p_dram = nc.dram_tensor("mode_tables", [NL, P, D * P], F32, kind="Internal").ap()
        v_dram = nc.dram_tensor("mode_tables_t", [NL, P, D * P], F32, kind="Internal").ap()
        k_dram = nc.dram_tensor("taps", [NL, D, 2 * P], F32, kind="Internal").ap()

        ctx_dram = nc.dram_tensor("context_row", [B * L], F32, kind="Internal").ap()
        y_dram = nc.dram_tensor("conv_out", [D, 32, P], F32, kind="Internal").ap()

        big = sb("big", [P, 4 * 8192])
        cst = sb("cst", [P, C_ALL])
        ht = sb("ht", [P, NT, B, D])
        amp = sb("amp", [P, B * NT, 68])
        pos = sb("pos", [P, B, L])
        xd = sb("xd", [P, 2, 2, L])
        xq = sb("xq", [P, 2, 2, L])
        ampw = sb("ampw", [P, 2, 2, SC, D])
        prm = sb("prm", [P, B, NT, 17])
        prb = sb("prb", [P, 2, NT, 17])
        ctxp = sb("ctxp", [P, B * NT])
        la = sb("la", [P, 4, NL, 32])
        lnw = sb("lnw", [P, 6, 32])

        def cut(off, *shape, parts=P, dt=F32):
            n = 1
            for s in shape:
                n *= s
            v = big[0:parts, off:off + n]
            if dt is not F32:
                v = v.bitcast(dt)
            if len(shape) == 1:
                return v
            names = "abcde"[:len(shape)]
            return v.rearrange(f"p ({' '.join(names)}) -> p {' '.join(names)}",
                               **{k: s for k, s in zip(names[1:], shape[1:])})

        ident = cst[:, C_ID:C_ID + P]
        trow = cst[:, C_T:C_T + P]
        n3pi = cst[:, C_N3PI:C_N3PI + 1]

        pe_t = cut(0, D, P)
        ph_t = cut(8192, D, P)
        ph_f = cut(8192, D * P)
        ph_i = cut(8192, D * P, dt=I32)
        o = 16384
        xb = cut(o, 1032, dt=I32); o += 1032
        oh = cut(o, 1032); o += 1032
        h1 = cut(o, 1028); o += 1028
        h2 = cut(o, 1026, parts=64); o += 1026
        w1r = cut(o, 448); o += 448
        w2r = cut(o, 640, parts=64); o += 640
        w3r = cut(o, 192, parts=1); o += 192
        w1t = cut(o, 4, P); o += 512
        w2t = cut(o, 5, D); o += 320
        w3t = cut(o, 3, parts=64); o += 4
        el = cut(o, 68, parts=64); o += 68
        b1c = cut(o, 1); o += 1
        b2c = cut(o, 1); o += 1
        b3c = cut(o, 1); o += 1
        msc = cut(o, SC); o += SC
        swc = cut(o, SC); o += SC
        ldt = cut(o, 2); o += 2
        dtc = cut(o, 2); o += 2
        row = cut(o, 26, 2, N); o += 26 * 2 * N
        tin = cut(o, 7, 2, 2, N); o += 7 * 4 * N
        rt = cut(o, 3, NL, D); o += 3 * NL * D
        coef = cut(o, D + 32); o += D + 32
        post = cut(o, 16, B * NT, SC); o += 16 * 32 * SC
        zk = cut(o, P, parts=64); o += P
        skip = cut(o, NL, 16); o += NL * 16
        assert o <= 32768, o

        vout = [w[:, :, :, :].rearrange("p a b c -> p (a b c)").rearrange("p (h t) -> p h t", t=P) for w in (xd, xq)]
        kst = ampw[:, :, :, :, :].rearrange("p a b s d -> p (a b s d)").rearrange("p (k g t) -> p k g t", k=2, t=P)

        eb = [cut(0, 2, SC, L), cut(8192, 2, SC, L)]
        qb = [cut(16384, 2, SC, L), cut(24576, 2, SC, L)]
        qi = [cut(16384, 8 * L, dt=I32), cut(24576, 8 * L, dt=I32)]
        accs = sb("accs", [P, 512])

        crow = accs

        mn = cut(0, NT, B, D)
        mnt = cut(2048, 2, L)
        xc = cut(4096, 32, D)
        sq = cut(6144, 32, D)
        gr = cut(8192, 2, HC)
        wqkvg = cut(8704, 4, HC)
        rr = cut(9728, 8, HC)
        r2 = cut(11776, 8, NH)
        att = cut(11840, 2, 2, 2, 2, NH)
        amx = cut(11968, 4, 32); 
        wvs = cut(12288, 2, 2, 2, HC)
        gt = cut(16384, 2, B, L)
        wo = cut(24576, 2, D)
        bgc = cut(24704, 2)
        gbc = cut(24706, 3, D)

        xn = cut(0, 32, D)
        x96 = cut(8192, 32, P)
        oht = cut(12288, 32, P, parts=32)
        hm = cut(16384, 2, 4, 512)
        f0 = cut(20480, 512)
        lg = cut(21000, 32, E0)
        o1 = cut(22024, 32, E0)
        o2 = cut(23048, 32, E0)
        rwr = cut(26000, D, parts=32)
        rwt = cut(24960, E0, parts=64)
        rbb = cut(24992, E0)
        w1x = cut(25024, 4, P, parts=96)
        b1x = cut(25536, 4)
        w2x = cut(25540, 4, D)
        b2x = cut(25796, D, parts=32)

        vt = cut(0, D, P)
        pt = cut(8192, D, P)
        t0 = cut(16384, D, P)
        w4 = 24576
        uu = cut(w4, 32, D); 
        us = amp[:, :, :].rearrange("p t c -> p (t c)")[:, 0:2048].rearrange("p (t d) -> p t d", d=D)
        xa = cut(w4 + 2048, 2, 7, 32, B)
        m4 = cut(w4 + 2048 + 1792, 4, 7 * 32 * B)
        sbt = pos[:, :, :].rearrange("p a b -> p (a b)")[:, 0:2048].rearrange("p (h c) -> p h c", h=D)
        yg = pos[:, :, :].rearrange("p a b -> p (a b)")[:, 2048:4096].rearrange("p (g t) -> p g t", g=16)
        yt = xd[0:65, :, :, :].rearrange("p a b c -> p (a b c)").rearrange("p (i b t) -> p i b t", i=NT, b=B)
        sg = xq[:, 0, :, :].rearrange("p a b -> p (a b)").rearrange("p (t d) -> p t d", d=D)
        gl = xq[:, 1, :, :].rearrange("p a b -> p (a b)").rearrange("p (t d) -> p t d", d=D)
        xc4 = sg
        sq4 = gl
        late = ampw[:, :, :, :, :].rearrange("p a b s d -> p (a b s d)")
        wo4 = late[0:65, 512:1024].rearrange("p (l o) -> p l o", l=NL)
        wor = prm[:, :, :, :].rearrange("p b t c -> p (b t c)")[:, 0:NL * D].rearrange("p (l d) -> p l d", l=NL)
        lsb = late[:, 0:512].rearrange("p (l k d) -> p l k d", l=NL, k=2)
        w4l = sb("w4l", [65, P])
        lax = cut(32000, 4, 128)

        cm24 = cut(0, 32, 3, E1)
        cm24i = cut(0, 32 * 24, dt=I32).rearrange("p (t q e) -> p t q e", t=32, q=3)
        wg32 = cut(1024, 32, parts=65)
        selr = cut(1056, E1, parts=24)
        fx = cut(2048, 2, 512)
        lgt1 = cut(14848, 2, 512)
        sel = cut(14336, E1 * P // 2, parts=24, dt=BF16).rearrange("p (e q) -> p e q", e=E1)
        cmtp = cut(12288, L * B // 2, parts=24, dt=BF16)
        x65 = cut(8192, 32, P, parts=65)
        h8 = cut(16384, 8, 512)
        w1e = cut(24576, E1, P, parts=64)
        w2e = cut(25600, E1, D)
        b1e = cut(26112, E1)
        bgx = cut(26128, 2, E1, parts=65)
        b2d = cut(26144, 16, D)
        cmb = cut(27168, 32, E1)
        cm2 = cut(27424, 32, E1)
        cm3 = cut(27680, 32, E1)
        cmt = cut(27936, 2, P)
        xn1 = cut(28192, 32, D)
        f1 = cut(30240, 32, D)

        turn = cut(32512, P)

        ps = ctx.enter_context(nc.psum_tensor("ps", [P, 8, 512], F32))

        names = """const_in w_in row_in x_in pos_in oh_ready wt_ps wt_out rt_ps rt_out row_act row_dve
            gat_ps amp_out c1_ps h1_ready c2_ps h2_ready h2_seen c3_ps arg_ready exp_done phase_ready sin_done
            p_ready v_ps v_out_dve v_out_act k_out zk_ready zk_stored coef_ready turned_ready tin_ready ctx_row ctx_stored ctx_in d_order f_order sig_in sig_out
            m_order prb_ready acc_out acc_ps htr_ps ht_out ln_var ln_sd ln_out
            a_in mnt_ps mnt_out g_ps g_out u_ps r_ready lsum_ps amax_ready att_exp wvs_ready gate_ps gate_out
            pv_ps og_ready o_ps ht_att
            e_in rw_ps rw_out x_ps x_out lg_ps oh0_ready oht_ps oht_out hx_ps hm_ready hm_used f0_ps f0_out f0t_ps ht_ffn
            s_in vt_in pt_in t0_in turn_ps lt_ps lt_out xm_ps st_ready y_ps yg_ready yt_in yd_in z_ps sig_done us_out xm_done
            s_order mask_ready
            m_in x65_ps x65_out gl_ps gexp_in gexp_out cmt_ps cmt_out hh_ps hid_out bc_ps hw_out w2_ps
            fx_out ft_ps lgt_out lgr_ps parts_ready ct_ps ct_out_a ct_out_d b2_ps b2d_in out_ready stored
            """.split()
        s = {n: sem(n) for n in names}
        par = {n: [sem(f"{n}_{j}") for j in range(2)] for n in
               ("xq_ready", "ph_ready", "e_done", "s_done", "mul_dve", "mul_pool", "aw_ready", "field_ps", "k_stored")}
        p_stored = [sem(f"p_stored_{c}") for c in range(CHUNKS)]
        v_stored = [sem(f"v_stored_{c}") for c in range(CHUNKS)]
        chunk_used = [sem(f"chunk_used_{c}") for c in range(CHUNKS)]

        def back(x):
            step = x.ap[-1][0]
            return bass.AP(tensor=x.tensor, offset=x.offset + step * (P - 1), ap=[list(x.ap[0]), [-step, P]])

        def past(i):
            return not isinstance(i, int) or i > 0

        class Order:

            def __init__(self, eng, sm, base=0):
                self.eng, self.sm, self.n, self.base = eng, sm, 0, base

            def __call__(self, ins):
                self.n += 1
                ins.then_inc(self.sm, 1)
                self.eng.wait_ge(self.sm, self.base + self.n)

        ln_no = {"attn": 1, "ffn0": 2, "s4in": 3, "s4": 4, "ffn1": 8}
        block = ctx.enter_context(nc.Block())
        col = lambda ap, n: ap.rearrange("(p a) -> p a", a=1) if n else ap
        TWO_PI = 6.2831845
        W_IN = 11 * 16
        ROW_IN = 9 * 16

        @block.sync
        def _(sp):
            def load(dst, src, sm):
                sp.dma_start(dst, src, allow_slow_non_contiguous=True).then_inc(sm, 16)

            load(cst[:, :], a["shape_constants"][:, 0:C_ALL], s["const_in"])
            load(w1r, a["L0_tok_w1"].rearrange("o c k -> o (c k)"), s["w_in"])
            load(w2r, a["L0_tok_w2"].rearrange("o c k -> o (c k)"), s["w_in"])
            load(el[:, 0:D], a["L0_tok_emb"], s["w_in"])
            load(el[:, D:68], a["L0_tok_locality_shapes"], s["w_in"])
            load(w3t, a["L0_tok_w3"].rearrange("o c k -> c (o k)"), s["w_in"])
            load(b1c, col(a["L0_tok_b1"], 1), s["w_in"])
            load(b2c[0:64], col(a["L0_tok_b2"], 1), s["w_in"])
            load(b2c[64:128], col(a["L0_tok_b2"], 1), s["w_in"])
            load(b3c, dram(a["L0_tok_b3"], 0, [[0, P], [1, 1]]), s["w_in"])
            load(msc, dram(a["L0_tok_multiscale_widths"], 0, [[0, P], [1, SC]]), s["w_in"])
            load(swc, dram(a["L0_tok_scale_weights"], 0, [[0, P], [1, SC]]), s["w_in"])
            for j, n in enumerate(("Alog", "Aim", "Cre", "Cim")):
                load(row[:, j], a["L1_attn_" + n].rearrange("(q r) h n -> (r h) q n", r=2), s["row_in"])
            load(ldt, a["L1_attn_log_dt"].rearrange("(q r) h -> (r h) q", r=2), s["row_in"])
            for q in range(4):
                load(skip[32 * q:32 * q + 32], dram(a["L1_attn_D"], q, [[0, 32], [D, NL], [4, 16]]), s["row_in"])
            load(pos[:, :, :], dram(a["fside_BS_continuous_positions"], 0, [[0, P], [L, B], [1, L]]), s["pos_in"])
            sp.wait_ge(s["zk_ready"], 2)
            sp.wait_ge(s["mask_ready"], 1)
            def load_bytes(i):
                if i:
                    sp.wait_ge(s["oh_ready"], i)
                load(xb[0:64, 3:1027], dram(a["x"], i * L, [[0, 64], [1, L]]), s["x_in"])
                load(xb[64:128, 2:1026], dram(a["x"], i * L, [[0, 64], [1, L]]), s["x_in"])

            load_bytes(0)
            for l in range(NL):
                load(k_dram[l][:, 0:P], zk, s["zk_stored"])

            def context(b):
                sp.wait_ge(s["ctx_row"], 2 * b + 2)
                for j in range(2):
                    load(dram(ctx_dram, b * L + 512 * j, [[512, 1], [1, 512]]), crow[64 * j:64 * j + 1, :],
                         s["ctx_stored"])
                sp.wait_ge(s["ctx_stored"], 32 * b + 32)
                load(ctxp[:, NT * b:NT * b + NT], dram(ctx_dram, b * L, [[1, P], [P, NT]]), s["ctx_in"])

            for i in range(NL):
                for c in range(CHUNKS + 1):
                    if c < CHUNKS:
                        sp.wait_ge(s["p_ready"], i * CHUNKS + c + 1)
                        load(p_dram[i][:, c * HCH * P:(c + 1) * HCH * P], pe_t[:, c * HCH:(c + 1) * HCH, :],
                             p_stored[c])
                    if c == 0 and i + 1 < B:
                        load_bytes(i + 1)
                    if c == 2 and i:
                        context(i - 1)
                    if c:
                        d = c - 1
                        sp.wait_ge(s["v_out_dve"], i * 8 + 2 * d + 2)
                        sp.wait_ge(s["v_out_act"], i * 8 + 2 * d + 2)
                        load(v_dram[i][:, d * HCH * P:(d + 1) * HCH * P],
                             vout[d // 2][:, 16 * (d % 2):16 * (d % 2) + 16, :], v_stored[d])
                        sp.wait_ge(s["k_out"], i * 4 + d + 1)
                        for q in range(4):
                            load(dram(k_dram, (i * D + HCH * d + q) * 2 * P + P, [[4 * 2 * P, 1], [4 * 2 * P, 4], [1, P]]),
                                 kst[32 * q:32 * q + 1, d % 2], par["k_stored"][d % 2])
            context(B - 1)
            sp.wait_ge(s["ht_out"], B)
            for j, n in enumerate(("Wq", "Wk", "Wv", "Wg")):
                load(wqkvg[0:64, j], a["L0_attn_" + n], s["a_in"])
                load(wqkvg[64:128, j], a["L0_attn_" + n], s["a_in"])
            load(wo, a["L0_attn_Wo"].rearrange("(g p) d -> p g d", p=P), s["a_in"])
            load(bgc, a["L0_attn_bg"].rearrange("(g p) -> p g", p=P), s["a_in"])
            for j, n in enumerate(("gamma", "beta", "bo")):
                load(gbc[:, j], dram(a["L0_attn_" + n], 0, [[0, P], [1, D]]), s["a_in"])
            load(rwr, a["L0_ffn_router_w"], s["e_in"])
            load(rbb, dram(a["L0_ffn_router_b"], 0, [[0, P], [1, E0]]), s["e_in"])
            for g in range(4):
                load(w1x[0:64, g, :].rearrange("d (e h) -> d e h", e=8),
                     a["L0_ffn_W1"][8 * g:8 * g + 8].rearrange("e d h -> d e h"), s["e_in"])
            load(b1x, a["L0_ffn_b1"].rearrange("(g e) h -> (e h) g", g=4), s["e_in"])
            load(w2x, a["L0_ffn_W2"].rearrange("(g e) h d -> (e h) g d", g=4), s["e_in"])
            load(b2x, a["L0_ffn_b2"], s["e_in"])
            load(wor, a["L1_attn_Wout"].rearrange("l o h -> o l h"), s["s_in"])
            load(wo4[64:65, :, :], dram(a["L1_attn_bout"], 0, [[NL * P, 1], [P, NL], [1, P]]), s["s_in"])
            load(turn, a["shape_constants"][:, C_J:C_J + P], s["s_in"])
            load(lsb[:, :, 0], dram(a["L1_attn_ln_scale"], 0, [[0, P], [D, NL], [1, D]]), s["s_in"])
            load(lsb[:, :, 1], dram(a["L1_attn_ln_bias"], 0, [[0, P], [D, NL], [1, D]]), s["s_in"])
            for c in range(CHUNKS):
                sp.wait_ge(p_stored[c], 16 * NL)
                sp.wait_ge(v_stored[c], 16 * NL)
            for j in range(2):
                sp.wait_ge(par["k_stored"][j], 64 * 2 * NL)
            sp.wait_ge(s["zk_stored"], 16 * NL)
            sp.wait_ge(s["ht_ffn"], 4)
            for l in range(NL):
                if l:
                    sp.wait_ge(s["xm_done"], l)
                load(vt.rearrange("p h t -> p (h t)"), v_dram[l], s["vt_in"])
                if l:
                    sp.wait_ge(s["y_ps"], 4 * l)
                load(pt.rearrange("p h t -> p (h t)"), p_dram[l], s["pt_in"])
                load(t0, dram(k_dram, l * 2 * P * D + 1, [[1, P], [2 * P, D], [1, P]]), s["t0_in"])
                sp.wait_ge(s["z_ps"], 8 * l)
                sp.wait_ge(s["yg_ready"], 4 * l + 4)
                for hq in range(4):
                    load(y_dram[16 * hq:16 * hq + 16].rearrange("h c t -> c h t"), yg[32 * hq:32 * hq + 32, :, :],
                         s["yd_in"])
                sp.wait_ge(s["yd_in"], 64 * (l + 1))
                load(yt[0:64].rearrange("h i b t -> h (i b t)"), y_dram.rearrange("h c t -> h (c t)"), s["yt_in"])
            sp.wait_ge(s["us_out"], NL)
            load(w1e, a["L1_ffn_W1"].rearrange("e d f -> d e f"), s["m_in"])
            load(w2e, a["L1_ffn_W2"].rearrange("e f d -> f e d"), s["m_in"])
            load(b1e, a["L1_ffn_b1"].rearrange("e f -> f e"), s["m_in"])
            sp.wait_ge(s["zk_ready"], 3)
            load(wg32[0:64, 0:E1], a["L1_ffn_Wg"], s["m_in"])
            load(selr, a["shape_constants"][0:24, C_SEL:C_SEL + E1], s["m_in"])
            load(bgx[64:65, 0], dram(a["L1_ffn_bg"], 0, [[E1, 1], [1, E1]]), s["m_in"])
            load(bgx[64:65, 1], dram(a["L1_ffn_bias"], 0, [[E1, 1], [1, E1]]), s["m_in"])
            sp.wait_ge(s["zk_ready"], 4)
            for t in range(16):
                load(b2d[8 * t:8 * t + 8, t, :], a["L1_ffn_b2"], s["b2d_in"])
            for k in range(4):
                sp.wait_ge(s["out_ready"], k + 1)
                for i in range(2 * k, 2 * k + 2):
                    load(dram(a["out"], i * P * D, [[D, P], [L * D, B], [1, D]]), ht[:, i], s["stored"])
            sp.wait_ge(s["stored"], 16 * NT)

        @block.gpsimd
        def _(pool):
            pool.memset(zk, 0.0).then_inc(s["zk_ready"], 1)
            pool.memset(h1, 0.0).then_inc(s["zk_ready"], 1)
            pool.wait_ge(s["rt_out"], 1)
            def exponents(l, c):
                hs = slice(c * HCH, (c + 1) * HCH)
                rate = rt[:, 0, bass.ds(l, 1), hs].rearrange("p a h -> p (a h)")
                pool.tensor_tensor(pe_t[:, hs, :], rate.rearrange("p (h a) -> p h a", a=1).broadcast_to([P, HCH, P]),
                                   trow.rearrange("p (a t) -> p a t", a=1).broadcast_to([P, HCH, P]),
                                   ALU.mult).then_inc(s["arg_ready"], 1)

            def turned(l, c):
                hs = slice(c * HCH, (c + 1) * HCH)
                turns = rt[:, 1, bass.ds(l, 1), hs].rearrange("p a h -> p (a h)")
                pool.tensor_tensor(ph_t[:, hs, :], turns.rearrange("p (h a) -> p h a", a=1).broadcast_to([P, HCH, P]),
                                   trow.rearrange("p (a t) -> p a t", a=1).broadcast_to([P, HCH, P]),
                                   ALU.mult).then_inc(s["turned_ready"], 1)

            for c in range(CHUNKS):
                turned(0, c)
            for c in range(CHUNKS):
                exponents(0, c)
            with pool.Fori(0, NL - 1) as l:
                for c in range(CHUNKS + 1):
                    if c < CHUNKS:
                        pool.wait_ge(s["p_ready"], l * 4 + c + 1)
                        turned(l + 1, c)
                    if c:
                        pool.wait_ge(p_stored[c - 1], l * 16 + 16)
                        pool.wait_ge(chunk_used[c - 1], l + 1)
                        exponents(l + 1, c - 1)
            for it in range(2):
                for g in range(8):
                    p, bp, st = g % 2, g // 4, 2 * (g % 4)
                    pool.wait_ge(s["prb_ready"], it * 2 + bp + 1)
                    pool.wait_ge(par["field_ps"][p], it * 4 + g // 2)
                    for j in range(2):
                        rows = amp[:, bass.ds(it * 16 + bp * 8 + st + j, 1), 0:D].broadcast_to([P, SC, D])
                        ins = pool.tensor_tensor(ampw[:, p, j], rows,
                                                 prb[:, bp, st + j, 13:17].rearrange("p (s a) -> p s a", a=1)
                                                 .broadcast_to([P, SC, D]), ALU.mult)
                    ins.then_inc(par["aw_ready"][p], 1)
                    pool.wait_ge(par["e_done"][p], it * 4 + g // 2 + 1)
                    pool.wait_ge(par["s_done"][p], it * 4 + g // 2 + 1)
                    pool.tensor_tensor(eb[p][:, 1], eb[p][:, 1], qb[p][:, 1], ALU.mult)\
                        .then_inc(par["mul_pool"][p], 1)
            pool.wait_ge(s["us_out"], NL)
            pool.memset(wg32, 0.0).then_inc(s["zk_ready"], 1)
            pool.memset(b2d, 0.0).then_inc(s["zk_ready"], 1)

        @block.scalar
        def _(act):
            A = act.activation
            act.wait_ge(s["row_in"], ROW_IN)
            A(dtc, ldt, ACT.Exp).then_inc(s["row_act"], 1)
            A(row[:, 4], row[:, 0], ACT.Exp).then_inc(s["row_act"], 1)
            act.wait_ge(s["row_dve"], 1)
            A(row[:, 8], row[:, 5], ACT.Tanh, scale=0.5).then_inc(s["row_act"], 1)
            A(row[:, 9], row[:, 5], ACT.Exp).then_inc(s["row_act"], 1)
            A(row[:, 10], row[:, 5], ACT.Exp, scale=128.0).then_inc(s["row_act"], 1)
            act.wait_ge(s["row_dve"], 2)
            A(row[:, 16:21], row[:, 11:16], ACT.Sin, scale=TWO_PI).then_inc(s["row_act"], 1)
            def decay(i, c):
                hs = slice(c * HCH, (c + 1) * HCH)
                act.wait_ge(s["arg_ready"], i * 4 + c + 1)
                A(pe_t[:, hs, :], pe_t[:, hs, :], ACT.Exp).then_inc(s["exp_done"], 1)

            def sines(i, c):
                hs = slice(c * HCH, (c + 1) * HCH)
                act.wait_ge(s["phase_ready"], i * 4 + c + 1)
                A(ph_t[:, hs, :], ph_t[:, hs, :], ACT.Sin, scale=TWO_PI, bias=n3pi).then_inc(s["sin_done"], 1)

            for c in range(CHUNKS):
                sines(0, c)
            for c in range(CHUNKS):
                decay(0, c)

            def context_out(i):
                act.wait_ge(s["c3_ps"], i)
                if not isinstance(i, int) or i > 1:
                    act.wait_ge(s["ctx_stored"], (i - 1) * 32)
                for j in range(2):
                    A(crow[64 * j:64 * j + 1, :], ps[64 * j:64 * j + 1, 2, :], ACT.Copy).then_inc(s["ctx_row"], 1)

            def step(i, last=False):
                def table_out(c):
                    if past(i):
                        act.wait_ge(v_stored[c], i * 16)
                    for g in (4 * c + 1, 4 * c + 3):
                        act.wait_ge(s["v_ps"], i * 16 + g + 1)
                        h = 4 * (g % 8)
                        A(vout[c // 2][:, h:h + 4, :].rearrange("p h t -> p (h t)"), ps[:, 6, :], ACT.Copy)\
                            .then_inc(s["v_out_act"], 1)

                def ahead(what, *chunks):
                    if not last:
                        for c in chunks:
                            what(i + 1, c)

                table_out(0)
                table_out(1)
                ahead(sines, 0)
                if past(i):
                    context_out(i)
                for j in range(2):
                    act.wait_ge(s["c1_ps"], i * 2 + j + 1)
                    act.wait_ge(s["zk_ready"], 2)
                    if past(i):
                        act.wait_ge(s["c2_ps"], i)
                    A(h1[:, 2 + 512 * j:514 + 512 * j], ps[:, j, :], ACT.Gelu, bias=b1c).then_inc(s["h1_ready"], 1)
                table_out(2)
                ahead(sines, 1)
                table_out(3)
                ahead(sines, 2, 3)
                ahead(decay, 0, 1)
                act.wait_ge(s["c2_ps"], i + 1)
                act.wait_ge(s["mask_ready"], 1)
                if past(i):
                    act.wait_ge(s["ctx_row"], i * 2)
                for j in range(2):
                    A(h2[:, 1 + 512 * j:513 + 512 * j], ps[64 * j:64 * j + 64, 2, :], ACT.Gelu,
                      bias=b2c[64 * j:64 * j + 64]).then_inc(s["h2_ready"], 1)
                ahead(decay, 2, 3)
            step(0)
            step(1)
            with act.Fori(2, NL - 1) as i:
                step(i)
            step(NL - 1, True)
            context_out(NL)
            act.wait_ge(s["sig_in"], 1)
            act.wait_ge(s["ctx_in"], 16 * B)
            A(post[:, 2, :, 0], ctxp[:, :], ACT.Sigmoid, bias=b3c).then_inc(s["sig_out"], 1)
            A(post[:, 3, :, 0], amp[:, :, 66], ACT.Sigmoid).then_inc(s["sig_out"], 1)
            for it in range(2):
                def gauss(g):
                    p, bp, st, k = g % 2, g // 4, 2 * (g % 4), g // 2
                    act.wait_ge(par["xq_ready"][p], it * 4 + k + 1)
                    act.wait_ge(par["field_ps"][p], it * 4 + k)
                    for j in range(2):
                        for sc in range(SC):
                            ins = A(eb[p][:, j, sc], xq[:, p, j], ACT.Exp,
                                    scale=prb[:, bp, st + j, 9 + sc:10 + sc])
                    ins.then_inc(par["e_done"][p], 1)

                def wave(g):
                    p, k = g % 2, g // 2
                    act.wait_ge(par["ph_ready"][p], it * 4 + k + 1)
                    A(qb[p], qb[p], ACT.Sin, scale=TWO_PI, bias=n3pi).then_inc(par["s_done"][p], 1)

                def field_out(bp):
                    act.wait_ge(s["acc_ps"], it * 2 + bp + 1)
                    act.wait_ge(s["htr_ps"], it * 2 + bp)
                    A(accs[:, :], ps[:, bp, :], ACT.Copy).then_inc(s["acc_out"], 1)

                for g in range(8):
                    (gauss if g % 2 == 0 else wave)(g)
                    (wave if g % 2 == 0 else gauss)(g)
                    if g == 4:
                        field_out(0)
                field_out(1)

            def sqrt(k):
                act.wait_ge(s["ln_var"], k)
                A(lnw[:, 3], lnw[:, 2], ACT.Sqrt).then_inc(s["ln_sd"], 1)

            sqrt(1)
            act.wait_ge(s["ln_var"], 2)
            A(lnw[:, 3], lnw[:, 2], ACT.Sqrt).then_inc(s["ln_sd"], 1)
            for j in range(2):
                act.wait_ge(s["mnt_ps"], 3 + j)
                A(mnt[:, 1, 512 * j:512 * j + 512], ps[:, 2 + j, :], ACT.Copy).then_inc(s["mnt_out"], 1)
            act.wait_ge(s["amax_ready"], 1)
            A(att.rearrange("p a b c d e -> p (a b c d e)"), amx.rearrange("p a b -> p (a b)"), ACT.Exp)\
                .then_inc(s["att_exp"], 1)
            act.wait_ge(s["a_in"], 16 * 13)
            for u in range(16):
                act.wait_ge(s["gate_ps"], u + 1)
                g, b, j = u % 2, u // 4, (u // 2) % 2
                A(gt[:, g, b, 512 * j:512 * j + 512], ps[:, 4 + u % 2, :], ACT.Sigmoid, bias=bgc[:, g:g + 1])\
                    .then_inc(s["gate_out"], 1)
            sqrt(3)
            for k in range(4):
                act.wait_ge(s["x_ps"], 2 * k + 2)
                A(x96[0:64, 8 * k + 4:8 * k + 8, :], ps[0:64, 1, :], ACT.Copy).then_inc(s["x_out"], 1)
            for k in range(4):
                for j in range(2):
                    for g in range(4):
                        u = 8 * k + 4 * j + g
                        if u % 2:
                            continue
                        act.wait_ge(s["hx_ps"], u + 1)
                        if k:
                            act.wait_ge(s["f0_ps"], k)
                        A(hm[:, j, g], ps[:, 2 + u % 4, :], ACT.Relu, bias=b1x[:, g:g + 1]).then_inc(s["hm_ready"], 1)
                act.wait_ge(s["f0_ps"], k + 1)
                if k:
                    act.wait_ge(s["f0t_ps"], k)
                A(f0, ps[:, 6, :], ACT.Relu).then_inc(s["f0_out"], 1)
            sqrt(4)
            def step(l):
                act.wait_ge(s["ln_var"], l + 5)
                A(lnw[:, 3], lnw[:, 2], ACT.Sqrt).then_inc(s["ln_sd"], 1)
                for g in range(4):
                    act.wait_ge(s["y_ps"], l * 4 + g + 1)
                    if past(l):
                        act.wait_ge(s["yd_in"], l * 64)
                    A(yg[:, 4 * g:4 * g + 4, :], ps[:, 4 + g, :].rearrange("p (g t) -> p g t", g=4),
                      ACT.Gelu_apprx_tanh).then_inc(s["yg_ready"], 1)
                for g in range(8):
                    act.wait_ge(s["z_ps"], l * 8 + g + 1)
                    A(sg[:, 4 * g:4 * g + 4, :], ps[:, g, :].rearrange("p (t d) -> p t d", t=4)[:, :, D:P],
                      ACT.Sigmoid).then_inc(s["sig_done"], 1)
            step(0)
            with act.Fori(1, NL) as l:
                step(l)
            sqrt(9)
            for k in range(4):
                act.wait_ge(s["x65_ps"], 2 * k + 2)
                A(x65[0:64, 8 * k + 4:8 * k + 8, :], ps[0:64, 1, :], ACT.Copy).then_inc(s["x65_out"], 1)
            act.wait_ge(s["gl_ps"], 2)
            A(lgt1[:, 1], ps[:, 3, :], ACT.Copy).then_inc(s["lgt_out"], 1)
            act.wait_ge(s["gexp_in"], 1)
            A(lnw[:, 5], lnw[:, 4], ACT.Exp).then_inc(s["gexp_out"], 1)
            for c in range(0, 8, 2):
                act.wait_ge(s["ct_ps"], c + 1)
                A(cmtp[:, 512 * c:512 * c + 512], ps[0:24, 3, :], ACT.Copy).then_inc(s["ct_out_a"], 1)
            act.wait_ge(s["m_in"], 16 * 7)
            for n in range(69):
                if n < 64:
                    act.wait_ge(s["hh_ps"], n + 1)
                    if n >= 8:
                        act.wait_ge(s["w2_ps"], (n - 8) // 2 + 1)
                    e = (n // 2) % E1
                    A(h8[:, n % 8, :], ps[:, n % 3, :], ACT.Relu, bias=b1e[:, e:e + 1]).then_inc(s["hid_out"], 1)
                if n % 16 == 4 and n > 16:
                    k = n // 16 - 1
                    act.wait_ge(s["w2_ps"], 8 * k + 8)
                    if k >= 2:
                        act.wait_ge(s["ft_ps"], k - 1)
                    A(fx[:, k % 2], ps[:, 5 + k % 2, :], ACT.Copy).then_inc(s["fx_out"], 1)

        @block.tensor
        def _(pe):
            def mm(out, lhsT, rhs, start=True, stop=True):
                return pe.matmul(out, lhsT, rhs, start=start, stop=stop)

            pe.wait_ge(s["const_in"], 16)
            pe.wait_ge(s["w_in"], W_IN)
            w1v = w1r.rearrange("o (c k) -> o k c", k=7)
            w2v = w2r.rearrange("o (c k) -> o k c", k=5)
            for j in range(3):
                for r in range(2):
                    mm(ps[64 * r:64 * r + 64, 0, P * j:P * j + P], w1v[:, 2 * j + r], ident)
            mm(ps[0:64, 0, 3 * P:4 * P], w1v[:, 6], ident).then_inc(s["wt_ps"], 1)
            for k in range(5):
                ins = mm(ps[:, 1, D * k:D * k + D], w2v[:, k], ident[0:64, 0:64])
            ins.then_inc(s["wt_ps"], 1)
            for q in range(7):
                if q in (0, 2):
                    pe.wait_ge(s["tin_ready"], q // 2 + 1)
                for r in range(2):
                    k = 2 * q + r
                    ins = pe.transpose(ps[:, 2 + k // 4, P * (k % 4):P * (k % 4) + P],
                                       tin[:, q, r].rearrange("p a n -> p (a n)"), ident)
                if q in (1, 6):
                    ins.then_inc(s["rt_ps"], 1)
            pe.wait_ge(s["wt_out"], 2)
            pe.wait_ge(s["rt_out"], 2)
            def third_conv(i):
                pe.wait_ge(s["h2_ready"], i * 2)
                pe.nop().then_inc(s["h2_seen"], 1)
                for k in range(3):
                    for j in range(2):
                        ins = mm(ps[64 * j:64 * j + 1, 2, :], w3t[:, k:k + 1], h2[:, k + 512 * j:k + 512 * j + 512],
                                 k == 0, k == 2)
                ins.then_inc(s["c3_ps"], 1)

            def step(i):
                pe.wait_ge(s["coef_ready"], i + 1)
                for c in range(CHUNKS):
                    pe.wait_ge(s["p_ready"], i * 4 + c + 1)
                    for g in range(4):
                        gg = 4 * c + g
                        if past(i) or gg >= 2:
                            pe.wait_ge(s["v_out_act"] if gg % 2 else s["v_out_dve"], i * 8 + gg // 2)
                        for q in range(4):
                            ins = pe.transpose(ps[:, 5 + gg % 2, P * q:P * q + P], pe_t[:, 4 * gg + q, :], ident)
                        ins.then_inc(s["v_ps"], 1)
                    if past(i) or c:
                        pe.wait_ge(s["k_out"], i * 4 + c)
                    for g in range(4):
                        for q in range(4):
                            h = HCH * c + 4 * g + q
                            ins = mm(ps[32 * q:32 * q + 32, 7, P * g:P * g + P], coef[:, h:h + 32], pe_t[:, h, :])
                    ins.then_inc(chunk_used[c], 1)
                    if c < 2:
                        pe.wait_ge(s["oh_ready"], i + 1)
                        if past(i):
                            pe.wait_ge(s["h1_ready"], i * 2)
                        for k in range(3):
                            mm(ps[:, c, :], w1t[:, k], oh[:, 2 * k + 512 * c:2 * k + 512 * c + 512], k == 0, False)
                        mm(ps[:, c, :], w1t[0:64, 3], oh[0:64, 6 + 512 * c:518 + 512 * c], False, True)\
                            .then_inc(s["c1_ps"], 1)
                    if c == 1 and past(i):
                        third_conv(i)
                    if c == 2:
                        if past(i):
                            pe.wait_ge(s["amp_out"], i * 2)
                        for t in range(NT):
                            ins = mm(ps[:, 3 + t // 4, 68 * (t % 4):68 * (t % 4) + 68],
                                     oh[0:64, 3 + P * t:3 + P * t + P], el)
                        ins.then_inc(s["gat_ps"], 1)
                pe.wait_ge(s["h1_ready"], i * 2 + 2)
                if past(i):
                    pe.wait_ge(s["ctx_row"], i * 2)
                for k in range(5):
                    for j in range(2):
                        ins = mm(ps[64 * j:64 * j + 64, 2, :], w2t[:, k], h1[:, k + 512 * j:k + 512 * j + 512],
                                 k == 0, k == 4)
                ins.then_inc(s["c2_ps"], 1)
            step(0)
            with pe.Fori(1, NL) as i:
                step(i)
            third_conv(NL)
            for it in range(2):
                def turn_out(bp):
                    pe.wait_ge(s["acc_out"], it * 2 + bp + 1)
                    pe.wait_ge(s["ht_out"], it * 2 + bp)
                    for c in range(4):
                        ins = pe.transpose(ps[:, 2, P * c:P * c + P], accs[:, P * c:P * c + P], ident)
                    ins.then_inc(s["htr_ps"], 1)

                for g in range(8):
                    p, bp, k = g % 2, g // 4, g // 2
                    pe.wait_ge(par["aw_ready"][p], it * 4 + k + 1)
                    if g % 4 == 0:
                        pe.wait_ge(s["acc_out"], it * 2)
                    for j in range(2):
                        pe.wait_ge(par["mul_pool" if j else "mul_dve"][p], it * 4 + k + 1)
                        for sc in range(SC):
                            for hf in range(2):
                                ins = mm(ps[64 * hf:64 * hf + 64, bp, :], ampw[:, p, j, sc],
                                         eb[p][:, j, sc, 512 * hf:512 * hf + 512],
                                         g % 4 == 0 and j == 0 and sc == 0, g % 4 == 3 and j == 1 and sc == SC - 1)
                    ins.then_inc(par["field_ps"][p], 1)
                    if g % 4 == 3:
                        pe.wait_ge(par["field_ps"][p], it * 4 + k + 1)
                        pe.nop().then_inc(s["acc_ps"], 1)
                    if g == 4:
                        turn_out(0)
                turn_out(1)
            pe.wait_ge(s["ln_out"], 1)
            for bp in range(2):
                for i in range(NT):
                    ins = pe.transpose(ps[:, 2 * bp + i // 4, P * (i % 4):P * (i % 4) + P],
                                       mn[:, i, 2 * bp:2 * bp + 2, :].rearrange("p b d -> p (b d)"), ident)
                    if i % 4 == 3:
                        ins.then_inc(s["mnt_ps"], 1)
            for sp_ in range(2):
                for i in range(NT):
                    ins = mm(ps[:, 4, 256 * sp_:256 * sp_ + 256],
                             mn[:, i, 2 * sp_:2 * sp_ + 2, :].rearrange("p b d -> p (b d)"),
                             mn[:, i].rearrange("p b d -> p (b d)"), i == 0, i == NT - 1)
            ins.then_inc(s["g_ps"], 1)
            pe.wait_ge(s["g_out"], 1)
            pe.wait_ge(s["a_in"], 16 * 13)
            pe.wait_ge(s["mnt_out"], 4)
            for tp in range(2):
                for sp_ in range(2):
                    for t2 in range(2):
                        ins = mm(ps[:, 2 * t2 + tp, 256 * sp_:256 * sp_ + 256],
                                 gr[64 * t2:64 * t2 + 64, tp, 128 * sp_:128 * sp_ + 128],
                                 wqkvg[64 * t2:64 * t2 + 64, 1])
            ins.then_inc(s["u_ps"], 1)
            pe.wait_ge(s["r_ready"], 1)
            r2f = r2.rearrange("p a h -> p (a h)")
            mm(ps[:, 4, 0:64], cst[:, C_LO:C_LO + P], r2f)
            mm(ps[:, 4, 64:128], cst[:, C_HI:C_HI + P], r2f).then_inc(s["lsum_ps"], 1)
            pe.wait_ge(s["amax_ready"], 1)
            pe.wait_ge(s["wvs_ready"], 1)
            for u in range(16):
                g, b, j = u % 2, u // 4, (u // 2) % 2
                rows = slice(64 * (b % 2), 64 * (b % 2) + 64)
                if u >= 2:
                    pe.wait_ge(s["gate_out"], u - 1)
                    pe.wait_ge(s["gate_ps"], u)
                mm(ps[:, 4 + u % 2, :], wqkvg[rows, 3, P * g:P * g + P], mnt[rows, b // 2, 512 * j:512 * j + 512])\
                    .then_inc(s["gate_ps"], 1)
                if u >= 2:
                    pe.wait_ge(s["og_ready"], u - 1)
                for tp in range(2):
                    ins = mm(ps[:, 6 + u % 2, :], wvs[:, b // 2, b % 2, tp, P * g:P * g + P],
                             mnt[:, tp, 512 * j:512 * j + 512], tp == 0, tp == 1)
                ins.then_inc(s["pv_ps"], 1)
            pe.wait_ge(s["og_ready"], 16)
            for t in range(32):
                i, b = t // 4, t % 4
                for g in range(2):
                    ins = mm(ps[:, t // 8, D * (t % 8):D * (t % 8) + D], gt[:, g, b, P * i:P * i + P], wo[:, g],
                             g == 0, g == 1)
                if t % 8 == 7:
                    ins.then_inc(s["o_ps"], 1)
            pe.wait_ge(s["e_in"], 16 * 9)
            pe.wait_ge(s["ht_att"], 4)
            pe.transpose(ps[0:64, 7, 0:E0], rwr, ident[0:32, 0:32]).then_inc(s["rw_ps"], 1)
            pe.wait_ge(s["ln_out"], 2)
            for k in range(8):
                if k >= 2:
                    pe.wait_ge(s["x_out"] if k % 2 else s["rw_out"], k // 2 if k % 2 else k // 2 + 1)
                for t in range(4):
                    ins = pe.transpose(ps[0:64, k % 2, P * t:P * t + P], xn[:, 4 * k + t], ident)
                ins.then_inc(s["x_ps"], 1)
            pe.wait_ge(s["rw_out"], 5)
            pe.wait_ge(s["x_out"], 4)
            for t in range(32):
                ins = mm(ps[:, 2 + t // 16, E0 * (t % 16):E0 * (t % 16) + E0], x96[0:64, t], rwt)
            ins.then_inc(s["lg_ps"], 1)
            for k in range(8):
                pe.wait_ge(s["oh0_ready"], 1)
                pe.wait_ge(s["oht_out"], 2 * max(k - 1, 0))
                for t in range(4):
                    ins = pe.transpose(ps[0:32, k % 2, P * t:P * t + P], o2[:, 4 * k + t], ident)
                ins.then_inc(s["oht_ps"], 1)
            pe.wait_ge(s["oht_out"], 16)
            pe.wait_ge(s["mask_ready"], 2)
            for k in range(4):
                for j in range(2):
                    c = 2 * k + j
                    for g in range(4):
                        u = 8 * k + 4 * j + g
                        if u >= 4:
                            pe.wait_ge(s["hm_ready"] if u % 2 == 0 else s["hm_used"], (u - 4) // 2 + 1)
                        mm(ps[:, 2 + u % 4, :], w1x[:, g],
                           x96[0:96, 4 * c:4 * c + 4, :].rearrange("p t q -> p (t q)")).then_inc(s["hx_ps"], 1)
                pe.wait_ge(s["hm_ready"], 4 * k + 4)
                pe.wait_ge(s["hm_used"], 4 * k + 4)
                if k:
                    pe.wait_ge(s["f0_out"], k)
                for g in range(4):
                    for j in range(2):
                        mm(ps[64 * j:64 * j + 64, 6, :], w2x[:, g], hm[:, j, g], g == 0, False)
                for j in range(2):
                    c = 2 * k + j
                    ins = mm(ps[64 * j:64 * j + 64, 6, :], b2x,
                             oht[:, 4 * c:4 * c + 4, :].rearrange("p t q -> p (t q)"), False, True)
                ins.then_inc(s["f0_ps"], 1)
                pe.wait_ge(s["f0_out"], k + 1)
                if k:
                    pe.wait_ge(s["ht_ffn"], k)
                for b in range(B):
                    ins = pe.transpose(ps[:, 7, P * b:P * b + P], f0[:, P * b:P * b + P], ident)
                ins.then_inc(s["f0t_ps"], 1)
            pe.wait_ge(s["s_in"], 80)
            for l in range(NL):
                ins = pe.transpose(ps[0:64, 0, P * l:P * l + P], wor[:, l, :], ident)
            ins.then_inc(s["lt_ps"], 1)
            pe.wait_ge(s["lt_out"], 2)
            pe.wait_ge(s["ln_out"], 3)
            for k in range(4):
                ins = mm(ps[:, 4 + k, :], turn, uu[:, 8 * k:8 * k + 8, :].rearrange("p t d -> p (t d)"))
                ins.then_inc(s["turn_ps"], 1)
            def step(l):
                pe.wait_ge(s["ln_out"], l + 4)
                pe.wait_ge(s["vt_in"], l * 16 + 16)
                if past(l):
                    pe.wait_ge(s["us_out"], l)
                for h in range(D):
                    ins = mm(ps[:, h // 16, 32 * (h % 16):32 * (h % 16) + 28], vt[:, h, :], uu[:, 0:28, h])
                    if h % 16 == 15:
                        ins.then_inc(s["xm_ps"], 1)
                pe.wait_ge(s["xm_ps"], l * 4 + 4)
                pe.nop().then_inc(s["xm_done"], 1)
                pe.wait_ge(s["t0_in"], l * 16 + 16)
                pe.wait_ge(s["pt_in"], l * 16 + 16)
                pe.wait_ge(s["st_ready"], l + 1)
                for g in range(16):
                    for hq in range(4):
                        h = 16 * hq + g
                        mm(ps[32 * hq:32 * hq + 32, 4 + g // 4, P * (g % 4):P * (g % 4) + P], uu[:, :, h],
                           back(t0[:, h, :]), True, False)
                    for hq in range(4):
                        h = 16 * hq + g
                        ins = mm(ps[32 * hq:32 * hq + 32, 4 + g // 4, P * (g % 4):P * (g % 4) + P], sbt[:, h, :],
                                 back(pt[:, h, :]), False, True)
                    if g % 4 == 3:
                        ins.then_inc(s["y_ps"], 1)
                pe.wait_ge(s["yt_in"], l * 16 + 16)
                pe.wait_ge(s["yg_ready"], l * 4 + 4)
                for t in range(32):
                    ins = mm(ps[:, t // 4, P * (t % 4):P * (t % 4) + P], yt[:, t // 4, t % 4, :],
                             w4l[:, :])
                    if t % 4 == 3:
                        ins.then_inc(s["z_ps"], 1)
            step(0)
            with pe.Fori(1, NL) as l:
                step(l)
            for k in range(4):
                pe.wait_ge(s["us_out"], NL)
                mm(ps[:, k, :], turn, us[:, 8 * k:8 * k + 8, :].rearrange("p t d -> p (t d)"))\
                    .then_inc(s["turn_ps"], 1)
            pe.wait_ge(s["ln_out"], 8)
            pe.wait_ge(s["us_out"], NL)
            for k in range(8):
                if k >= 2:
                    pe.wait_ge(s["x65_out"] if k % 2 else s["rw_out"], k // 2 if k % 2 else 5 + k // 2)
                for t in range(4):
                    ins = pe.transpose(ps[0:64, k % 2, P * t:P * t + P], xn1[:, 4 * k + t], ident)
                ins.then_inc(s["x65_ps"], 1)
            pe.wait_ge(s["rw_out"], 9)
            pe.wait_ge(s["x65_out"], 4)
            pe.wait_ge(s["mask_ready"], 4)
            pe.wait_ge(s["m_in"], 16 * 7)
            for c in range(8):
                ins = mm(ps[32 * (c % 4):32 * (c % 4) + 32, 2 + c // 4, :], wg32,
                         x65[0:65, 4 * c:4 * c + 4, :].rearrange("p t q -> p (t q)"))
                if c % 4 == 3:
                    ins.then_inc(s["gl_ps"], 1)
            pe.wait_ge(s["lgt_out"], 2)
            for r in range(2):
                for b in range(B):
                    ins = pe.transpose(ps[:, 4 + r, P * b:P * b + P], lgt1[:, r, P * b:P * b + P], ident)
            ins.then_inc(s["lgr_ps"], 1)
            pe.wait_ge(s["parts_ready"], 1)
            for c in range(8):
                if c >= 2:
                    pe.wait_ge(s["ct_out_d"] if c % 2 else s["ct_out_a"], c // 2)
                for b in range(B):
                    ins = pe.transpose(ps[0:24, 3 + c % 2, P * b:P * b + P],
                                       cm24[:, 4 * c + b].rearrange("p q e -> p (q e)"), ident)
                ins.then_inc(s["ct_ps"], 1)
            pe.wait_ge(s["b2d_in"], 256)
            for r in range(2):
                ins = pe.transpose(ps[:, 7, P * r:P * r + P],
                                   cmb[:, 16 * r:16 * r + 16, :].rearrange("p t e -> p (t e)"), ident)
            ins.then_inc(s["cmt_ps"], 1)
            pe.wait_ge(s["cmt_out"], 1)
            pe.wait_ge(s["ct_out_d"], 4)
            for r in range(2):
                for q in range(2):
                    ins = mm(ps[:, [5, 6, 7, 4][2 * r + q], :], cmt[:, r],
                             b2d[:, 8 * q:8 * q + 8, :].rearrange("p t d -> p (t d)"))
            ins.then_inc(s["b2_ps"], 1)
            pe.wait_ge(s["ct_out_a"], 4)
            for n in range(72):
                if n < 64:
                    k, e, j = n // 16, (n // 2) % E1, n % 2
                    c = 2 * k + j
                    if n >= 3:
                        pe.wait_ge(s["hid_out"], n - 2)
                    mm(ps[:, n % 3, :], w1e[:, e], x65[0:64, 4 * c:4 * c + 4, :].rearrange("p t q -> p (t q)"))\
                        .then_inc(s["hh_ps"], 1)
                    if n == 1:
                        pe.wait_ge(s["cmt_out"], 2)
                    if n >= 2:
                        pe.wait_ge(s["hw_out"], n - 1)
                    mm(ps[:, 3 + n % 2, :], sel[:, e], cmtp[:, 512 * c:512 * c + 512]).then_inc(s["bc_ps"], 1)
                if n % 2 == 1 and 5 <= n < 69:
                    u = n - 5
                    k, e = u // 16, (u // 2) % E1
                    pe.wait_ge(s["hw_out"], u + 2)
                    if e == 0 and k >= 2:
                        pe.wait_ge(s["fx_out"], k - 1)
                    for j in range(2):
                        ins = mm(ps[64 * j:64 * j + 64, 5 + k % 2, :], w2e[:, e], h8[:, (u + j) % 8, :],
                                 e == 0, e == E1 - 1)
                    ins.then_inc(s["w2_ps"], 1)
                if n % 16 == 7 and n > 16:
                    k = n // 16 - 1
                    pe.wait_ge(s["fx_out"], k + 1)
                    if k:
                        pe.wait_ge(s["out_ready"], k)
                    for b in range(B):
                        ins = pe.transpose(ps[:, 7, P * b:P * b + P], fx[:, k % 2, P * b:P * b + P], ident)
                    ins.then_inc(s["ft_ps"], 1)

        @block.vector
        def _(v):
            TT, TS, TC = v.tensor_tensor, v.tensor_scalar, v.tensor_copy

            def bc(ap, n):
                return ap.rearrange("p (k a) -> p k a", a=1).broadcast_to([ap.shape[0], ap.shape[1], n])

            def bcr(ap, n):
                return ap.rearrange("p (a k) -> p a k", a=1).broadcast_to([ap.shape[0], n, ap.shape[1]])

            od = Order(v, s["d_order"])
            od(v.memset(xb, -1))
            v.memset(h2, 0.0).then_inc(s["mask_ready"], 1)
            R = lambda j: row[:, j].rearrange("p q n -> p (q n)")
            v.wait_ge(s["row_act"], 2)
            for q in range(2):
                od(TS(row[:, 5, q], row[:, 4, q], dtc[:, q:q + 1], -1.0, ALU.mult, ALU.mult))
                od(TS(row[:, 6, q], row[:, 1, q], dtc[:, q:q + 1], 1.0 / 6.283185307179586, ALU.mult, ALU.mult))
            v.nop().then_inc(s["row_dve"], 1)

            def whole(dst, src, tmp):
                od(TS(tmp, src, ROUND, ROUND, ALU.add, ALU.subtract))
                od(TT(dst, src, tmp, ALU.subtract))

            whole(R(7), R(6), R(21))
            for r in range(2):
                od(TC(tin[:, 0, :, r], row[:, 5]))
                od(TS(tin[:, 1, :, r], row[:, 7], 2.0 ** MANT, None, ALU.mult))
            v.nop().then_inc(s["tin_ready"], 1)
            od(TC(R(11), R(7)))
            od(TS(R(22), R(7), 0.25, None, ALU.add))
            whole(R(12), R(22), R(21))
            od(TS(R(13), R(7), 0.5, None, ALU.mult))
            od(TS(R(22), R(7), 128.0, None, ALU.mult))
            whole(R(14), R(22), R(21))
            od(TS(R(22), R(14), 0.25, None, ALU.add))
            whole(R(15), R(22), R(21))
            v.nop().then_inc(s["row_dve"], 1)
            v.wait_ge(s["rt_ps"], 1)
            for q in range(2):
                od(TC(rt[:, q].rearrange("p l h -> p (l h)"), ps[:, 2, 256 * q:256 * q + 256]))
            v.nop().then_inc(s["rt_out"], 1)
            v.wait_ge(s["row_act"], 6)
            od(TS(R(21), R(8), -1.0, 1.0, ALU.mult, ALU.add))
            od(v.reciprocal(R(22), R(21)))
            od(TT(R(21), R(8), R(22), ALU.mult))
            od(TS(R(21), R(21), 2.0, None, ALU.mult))
            od(TT(R(21), R(21), R(17), ALU.mult))
            od(TT(R(22), R(18), R(18), ALU.mult))
            od(TS(R(22), R(22), -2.0, None, ALU.mult))
            od(TT(R(21), R(21), R(22), ALU.add))
            od(TT(R(22), R(9), R(16), ALU.mult))
            od(TT(R(23), R(4), R(4), ALU.mult))
            od(TT(R(24), R(1), R(1), ALU.mult))
            od(TT(R(23), R(23), R(24), ALU.add))
            od(v.reciprocal(R(23), R(23)))
            od(TT(R(24), R(22), R(1), ALU.mult))
            od(TT(R(25), R(21), R(4), ALU.mult))
            od(TT(R(24), R(24), R(25), ALU.subtract))
            od(TT(R(24), R(24), R(23), ALU.mult))
            od(TT(R(25), R(22), R(4), ALU.mult))
            od(TT(R(21), R(21), R(1), ALU.mult))
            od(TT(R(25), R(25), R(21), ALU.add))
            od(TT(R(25), R(25), R(23), ALU.mult))
            od(TS(R(25), R(25), -1.0, None, ALU.mult))
            od(TT(R(21), R(2), R(24), ALU.mult))
            od(TT(R(22), R(3), R(25), ALU.mult))
            od(TT(R(21), R(21), R(22), ALU.subtract))
            od(TT(R(22), R(2), R(25), ALU.mult))
            od(TT(R(23), R(3), R(24), ALU.mult))
            od(TT(R(22), R(22), R(23), ALU.add))
            od(TS(tin[:, 2, :, 0], row[:, 21], 2.0, None, ALU.mult))
            od(TS(tin[:, 2, :, 1], row[:, 22], -2.0, None, ALU.mult))
            od(TT(R(23), R(9), R(17), ALU.mult))
            od(TT(R(24), R(9), R(16), ALU.mult))
            od(TT(R(25), R(21), R(23), ALU.mult))
            od(TT(R(11), R(22), R(24), ALU.mult))
            od(TT(R(25), R(25), R(11), ALU.subtract))
            od(TT(R(21), R(21), R(24), ALU.mult))
            od(TT(R(22), R(22), R(23), ALU.mult))
            od(TT(R(21), R(21), R(22), ALU.add))
            for r in range(2):
                od(TT(tin[:, 3, :, r], row[:, 10], row[:, 20], ALU.mult))
                od(TT(tin[:, 4, :, r], row[:, 10], row[:, 19], ALU.mult))
                od(TS(tin[:, 5, :, r], row[:, 25], 2.0, None, ALU.mult))
                od(TS(tin[:, 6, :, r], row[:, 21], 2.0, None, ALU.mult))
            v.nop().then_inc(s["tin_ready"], 1)
            v.wait_ge(s["wt_ps"], 2)
            TC(w1t[:, 0:3].rearrange("p a b -> p (a b)"), ps[:, 0, 0:384])
            TC(w1t[0:64, 3], ps[0:64, 0, 384:512]).then_inc(s["wt_out"], 1)
            TC(w2t.rearrange("p a b -> p (a b)"), ps[:, 1, 0:320]).then_inc(s["wt_out"], 1)
            v.wait_ge(s["rt_ps"], 2)
            od(TC(rt[:, 2].rearrange("p l h -> p (l h)"), ps[:, 3, 0:256]))
            for q in range(4):
                k = 3 + q
                src = ps[:, 2 + k // 2, 256 * (k % 2):256 * (k % 2) + 256].rearrange("p (l h) -> p l h", l=NL)
                for hf in range(2):
                    od(TC(la[64 * hf:64 * hf + 64, q], src[64 * hf:64 * hf + 64, :, 32 * hf:32 * hf + 32]))
            v.nop().then_inc(s["rt_out"], 1)
            def phases(i, c, order):
                v.wait_ge(s["turned_ready"], i * 4 + c + 1)
                w = ph_i[:, c * HCH * P:(c + 1) * HCH * P]
                order(TS(w, ph_f[:, c * HCH * P:(c + 1) * HCH * P], cst[:, C_PH:C_PH + 1], None, ALU.add))
                TS(w, w, (1 << MANT) - 1, ONE_BITS, ALU.bitwise_and, ALU.bitwise_or).then_inc(s["phase_ready"], 1)

            od(v.memset(coef, 0.0))
            for c in range(CHUNKS):
                phases(0, c, od)

            def step(i, last=False):
                ot = Order(v, s["f_order"], i * 16)

                def table_out(c):
                    if past(i):
                        v.wait_ge(v_stored[c], i * 16)
                    for g in (4 * c, 4 * c + 2):
                        v.wait_ge(s["v_ps"], i * 16 + g + 1)
                        h = 4 * (g % 8)
                        TC(vout[c // 2][:, h:h + 4, :].rearrange("p h t -> p (h t)"), ps[:, 5, :])\
                            .then_inc(s["v_out_dve"], 1)
                    v.wait_ge(chunk_used[c], i + 1)
                    if past(i) or c >= 2:
                        v.wait_ge(par["k_stored"][c % 2], i * 128 + 64 * (c // 2))
                    ot(TC(kst[:, c % 2].rearrange("p g t -> p (g t)"), ps[:, 7, :]))
                    first = kst[:, c % 2, :, 0]
                    TT(first, first, skip[:, bass.ds(i, 1), 4 * c:4 * c + 4].rearrange("p a g -> p (a g)"), ALU.add)\
                        .then_inc(s["k_out"], 1)

                if past(i):
                    v.wait_ge(chunk_used[CHUNKS - 1], i)
                TC(coef[:, 0:D], rt[:, 2, bass.ds(i, 1), :].rearrange("p a h -> p (a h)")).then_inc(s["coef_ready"], 1)
                v.wait_ge(s["x_in"], i * 32 + 32)
                if past(i):
                    v.wait_ge(s["gat_ps"], i)
                TS(oh, xb, cst[:, C_PC:C_PC + 1], None, ALU.is_equal).then_inc(s["oh_ready"], 1)
                def product(c):
                    hs = slice(c * HCH, (c + 1) * HCH)
                    v.wait_ge(s["exp_done"], i * 4 + c + 1)
                    v.wait_ge(s["sin_done"], i * 4 + c + 1)
                    TT(pe_t[:, hs, :], pe_t[:, hs, :], ph_t[:, hs, :], ALU.mult).then_inc(s["p_ready"], 1)

                product(0)
                product(1)
                for c in range(CHUNKS):
                    table_out(c)
                    if not last:
                        phases(i + 1, c, ot)
                    if c < 2:
                        product(c + 2)
                v.wait_ge(s["gat_ps"], i + 1)
                for j in range(2):
                    TC(amp[:, bass.ds(i * 8 + 4 * j, 4), :], ps[:, 3 + j, 0:272].rearrange("p (t c) -> p t c", t=4))\
                        .then_inc(s["amp_out"], 1)
                v.wait_ge(s["k_out"], i * 4 + 4)
                v.nop().then_inc(s["f_order"], 16 - ot.n)
            step(0)
            with v.Fori(1, NL - 1) as i:
                step(i)
            step(NL - 1, True)
            v.wait_ge(s["amp_out"], 2 * B)
            v.nop().then_inc(s["sig_in"], 1)
            lp = lambda j: amp[:, :, 64 + j]
            prf = prm[:, :, :, :].rearrange("p b t c -> p (b t) c")
            od(TS(post[:, 0, :, 0], lp(0), 0.05, None, ALU.mult))
            for b in range(B):
                od(TT(prf[:, 8 * b:8 * b + 8, 0], post[:, 0, 8 * b:8 * b + 8, 0], cst[:, C_BP:C_BP + NT], ALU.add))
            od(TS(post[:, 10, :, 0], lp(1), -1.0, None, ALU.mult))
            od(TT(post[:, 1, :, 0], post[:, 10, :, 0], lp(1), ALU.max))
            od(TT(post[:, 4], bc(post[:, 1, :, 0], SC), bcr(msc, 32), ALU.mult))
            od(TS(post[:, 4], post[:, 4], 1e-5, None, ALU.add))
            od(v.reciprocal(post[:, 5], post[:, 4]))
            od(TS(prf[:, :, 1:5], post[:, 5], 2.0 ** MANT, None, ALU.mult))
            od(TT(post[:, 6], post[:, 5], post[:, 5], ALU.mult))
            od(TS(prf[:, :, 9:13], post[:, 6], -0.5, None, ALU.mult))
            od(TS(post[:, 7, :, 0], lp(3), 0.5, 0.75, ALU.mult, ALU.add))
            od(TS(post[:, 8, :, 0], post[:, 7, :, 0], ROUND, ROUND, ALU.add, ALU.subtract))
            od(TT(post[:, 7, :, 0], post[:, 7, :, 0], post[:, 8, :, 0], ALU.subtract))
            od(TS(post[:, 7, :, 0], post[:, 7, :, 0], 2.0 ** MANT, None, ALU.mult))
            od(TC(prf[:, :, 5:9], bc(post[:, 7, :, 0], SC)))
            od(TT(swc, swc, swc, ALU.mult))
            v.wait_ge(s["sig_out"], 2)
            od(TT(post[:, 9, :, 0], post[:, 2, :, 0], post[:, 3, :, 0], ALU.mult))
            od(TT(prf[:, :, 13:17], bc(post[:, 9, :, 0], SC), bcr(swc, 32), ALU.mult))
            for c in range(CHUNKS):
                v.wait_ge(p_stored[c], 16 * NL)
                v.wait_ge(v_stored[c], 16 * NL)
            for j in range(2):
                v.wait_ge(par["k_stored"][j], 64 * 2 * NL)
            v.wait_ge(s["zk_stored"], 16 * NL)
            v.wait_ge(s["pos_in"], 16)
            for it in range(2):
                om = Order(v, s["m_order"], it * 64)

                def front(g):
                    p, bp, st, k = g % 2, g // 4, 2 * (g % 4), g // 2
                    if g % 4 == 0:
                        v.wait_ge(par["e_done"][1], it * 4)
                        v.wait_ge(par["aw_ready"][1], it * 4)
                        TC(prb[:, bp], prm[:, bass.ds(it * 2 + bp, 1)].rearrange("p a t c -> p (a t) c"))\
                            .then_inc(s["prb_ready"], 1)
                        v.wait_ge(s["prb_ready"], it * 2 + bp + 1)
                    v.wait_ge(par["mul_dve"][p], it * 4 + k)
                    v.wait_ge(par["ph_ready"][p], it * 4 + k)
                    for j in range(2):
                        ins = TS(xd[:, p, j], pos[:, bass.ds(it * 2 + bp, 1), :].rearrange("p a l -> p (a l)"),
                                 prb[:, bp, st + j, 0:1], None, ALU.subtract)
                    om(ins)
                    v.wait_ge(par["e_done"][p], it * 4 + k)
                    TT(xq[:, p], xd[:, p], xd[:, p], ALU.mult).then_inc(par["xq_ready"][p], 1)
                    v.wait_ge(par["mul_pool"][p], it * 4 + k)
                    for j in range(2):
                        for sc in range(SC):
                            w = (4 * j + sc) * L
                            ins = TS(qi[p][:, w:w + L], xd[:, p, j], prb[:, bp, st + j, 1 + sc:2 + sc],
                                     prb[:, bp, st + j, 5 + sc:6 + sc], ALU.mult, ALU.add)
                    om(ins)
                    TS(qi[p], qi[p], (1 << MANT) - 1, ONE_BITS, ALU.bitwise_and, ALU.bitwise_or)\
                        .then_inc(par["ph_ready"][p], 1)

                def product(g):
                    p, k = g % 2, g // 2
                    v.wait_ge(par["e_done"][p], it * 4 + k + 1)
                    v.wait_ge(par["s_done"][p], it * 4 + k + 1)
                    TT(eb[p][:, 0], eb[p][:, 0], qb[p][:, 0], ALU.mult).then_inc(par["mul_dve"][p], 1)

                def field_out(bp):
                    v.wait_ge(s["htr_ps"], it * 2 + bp + 1)
                    for hf in range(2):
                        dst = ht[:, 4 * hf:4 * hf + 4, bass.ds(it * 2 + bp, 1), :].rearrange("p i a d -> p i (a d)")
                        src = ps[:, 2, :].rearrange("p (c f d) -> p c f d", c=4, f=2)[:, :, hf]
                        ins = TC(dst, src)
                    ins.then_inc(s["ht_out"], 1)

                front(0)
                for g in range(1, 8):
                    front(g)
                    product(g - 1)
                    if g == 6:
                        field_out(0)
                product(7)
                field_out(1)
                assert om.n == 16
                v.nop().then_inc(s["m_order"], 48)
            v.wait_ge(s["ht_out"], B)

            neg_mean, ve = lnw[:, 0], lnw[:, 2]

            def centre(x, xc_, sq_):
                od(v.reduce_sum(lnw[:, 0], x, axis=AX.X))
                od(TS(lnw[:, 0], lnw[:, 0], -1.0 / D, None, ALU.mult))
                od(TT(xc_, x, bc(lnw[:, 0], D), ALU.add))
                od(TT(sq_, xc_, xc_, ALU.mult))
                od(v.reduce_sum(lnw[:, 1], sq_, axis=AX.X))

            def rstd(k):
                TS(lnw[:, 2], lnw[:, 1], 1.0 / D, EPS, ALU.mult, ALU.add).then_inc(s["ln_var"], 1)
                v.wait_ge(s["ln_sd"], k)
                od(v.reciprocal(lnw[:, 4], lnw[:, 3]))

            flat = lambda t: t.rearrange("p i b d -> p (i b) d")
            htf = flat(ht[:, :, :, :])
            centre(htf, xc, sq)
            rstd(1)
            od(TT(lnw[:, 5], lnw[:, 4], lnw[:, 4], ALU.mult))
            od(TT(lnw[:, 1], lnw[:, 1], lnw[:, 5], ALU.mult))
            od(TC(lnw[:, 5], lnw[:, 4]))
            rstd(2)
            od(TT(lnw[:, 4], lnw[:, 4], lnw[:, 5], ALU.mult))
            od(TT(xc, xc, bc(lnw[:, 4], D), ALU.mult))
            v.wait_ge(s["a_in"], 16 * 13)
            od(TT(xc, xc, bcr(gbc[:, 0], 32), ALU.mult))
            TT(flat(mn), xc, bcr(gbc[:, 1], 32), ALU.add).then_inc(s["ln_out"], 1)
            for j in range(2):
                v.wait_ge(s["mnt_ps"], 1 + j)
                TC(mnt[:, 0, 512 * j:512 * j + 512], ps[:, j, :]).then_inc(s["mnt_out"], 1)
            v.wait_ge(s["g_ps"], 1)
            TC(gr.rearrange("p a b -> p (a b)"), ps[:, 4, :]).then_inc(s["g_out"], 1)
            v.wait_ge(s["u_ps"], 1)
            for k in range(4):
                od(TT(rr[:, 2 * k:2 * k + 2], ps[:, k, :].rearrange("p (a c) -> p a c", a=2),
                      bcr(wqkvg[:, 0], 2), ALU.mult))
            v.reduce_sum(r2.rearrange("p a h -> p (a h)"), rr.rearrange("p a (h c) -> p (a h) c", c=CH), axis=AX.X)\
                .then_inc(s["r_ready"], 1)
            v.wait_ge(s["lsum_ps"], 1)
            sc_att = 1.0 / (CH ** 0.5) / (L ** 0.5)
            lgt = rr.rearrange("p a c -> p (a c)")[:, 0:128]
            od(TS(lgt, ps[:, 4, 0:128], sc_att, None, ALU.mult))
            by_t = lambda x: x.rearrange("p (s t k) -> p s k t", s=2, t=4)
            mx = rr.rearrange("p a c -> p (a c)")[:, 128:160]
            od(v.reduce_max(mx.rearrange("p (s k) -> p s k", s=2), by_t(lgt), axis=AX.X))
            amf = amx.rearrange("p a b -> p (a b)")
            for s2 in range(2):
                ins = TT(amf[:, 64 * s2:64 * s2 + 64].rearrange("p (t k) -> p t k", t=4),
                         lgt[:, 64 * s2:64 * s2 + 64].rearrange("p (t k) -> p t k", t=4),
                         bcr(mx[:, 16 * s2:16 * s2 + 16], 4), ALU.subtract)
            ins.then_inc(s["amax_ready"], 1)
            v.wait_ge(s["att_exp"], 1)
            atf = att.rearrange("p a b c d e -> p (a b c d e)")
            od(v.reduce_sum(mx.rearrange("p (s k) -> p s k", s=2), by_t(atf), axis=AX.X))
            od(v.reciprocal(mx, mx))
            for s2 in range(2):
                w = atf[:, 64 * s2:64 * s2 + 64].rearrange("p (t k) -> p t k", t=4)
                od(TT(w, w, bcr(mx[:, 16 * s2:16 * s2 + 16], 4), ALU.mult))
            for t2 in range(2):
                rows = slice(64 * t2, 64 * t2 + 64)
                for sp_ in range(2):
                    for s2 in range(2):
                        for tp in range(2):
                            ins = TT(wvs[rows, sp_, s2, tp].rearrange("p (h c) -> p h c", h=NH),
                                     wqkvg[rows, 2].rearrange("p (h c) -> p h c", h=NH),
                                     bc(att[rows, s2, t2, tp, sp_], CH), ALU.mult)
            ins.then_inc(s["wvs_ready"], 1)
            for u in range(16):
                g, b, j = u % 2, u // 4, (u // 2) % 2
                w = gt[:, g, b, 512 * j:512 * j + 512]
                v.wait_ge(s["gate_out"], u + 1)
                v.wait_ge(s["pv_ps"], u + 1)
                TT(w, ps[:, 6 + u % 2, :], w, ALU.mult).then_inc(s["og_ready"], 1)
            for k in range(4):
                v.wait_ge(s["o_ps"], k + 1)
                w = htf[:, 8 * k:8 * k + 8]
                od(TT(w, w, bcr(gbc[:, 2], 8), ALU.add))
                TT(w, w, ps[:, k, :].rearrange("p (t d) -> p t d", t=8), ALU.add).then_inc(s["ht_att"], 1)
            v.wait_ge(s["ht_att"], 4)
            v.wait_ge(s["e_in"], 16 * 9)
            for g in range(4):
                ins = TC(w1x[64:96, g].rearrange("p (e h) -> p e h", e=8),
                         bc(cst[64:96, C_BIG + 8 * g:C_BIG + 8 * g + 8], H0))
            ins.then_inc(s["mask_ready"], 1)
            v.wait_ge(s["rw_ps"], 1)
            TC(rwt, ps[0:64, 7, 0:E0]).then_inc(s["rw_out"], 1)
            centre(htf, xc, sq)
            rstd(3)
            TT(xn, xc, bc(lnw[:, 4], D), ALU.mult).then_inc(s["ln_out"], 1)
            for k in range(4):
                v.wait_ge(s["x_ps"], 2 * k + 1)
                TC(x96[0:64, 8 * k:8 * k + 4, :].rearrange("p t q -> p (t q)"), ps[0:64, 0, :])\
                    .then_inc(s["rw_out"], 1)
            v.wait_ge(s["lg_ps"], 1)
            for k in range(2):
                od(TT(lg[:, 16 * k:16 * k + 16], ps[:, 2 + k, :].rearrange("p (t e) -> p t e", t=16),
                      bcr(rbb, 16), ALU.add))
            od(v.reduce_max(lnw[:, 0], lg, axis=AX.X))
            od(TT(o1, lg, bc(lnw[:, 0], E0), ALU.is_equal))
            od(TT(o1, o1, bcr(cst[:, C_DESC:C_DESC + E0], 32), ALU.mult))
            od(v.reduce_max(lnw[:, 1], o1, axis=AX.X))
            TT(o2, o1, bc(lnw[:, 1], E0), ALU.is_equal).then_inc(s["oh0_ready"], 1)
            for k in range(8):
                v.wait_ge(s["oht_ps"], k + 1)
                TC(oht[:, 4 * k:4 * k + 4].rearrange("p t q -> p (t q)"), ps[0:32, k % 2, :])\
                    .then_inc(s["oht_out"], 1)
                TS(x96[64:96, 4 * k:4 * k + 4].rearrange("p t q -> p (t q)"), ps[0:32, k % 2, :], -1.0, None,
                   ALU.add).then_inc(s["oht_out"], 1)
            for k in range(4):
                for u in range(8 * k + 1, 8 * k + 8, 2):
                    j, g = (u // 4) % 2, u % 4
                    v.wait_ge(s["hx_ps"], u + 1)
                    if k:
                        v.wait_ge(s["f0_ps"], k)
                    TS(hm[:, j, g], ps[:, 2 + u % 4, :], b1x[:, g:g + 1], 0.0, ALU.add, ALU.max)\
                        .then_inc(s["hm_used"], 1)
                v.wait_ge(s["f0t_ps"], k + 1)
                w = ht[:, 2 * k:2 * k + 2].rearrange("p i b d -> p b i d")
                for b in range(B):
                    ins = TT(ht[:, 2 * k:2 * k + 2, b, :], ht[:, 2 * k:2 * k + 2, b, :],
                             ps[:, 7, P * b:P * b + P].rearrange("p (i d) -> p i d", i=2), ALU.add)
                ins.then_inc(s["ht_ffn"], 1)
            v.wait_ge(s["lt_ps"], 1)
            TC(wo4[0:64, :, :].rearrange("p l o -> p (l o)"), ps[0:64, 0, :]).then_inc(s["lt_out"], 1)
            v.memset(yt[64:65].rearrange("p i b t -> p (i b t)"), 1.0).then_inc(s["lt_out"], 1)
            v.wait_ge(s["ht_ffn"], 4)
            v.wait_ge(s["s_in"], 80)
            usf = us
            centre(htf, xc4, sq4)
            rstd(4)
            TT(uu, xc4, bc(lnw[:, 4], D), ALU.mult).then_inc(s["ln_out"], 1)
            for k in range(4):
                v.wait_ge(s["turn_ps"], k + 1)
                od(TC(usf[:, 8 * k:8 * k + 8, :].rearrange("p t d -> p (t d)"), ps[:, 4 + k, :]))
            od(v.memset(sbt, 0.0))
            def step(l):
                global_od = Order(v, s["s_order"], l * 128)
                O = global_od
                O(v.reduce_sum(lnw[:, 0], usf, axis=AX.X))
                O(TS(lnw[:, 0], lnw[:, 0], -1.0 / D, None, ALU.mult))
                O(TT(xc4, usf, bc(lnw[:, 0], D), ALU.add))
                O(TT(sq4, xc4, xc4, ALU.mult))
                O(v.reduce_sum(lnw[:, 1], sq4, axis=AX.X))
                TS(lnw[:, 2], lnw[:, 1], 1.0 / D, EPS, ALU.mult, ALU.add).then_inc(s["ln_var"], 1)
                v.wait_ge(s["ln_sd"], l + 5)
                O(v.reciprocal(lnw[:, 4], lnw[:, 3]))
                O(TT(xc4, xc4, bc(lnw[:, 4], D), ALU.mult))
                O(TC(w4l[:, :], wo4[:, bass.ds(l, 1), :].rearrange("p a o -> p (a o)")))
                O(TT(xc4, xc4, lsb[:, bass.ds(l, 1), 0, :].broadcast_to([P, 32, D]), ALU.mult))
                TT(uu, xc4, lsb[:, bass.ds(l, 1), 1, :].broadcast_to([P, 32, D]), ALU.add).then_inc(s["ln_out"], 1)
                for q in range(4):
                    ins = TC(lax[:, q].rearrange("p (h b) -> p h b", b=B),
                             bc(la[:, q, bass.ds(l, 1), :].rearrange("p a h -> p (a h)"), B))
                O(ins)
                for k in range(4):
                    v.wait_ge(s["xm_ps"], l * 4 + k + 1)
                    hp, hh = k // 2, 16 * (k % 2)
                    for ri in range(2):
                        src = ps[64 * ri:64 * ri + 64, k, :].rearrange("p (h c) -> p h c", h=16)[:, :, 0:28]
                        ins = TC(xa[64 * hp:64 * hp + 64, ri, :, hh:hh + 16, :],
                                 src.rearrange("p h (i b) -> p i h b", i=7))
                    O(ins)
                for i in range(1, 7):
                    last = xa[:, :, i - 1].rearrange("p r h b -> p r (h b)")
                    xi = xa[:, :, i].rearrange("p r h b -> p r (h b)")
                    TT(m4[:, 0:2, 0:128], last, bcr(lax[:, 0], 2), ALU.mult)
                    O(TT(m4[:, 2:4, 0:128], last, bcr(lax[:, 1], 2), ALU.mult))
                    O(TT(xi, xi, m4[:, 0:2, 0:128], ALU.add))
                    TT(xi[:, 0], xi[:, 0], m4[:, 3, 0:128], ALU.subtract)
                    O(TT(xi[:, 1], xi[:, 1], m4[:, 2, 0:128], ALU.add))
                for ri in range(2):
                    for gi in range(2):
                        ins = TT(m4[:, 2 * ri + gi].rearrange("p (i k) -> p i k", i=7),
                                 xa[:, ri].rearrange("p i h b -> p i (h b)"), bcr(lax[:, 2 + gi], 7), ALU.mult)
                O(ins)
                for hp in range(2):
                    rows = slice(64 * hp, 64 * hp + 64)
                    re, im = sbt[0:64, 32 * hp:32 * hp + 32, 4:32], sbt[64:128, 32 * hp:32 * hp + 32, 4:32]
                    m = lambda k: m4[rows, k].rearrange("p (i h b) -> p h i b", i=7, b=B)
                    shp = lambda w: w.rearrange("p h (i b) -> p h i b", i=7)
                    TT(shp(re), m(0), m(3), ALU.subtract)
                    O(TT(m(1), m(1), m(2), ALU.add))
                    O(TS(shp(im), m(1), -1.0, None, ALU.mult))
                v.nop().then_inc(s["st_ready"], 1)
                for g in range(8):
                    v.wait_ge(s["sig_done"], l * 8 + g + 1)
                    w = slice(4 * g, 4 * g + 4)
                    O(TT(gl[:, w], ps[:, g, :].rearrange("p (t d) -> p t d", t=4)[:, :, 0:D], sg[:, w], ALU.mult))
                TT(usf, usf, gl, ALU.add).then_inc(s["us_out"], 1)
                v.wait_ge(s["us_out"], l + 1)
                v.nop().then_inc(s["s_order"], 128 - O.n)
            step(0)
            with v.Fori(1, NL) as l:
                step(l)
            for k in range(4):
                v.wait_ge(s["turn_ps"], 5 + k)
                w = htf[:, 8 * k:8 * k + 8]
                od(TT(w, w, ps[:, k, :].rearrange("p (t d) -> p t d", t=8), ALU.add))
            centre(htf, xc4, sq4)
            rstd(9)
            TT(xn1, xc4, bc(lnw[:, 4], D), ALU.mult).then_inc(s["ln_out"], 1)
            v.wait_ge(s["m_in"], 16 * 7)
            TC(sel.rearrange("p e q -> p (e q)").rearrange("p (e q) -> p e q", e=E1), bc(selr, P))
            TT(wg32[64:65, 0:E1], bgx[64:65, 0], bgx[64:65, 1], ALU.add).then_inc(s["mask_ready"], 1)
            v.memset(x65[64:65].rearrange("p t q -> p (t q)"), 1.0).then_inc(s["mask_ready"], 1)
            for k in range(4):
                v.wait_ge(s["x65_ps"], 2 * k + 1)
                TC(x65[0:64, 8 * k:8 * k + 4, :].rearrange("p t q -> p (t q)"), ps[0:64, 0, :])\
                    .then_inc(s["rw_out"], 1)
            v.wait_ge(s["gl_ps"], 1)
            TC(lgt1[:, 0], ps[:, 2, :]).then_inc(s["lgt_out"], 1)
            v.wait_ge(s["lgr_ps"], 1)
            desc = bcr(cst[:, C_DESC + E0 - E1:C_DESC + E0], 32)

            def first_max(dst, src, mxc):
                od(v.reduce_max(mxc, src, axis=AX.X))
                od(TT(cm3, src, bc(mxc, E1), ALU.is_equal))
                od(TT(cm3, cm3, desc, ALU.mult))
                od(v.reduce_max(lnw[:, 3], cm3, axis=AX.X))
                od(TT(dst, cm3, bc(lnw[:, 3], E1), ALU.is_equal))

            for r in range(2):
                ins = TC(cm2[:, 16 * r:16 * r + 16].rearrange("p (c b) e -> p b c e", b=B),
                         ps[:, 4 + r, :].rearrange("p (b c e) -> p b c e", b=B, c=4)[:, :, :, 0:E1])
            od(ins)
            first_max(cmb, cm2, lnw[:, 0])
            od(TS(f1[:, :, 0:E1], cmb, -3.0e38, None, ALU.mult))
            od(TT(cm2, cm2, f1[:, :, 0:E1], ALU.add))
            first_max(f1[:, :, 8:16], cm2, lnw[:, 1])
            TT(lnw[:, 4], lnw[:, 1], lnw[:, 0], ALU.subtract).then_inc(s["gexp_in"], 1)
            v.wait_ge(s["gexp_out"], 1)
            od(TS(lnw[:, 0], lnw[:, 5], 1.0, None, ALU.add))
            od(v.reciprocal(lnw[:, 1], lnw[:, 0]))
            od(TT(lnw[:, 2], lnw[:, 5], lnw[:, 1], ALU.mult))
            od(TT(cmb, cmb, bc(lnw[:, 1], E1), ALU.mult))
            od(TT(f1[:, :, 8:16], f1[:, :, 8:16], bc(lnw[:, 2], E1), ALU.mult))
            od(TT(cmb, cmb, f1[:, :, 8:16], ALU.add))
            high = -65536
            cmi = cut(27168, 32 * E1, dt=I32).rearrange("p (t e) -> p t e", t=32)
            od(TS(cm24i[:, :, 0], cmi, high, None, ALU.bitwise_and))
            od(TT(cm2, cmb, cm24[:, :, 0], ALU.subtract))
            cm2i = cut(27424, 32 * E1, dt=I32).rearrange("p (t e) -> p t e", t=32)
            od(TS(cm24i[:, :, 1], cm2i, high, None, ALU.bitwise_and))
            TT(cm24[:, :, 2], cm2, cm24[:, :, 1], ALU.subtract).then_inc(s["parts_ready"], 1)
            for c in range(1, 8, 2):
                v.wait_ge(s["ct_ps"], c + 1)
                TC(cmtp[:, 512 * c:512 * c + 512], ps[0:24, 4, :]).then_inc(s["ct_out_d"], 1)
            v.wait_ge(s["cmt_ps"], 1)
            TC(cmt.rearrange("p a b -> p (a b)"), ps[:, 7, 0:256]).then_inc(s["cmt_out"], 1)
            v.wait_ge(s["b2_ps"], 1)
            for k in range(4):
                w = htf[:, 8 * k:8 * k + 8]
                ins = TT(w, w, ps[:, [5, 6, 7, 4][k], :].rearrange("p (t d) -> p t d", t=8), ALU.add)
            ins.then_inc(s["cmt_out"], 1)
            v.wait_ge(s["cmt_out"], 2)
            for n in range(72):
                if n < 64:
                    v.wait_ge(s["hid_out"], n + 1)
                    v.wait_ge(s["bc_ps"], n + 1)
                    w = h8[:, n % 8, :]
                    TT(w, w, ps[:, 3 + n % 2, :], ALU.mult).then_inc(s["hw_out"], 1)
                if n % 16 == 7 and n > 16:
                    k = n // 16 - 1
                    v.wait_ge(s["ft_ps"], k + 1)
                    w = ht[:, 2 * k:2 * k + 2].rearrange("p i b d -> p b i d")
                    TT(w, w, ps[:, 7, :].rearrange("p (b i d) -> p b i d", b=B, i=2), ALU.add)\
                        .then_inc(s["out_ready"], 1)


def kernel(**inputs):
    import numpy as np
    from concourse import bacc
    from concourse.bass_utils import run_bass_kernel_spmd

    nc = bacc.Bacc("TRN2", target_bir_lowering=False, num_devices=1)
    c = np.zeros((P, C_SEL + E1), np.float32)
    c[:, C_ID:C_ID + P] = np.eye(P)
    c[:, C_T:C_T + P] = np.arange(P)
    c[:, C_BP:C_BP + NT] = (np.arange(L, dtype=np.float32) / np.float32(L - 1)).reshape(NT, P).T
    c[:, C_PC] = np.arange(P) % 64
    c[:, C_DESC:C_DESC + E0] = E0 - np.arange(E0)
    c[:, C_PH] = np.where(np.arange(P) < 64, 0.75, 0.5) * 2.0 ** MANT
    c[:64, C_LO:C_LO + P] = 1.0
    c[64:, C_HI:C_HI + P] = 1.0
    c[64:96, C_BIG:C_BIG + E0] = np.eye(E0) * BIG
    c[:, C_J:C_J + P] = np.eye(P)[::-1]
    c[:, C_SEL:C_SEL + E1] = np.tile(np.eye(E1), (P // E1, 1))
    c[:, C_N3PI] = -9.424777
    arrays = {n: np.ascontiguousarray(x) for n, x in inputs.items()}
    arrays["shape_constants"] = c
    aps = {n: nc.dram_tensor("in_" + n, x.shape, mybir.dt.from_np(x.dtype), kind="ExternalInput").ap()
           for n, x in arrays.items()}
    aps["out"] = nc.dram_tensor("out_0", (B, L, D), F32, kind="ExternalOutput").ap()
    tower_kernel(nc, aps)
    r = run_bass_kernel_spmd(nc, [{"in_" + n: x for n, x in arrays.items()}], core_ids=[0])
    return r.results[0]["out_0"]
```

```python
from contextlib import ExitStack

import concourse.bass as bass
from concourse import mybir

F32 = mybir.dt.float32
I32 = mybir.dt.int32
BF16 = mybir.dt.bfloat16
ALU = mybir.AluOpType
ACT = mybir.ActivationFunctionType
AX = mybir.AxisListType

P = 128
B, L, D = 4, 1024, 64
NT = L // P
SC = 4
NH, CH = 8, 32
HC = NH * CH
E0, H0 = 32, 16
NL, N = 4, 64
E1, H1 = 8, 128
EPS = 1e-5
MANT = 23
ONE_BITS = 0x3F800000
ROUND = 1.5 * 2.0 ** 23
BIG = 2.0 ** 100
CHUNKS = 4
HCH = D // CHUNKS
FIELD_GROUPS = B * NT // 2
POOL_UNITS = 3

C_ID, C_T, C_BP, C_PC, C_DESC, C_PH, C_LO, C_HI, C_BIG, C_N3PI = 0, 128, 256, 264, 265, 297, 298, 426, 554, 586
C_ALL = 588
C_J = C_ALL
C_SEL = C_J + P


def tower_kernel(nc, a):
    ctx = ExitStack()
    with ctx:
        def sb(name, shape, dt=F32):
            return ctx.enter_context(nc.sbuf_tensor(name, shape, dt))

        def sem(name):
            return ctx.enter_context(nc.semaphore(name))

        def dram(ap, offset, pattern):
            return bass.AP(tensor=ap.tensor, offset=ap.offset + offset, ap=pattern)

        p_dram = nc.dram_tensor("mode_tables", [NL, P, D * P], F32, kind="Internal").ap()
        v_dram = nc.dram_tensor("mode_tables_t", [NL, P, D * P], F32, kind="Internal").ap()
        k_dram = nc.dram_tensor("taps", [NL, D, 2 * P], F32, kind="Internal").ap()

        ctx_dram = nc.dram_tensor("context_row", [B * L], F32, kind="Internal").ap()

        big = sb("big", [P, 4 * 8192])
        cst = sb("cst", [P, C_ALL])
        ht = sb("ht", [P, NT, B, D])
        amp = sb("amp", [P, B * NT, 68])
        pos = sb("pos", [P, B, L])
        xd = sb("xd", [P, 2, 2, L])
        xq = sb("xq", [P, 2, 2, L])
        ampw = sb("ampw", [P, 2, 2, SC, D])
        prm = sb("prm", [P, B, NT, 17])
        prb = sb("prb", [P, 2, NT, 17])
        ctxp = sb("ctxp", [P, B * NT])
        la = sb("la", [P, 4, NL, 32])
        lnw = sb("lnw", [P, 6, 32])

        def cut(off, *shape, parts=P, dt=F32):
            n = 1
            for s in shape:
                n *= s
            v = big[0:parts, off:off + n]
            if dt is not F32:
                v = v.bitcast(dt)
            if len(shape) == 1:
                return v
            names = "abcde"[:len(shape)]
            return v.rearrange(f"p ({' '.join(names)}) -> p {' '.join(names)}",
                               **{k: s for k, s in zip(names[1:], shape[1:])})

        ident = cst[:, C_ID:C_ID + P]
        trow = cst[:, C_T:C_T + P]
        n3pi = cst[:, C_N3PI:C_N3PI + 1]

        pe_t = cut(0, D, P)
        ph_t = cut(8192, D, P)
        ph_f = cut(8192, D * P)
        ph_i = cut(8192, D * P, dt=I32)
        o = 16384
        xb = cut(o, 1032, dt=I32); o += 1032
        oh = cut(o, 1032); o += 1032
        h1 = cut(o, 1028); o += 1028
        h2 = cut(o, 1026, parts=64); o += 1026
        w1r = cut(o, 448); o += 448
        w2r = cut(o, 640, parts=64); o += 640
        w1t = cut(o, 4, P); o += 512
        w2t = cut(o, 5, D); o += 320
        w3t = cut(o, 3, parts=64); o += 4
        el = cut(o, 68, parts=64); o += 68
        b1c = cut(o, 1); o += 1
        b2c = cut(o, 1); o += 1
        b3c = cut(o, 1); o += 1
        msc = cut(o, SC); o += SC
        swc = cut(o, SC); o += SC
        ldt = cut(o, 2); o += 2
        dtc = cut(o, 2); o += 2
        row = cut(o, 26, 2, N); o += 26 * 2 * N
        tin = cut(o, 7, 2, 2, N); o += 7 * 4 * N
        rt = cut(o, 3, NL, D); o += 3 * NL * D
        coef = cut(o, D + 32); o += D + 32
        post = cut(o, 16, B * NT, SC); o += 16 * 32 * SC
        zk = cut(o, P, parts=64); o += P
        skip = cut(o, NL, 16); o += NL * 16
        assert o <= 32768, o

        vout = [w[:, :, :, :].rearrange("p a b c -> p (a b c)").rearrange("p (h t) -> p h t", t=P) for w in (xd, xq)]
        kst = ampw[:, :, :, :, :].rearrange("p a b s d -> p (a b s d)").rearrange("p (k g t) -> p k g t", k=2, t=P)

        eb = [cut(0, 2, SC, L), cut(8192, 2, SC, L)]
        qb = [cut(16384, 2, SC, L), cut(24576, 2, SC, L)]
        qi = [cut(16384, 8 * L, dt=I32), cut(24576, 8 * L, dt=I32)]
        accs = sb("accs", [P, 512])

        crow = accs

        mn = cut(0, NT, B, D)
        mnt = cut(2048, 2, L)
        xc = cut(4096, 32, D)
        sq = cut(6144, 32, D)
        gr = cut(8192, 2, HC)
        wqkvg = cut(8704, 4, HC)
        rr = cut(9728, 8, HC)
        r2 = cut(11776, 8, NH)
        att = cut(11840, 2, 2, 2, 2, NH)
        amx = cut(11968, 4, 32)
        wvs = cut(12288, 2, 2, 2, HC)
        gt = cut(16384, 2, B, L)
        wo = cut(24576, 2, D)
        bgc = cut(24704, 2)
        gbc = cut(24706, 2, D)
        boc = cut(24834, 1)
        ob = cut(14336, 2, 512)

        xn = cut(0, 32, D)
        x96 = cut(8192, 32, P)
        oht = cut(12288, 32, P, parts=32)
        hr = cut(16384, 8, 512)
        f0 = cut(20480, 512)
        lg = cut(21000, 32, E0)
        o1 = cut(22024, 32, E0)
        o2 = cut(23048, 32, E0)
        lgt0 = cut(22024, 2, 512)
        rwr = cut(26000, D, parts=32)
        rwt = cut(24960, E0, parts=64)
        rbb = cut(24992, E0)
        w1x = cut(25024, 4, P, parts=96)
        b1x = cut(25536, 4)
        w2x = cut(25540, 4, D)
        b2x = cut(25796, D, parts=32)

        vt = cut(0, D, P)
        pt = cut(8192, D, P)
        t0 = cut(16384, D, P)
        w4 = 24576
        uu = cut(w4, 32, D)
        us = amp[:, :, :].rearrange("p t c -> p (t c)")[:, 0:2048].rearrange("p (t d) -> p t d", d=D)
        xa = cut(w4 + 2048, 2, 7, 32, B)
        m4 = cut(w4 + 2048 + 1792, 4, 7 * 32 * B)
        x4 = cut(w4 + 2048 + 1792, 16, P)
        row_of = lambda t, k: t[:, :, :].rearrange("p a b -> p (a b)")[:, 2048 * k:2048 * k + 2048]
        flat4 = lambda t: t[:, :, :, :].rearrange("p a b c -> p (a b c)")
        sbt = row_of(pos, 0).rearrange("p (h c) -> p h c", h=D)
        yg = row_of(pos, 1).rearrange("p (g t) -> p g t", g=16)
        yy = flat4(xd)[:, 0:2048].rearrange("p (c h) -> p c h", h=D)
        yt = flat4(xd)[:, 2048:4096]
        sg = flat4(xq)[:, 0:2048].rearrange("p (u k) -> p u k", u=4)
        gl = flat4(xq)[:, 2048:4096].rearrange("p (u k) -> p u k", u=4)
        xc4 = flat4(xq)[:, 0:2048].rearrange("p (t d) -> p t d", d=D)
        sq4 = flat4(xq)[:, 2048:4096].rearrange("p (t d) -> p t d", d=D)

        def unit(t, u):
            jp, c2 = u // 2, u % 2
            return t[:, 16 * jp:16 * jp + 16].rearrange("p (x c) d -> p x c d", c=2)[:, :, c2, :]

        def by_chunk(m):
            return m.rearrange("p (h i b) -> p i h b", i=7, b=B)

        def every_chunk(f):
            return f.rearrange("p (a h b) -> p a h b", a=1, b=B).broadcast_to([P, 7, 32, B])

        late = ampw[:, :, :, :, :].rearrange("p a b s d -> p (a b s d)")
        wo4 = late[:, 512:1024].rearrange("p (l o) -> p l o", l=NL)
        prmf = prm[:, :, :, :].rearrange("p b t c -> p (b t c)")
        wor = prmf[:, 0:512].rearrange("p (l r d) -> p l r d", l=NL, r=2)
        bo = prmf[:, 512:520].rearrange("p (l z) -> p l z", l=NL)
        bcur = prmf[:, 520:522]
        lsb = late[:, 0:512].rearrange("p (l k d) -> p l k d", l=NL, k=2)
        w4l = sb("w4l", [P, P])
        lax = cut(32000, 4, 128)

        cm24 = cut(0, 32, 3, E1)
        cm24i = cut(0, 32 * 24, dt=I32).rearrange("p (t q e) -> p t q e", t=32, q=3)
        wg32 = cut(1024, 32, parts=65)
        selr = cut(1056, E1, parts=24)
        fx = cut(2048, 2, 512)
        lgt1 = cut(14848, 2, 512)
        sel = cut(14336, E1 * P // 2, parts=24, dt=BF16).rearrange("p (e q) -> p e q", e=E1)
        cmtp = cut(12288, L * B // 2, parts=24, dt=BF16)
        x65 = cut(8192, 32, P, parts=65)
        h8 = cut(16384, 8, 512)
        w1e = cut(24576, E1, P, parts=64)
        w2e = cut(25600, E1, D)
        b1e = cut(26112, E1)
        bgx = cut(26128, 2, E1, parts=65)
        b2d = cut(26144, 16, D)
        cmb = cut(27168, 32, E1)
        cm2 = cut(27424, 32, E1)
        cm3 = cut(27680, 32, E1)
        cmt = cut(27936, 2, P)
        xn1 = cut(28192, 32, D)
        f1 = cut(30240, 32, D)

        bias_now = cut(32640, D)
        turn = cut(32512, P)

        ps = ctx.enter_context(nc.psum_tensor("ps", [P, 8, 512], F32))

        names = (
            "const_in w_in row_in x_in pos_in s_in vt_in pt_in t0_in "
            "tin_ready wt_ps wt_out rt_ps rt_out row_act row_dve "
            "oh_ready gat_ps amp_out c1_ps h1_ready c2_ps h2_ready c3_ps ctx_row ctx_stored ctx_in "
            "turned_ready phase_ready sin_done arg_ready exp_done p_ready v_ps v_out_dve v_out_act coef_ready "
            "chunk_used k_out zk_ready zk_stored "
            "d_order f_order m_order s_order wait_taken "
            "prb_ready acc_ps acc_out htr_ps ht_out "
            "cen_ready sq_out ln_var ln_sd ln_out small_in small_out "
            "att_ps att_dve mnt_out gate_ps gate_out pv_ps og_ready o_ps o_out ot_ps ht_att "
            "x_ps x_out rw_out lg_ps lgt_out oh0_ready oht_ps oht_out mask_ready hx_ps hm_ready hm_used f0_ps "
            "f0_out f0t_ps ht_ffn "
            "turn_ps lt_ps lt_out xm_ps st_ready y_ps yg_ready z_ps sig_done us_out xc_ps x4_out xa_out "
            "rec_ready pm_ready t1_ps yy_out t2_ps yt_out_a yt_out_d gl_ready gt_ps nrm_part mean_ready cen_pool "
            "nrm_ready uu_ready "
            "gates_ps cmt_out hh_ps hid_out bc_ps hw_out w2_ps fx_out ft_ps parts_ready ct_ps ct_out_a ct_out_d "
            "out_ready stored "
        ).split()
        s = {n: sem(n) for n in names}
        par = {n: [sem(f"{n}_{j}") for j in range(2)] for n in
               ("xd_ready", "xq_ready", "ph_ready", "e_done", "s_done", "mul_dve", "mul_pool", "aw_ready", "field_ps", "k_stored")}
        p_stored = [sem(f"p_stored_{c}") for c in range(CHUNKS)]
        v_stored = [sem(f"v_stored_{c}") for c in range(CHUNKS)]

        def back(x):
            step = x.ap[-1][0]
            return bass.AP(tensor=x.tensor, offset=x.offset + step * (P - 1), ap=[list(x.ap[0]), [-step, P]])

        def past(i):
            return not isinstance(i, int) or i > 0

        class Order:

            def __init__(self, eng, sm, base=0):
                self.eng, self.sm, self.n, self.base = eng, sm, 0, base

            def __call__(self, ins):
                self.n += 1
                ins.then_inc(self.sm, 1)
                self.eng.wait_ge(self.sm, self.base + self.n)

        block = ctx.enter_context(nc.Block())
        col = lambda ap, n: ap.rearrange("(p a) -> p a", a=1) if n else ap
        CEN_LATE = 12 + (NL - 1) * (4 - POOL_UNITS)
        SQ_LATE = 12 + (NL - 1) * 4
        TWO_PI = 6.2831845
        W_IN = 11 * 16
        ROW_IN = 9 * 16
        ATT_IN = W_IN + 14 * 16
        MIX0_IN = ROW_IN + 9 * 16
        S4_IN = 7 * 16

        @block.sync
        def _(sp):
            def load(dst, src, sm):
                sp.dma_start(dst, src, allow_slow_non_contiguous=True).then_inc(sm, 16)

            load(cst[:, :], a["shape_constants"][:, 0:C_ALL], s["const_in"])
            load(w1r, a["L0_tok_w1"].rearrange("o c k -> o (c k)"), s["w_in"])
            load(w2r, a["L0_tok_w2"].rearrange("o c k -> o (c k)"), s["w_in"])
            load(el[:, 0:D], a["L0_tok_emb"], s["w_in"])
            load(el[:, D:68], a["L0_tok_locality_shapes"], s["w_in"])
            load(w3t, a["L0_tok_w3"].rearrange("o c k -> c (o k)"), s["w_in"])
            load(b1c, col(a["L0_tok_b1"], 1), s["w_in"])
            load(b2c[0:64], col(a["L0_tok_b2"], 1), s["w_in"])
            load(b2c[64:128], col(a["L0_tok_b2"], 1), s["w_in"])
            load(b3c, dram(a["L0_tok_b3"], 0, [[0, P], [1, 1]]), s["w_in"])
            load(msc, dram(a["L0_tok_multiscale_widths"], 0, [[0, P], [1, SC]]), s["w_in"])
            load(swc, dram(a["L0_tok_scale_weights"], 0, [[0, P], [1, SC]]), s["w_in"])
            for j, n in enumerate(("Alog", "Aim", "Cre", "Cim")):
                load(row[:, j], a["L1_attn_" + n].rearrange("(q r) h n -> (r h) q n", r=2), s["row_in"])
            load(ldt, a["L1_attn_log_dt"].rearrange("(q r) h -> (r h) q", r=2), s["row_in"])
            for q in range(4):
                load(skip[32 * q:32 * q + 32], dram(a["L1_attn_D"], q, [[0, 32], [D, NL], [4, 16]]), s["row_in"])
            load(pos[:, :, :], dram(a["fside_BS_continuous_positions"], 0, [[0, P], [L, B], [1, L]]), s["pos_in"])
            sp.wait_ge(s["zk_ready"], 2)
            sp.wait_ge(s["mask_ready"], 1)
            def load_bytes(i):
                if i:
                    sp.wait_ge(s["oh_ready"], i)
                load(xb[0:64, 3:1027], dram(a["x"], i * L, [[0, 64], [1, L]]), s["x_in"])
                load(xb[64:128, 2:1026], dram(a["x"], i * L, [[0, 64], [1, L]]), s["x_in"])

            load_bytes(0)
            for l in range(NL):
                load(k_dram[l][:, 0:P], zk, s["zk_stored"])

            def context(b):
                sp.wait_ge(s["ctx_row"], 2 * b + 2)
                for j in range(2):
                    load(dram(ctx_dram, b * L + 512 * j, [[512, 1], [1, 512]]), crow[64 * j:64 * j + 1, :],
                         s["ctx_stored"])
                sp.wait_ge(s["ctx_stored"], 32 * b + 32)
                load(ctxp[:, NT * b:NT * b + NT], dram(ctx_dram, b * L, [[1, P], [P, NT]]), s["ctx_in"])

            for i in range(NL):
                for c in range(CHUNKS + 1):
                    if c < CHUNKS:
                        sp.wait_ge(s["p_ready"], i * CHUNKS + c + 1)
                        load(p_dram[i][:, c * HCH * P:(c + 1) * HCH * P], pe_t[:, c * HCH:(c + 1) * HCH, :],
                             p_stored[c])
                    if c == 0 and i + 1 < B:
                        load_bytes(i + 1)
                    if c == 2 and i:
                        context(i - 1)
                    if c:
                        d = c - 1
                        sp.wait_ge(s["v_out_dve"], i * 8 + 2 * d + 2)
                        sp.wait_ge(s["v_out_act"], i * 8 + 2 * d + 2)
                        load(v_dram[i][:, d * HCH * P:(d + 1) * HCH * P],
                             vout[d // 2][:, 16 * (d % 2):16 * (d % 2) + 16, :], v_stored[d])
                        sp.wait_ge(s["k_out"], i * 4 + d + 1)
                        for q in range(4):
                            load(dram(k_dram, (i * D + HCH * d + q) * 2 * P + P, [[4 * 2 * P, 1], [4 * 2 * P, 4], [1, P]]),
                                 kst[32 * q:32 * q + 1, d % 2], par["k_stored"][d % 2])
            context(B - 1)
            for j in range(2):
                sp.wait_ge(par["field_ps"][j], FIELD_GROUPS // 2)
            for j, n in enumerate(("Wq", "Wk", "Wv", "Wg")):
                load(wqkvg[0:64, j], a["L0_attn_" + n], s["w_in"])
                load(wqkvg[64:128, j], a["L0_attn_" + n], s["w_in"])
            load(wo, a["L0_attn_Wo"].rearrange("(g p) d -> p g d", p=P), s["w_in"])
            load(bgc, a["L0_attn_bg"].rearrange("(g p) -> p g", p=P), s["w_in"])
            for r in range(2):
                load(boc[64 * r:64 * r + 64], col(a["L0_attn_bo"], 1), s["w_in"])
            for j, n in enumerate(("gamma", "beta")):
                load(gbc[:, j], dram(a["L0_attn_" + n], 0, [[0, P], [1, D]]), s["w_in"])
            load(rwr, a["L0_ffn_router_w"], s["row_in"])
            load(rbb, dram(a["L0_ffn_router_b"], 0, [[0, P], [1, E0]]), s["row_in"])
            for g in range(4):
                load(w1x[0:64, g, :].rearrange("d (e h) -> d e h", e=8),
                     a["L0_ffn_W1"][8 * g:8 * g + 8].rearrange("e d h -> d e h"), s["row_in"])
            load(b1x, a["L0_ffn_b1"].rearrange("(g e) h -> (e h) g", g=4), s["row_in"])
            load(w2x, a["L0_ffn_W2"].rearrange("(g e) h d -> (e h) g d", g=4), s["row_in"])
            load(b2x, a["L0_ffn_b2"], s["row_in"])
            for r in range(2):
                load(wor[:, :, r], a["L1_attn_Wout"].rearrange("l o h -> o l h"), s["s_in"])
                load(bo[64 * r:64 * r + 64], dram(a["L1_attn_bout"], 0, [[1, D], [P, NL], [D, 2]]), s["s_in"])
            load(turn, a["shape_constants"][:, C_J:C_J + P], s["s_in"])
            load(lsb[:, :, 0], dram(a["L1_attn_ln_scale"], 0, [[0, P], [D, NL], [1, D]]), s["s_in"])
            load(lsb[:, :, 1], dram(a["L1_attn_ln_bias"], 0, [[0, P], [D, NL], [1, D]]), s["s_in"])
            for c in range(CHUNKS):
                sp.wait_ge(p_stored[c], 16 * NL)
                sp.wait_ge(v_stored[c], 16 * NL)
            for j in range(2):
                sp.wait_ge(par["k_stored"][j], 64 * 2 * NL)
            sp.wait_ge(s["zk_stored"], 16 * NL)
            for l in range(NL):
                if l:
                    sp.wait_ge(s["xc_ps"], 4 * l)
                else:
                    sp.wait_ge(s["x_ps"], 8)
                load(vt.rearrange("p h t -> p (h t)"), v_dram[l], s["vt_in"])
                if l:
                    sp.wait_ge(s["y_ps"], 4 * l)
                else:
                    sp.wait_ge(s["f0_ps"], 16)
                load(pt.rearrange("p h t -> p (h t)"), p_dram[l], s["pt_in"])
                if l == 0:
                    sp.wait_ge(s["f0t_ps"], 4)
                load(t0, dram(k_dram, l * 2 * P * D + 1, [[1, P], [2 * P, D], [1, P]]), s["t0_in"])
            sp.wait_ge(s["us_out"], 1)
            load(w1e, a["L1_ffn_W1"].rearrange("e d f -> d e f"), s["s_in"])
            load(w2e, a["L1_ffn_W2"].rearrange("e f d -> f e d"), s["s_in"])
            load(b1e, a["L1_ffn_b1"].rearrange("e f -> f e"), s["s_in"])
            sp.wait_ge(s["zk_ready"], 3)
            load(wg32[0:64, 0:E1], a["L1_ffn_Wg"], s["s_in"])
            load(selr, a["shape_constants"][0:24, C_SEL:C_SEL + E1], s["s_in"])
            load(bgx[64:65, 0], dram(a["L1_ffn_bg"], 0, [[E1, 1], [1, E1]]), s["s_in"])
            load(bgx[64:65, 1], dram(a["L1_ffn_bias"], 0, [[E1, 1], [1, E1]]), s["s_in"])
            sp.wait_ge(s["zk_ready"], 4)
            for t in range(16):
                load(b2d[8 * t:8 * t + 8, t, :], a["L1_ffn_b2"], s["pos_in"])
            for k in range(4):
                sp.wait_ge(s["out_ready"], k + 1)
                for i in range(2 * k, 2 * k + 2):
                    load(dram(a["out"], i * P * D, [[D, P], [L * D, B], [1, D]]), ht[:, i], s["stored"])
            sp.wait_ge(s["stored"], 16 * NT)

        @block.gpsimd
        def _(pool):
            pool.memset(zk, 0.0).then_inc(s["zk_ready"], 1)
            pool.memset(h1, 0.0).then_inc(s["zk_ready"], 1)
            pool.wait_ge(s["rt_out"], 1)
            def exponents(l, c):
                hs = slice(c * HCH, (c + 1) * HCH)
                rate = rt[:, 0, bass.ds(l, 1), hs].rearrange("p a h -> p (a h)")
                pool.tensor_tensor(pe_t[:, hs, :], rate.rearrange("p (h a) -> p h a", a=1).broadcast_to([P, HCH, P]),
                                   trow.rearrange("p (a t) -> p a t", a=1).broadcast_to([P, HCH, P]),
                                   ALU.mult).then_inc(s["arg_ready"], 1)

            def turned(l, c):
                hs = slice(c * HCH, (c + 1) * HCH)
                turns = rt[:, 1, bass.ds(l, 1), hs].rearrange("p a h -> p (a h)")
                pool.tensor_tensor(ph_t[:, hs, :], turns.rearrange("p (h a) -> p h a", a=1).broadcast_to([P, HCH, P]),
                                   trow.rearrange("p (a t) -> p a t", a=1).broadcast_to([P, HCH, P]),
                                   ALU.mult).then_inc(s["turned_ready"], 1)

            for c in range(CHUNKS):
                turned(0, c)
            for c in range(CHUNKS):
                exponents(0, c)
            with pool.Fori(0, NL - 1) as l:
                for c in range(CHUNKS + 1):
                    if c < CHUNKS:
                        pool.wait_ge(s["p_ready"], l * 4 + c + 1)
                        turned(l + 1, c)
                    if c:
                        pool.wait_ge(p_stored[c - 1], l * 16 + 16)
                        pool.wait_ge(s["chunk_used"], l * 4 + c)
                        exponents(l + 1, c - 1)
            def square(g):
                p, k = g % 2, g // 2
                pool.wait_ge(par["xd_ready"][p], k + 1)
                pool.wait_ge(par["e_done"][p], k)
                pool.tensor_tensor(xq[:, p], xd[:, p], xd[:, p], ALU.mult).then_inc(par["xq_ready"][p], 1)

            square(0)
            for g in range(FIELD_GROUPS):
                p, b, st = g % 2, g // 4, 2 * (g % 4)
                pool.wait_ge(s["prb_ready"], b + 1)
                pool.wait_ge(par["field_ps"][p], g // 2)
                for j in range(2):
                    rows = amp[:, NT * b + st + j:NT * b + st + j + 1, 0:D].broadcast_to([P, SC, D])
                    ins = pool.tensor_tensor(ampw[:, p, j], rows,
                                             prb[:, b % 2, st + j, 13:17].rearrange("p (s a) -> p s a", a=1)
                                             .broadcast_to([P, SC, D]), ALU.mult)
                ins.then_inc(par["aw_ready"][p], 1)
                if g + 1 < FIELD_GROUPS:
                    square(g + 1)
                pool.wait_ge(par["e_done"][p], g // 2 + 1)
                pool.wait_ge(par["s_done"][p], g // 2 + 1)
                pool.tensor_tensor(eb[p][:, 1], eb[p][:, 1], qb[p][:, 1], ALU.mult)\
                    .then_inc(par["mul_pool"][p], 1)
            def centre(l, u):
                pool.wait_ge(s["mean_ready"], l * POOL_UNITS + u + 1)
                mean = lnw[:, 0, 8 * u:8 * u + 8].rearrange("p (k a) -> p k a", a=1).broadcast_to([P, 8, D])
                pool.tensor_tensor(xc4[:, 8 * u:8 * u + 8], unit(us, u), mean, ALU.add).then_inc(s["cen_pool"], 1)

            def step(l, last=False):
                for u in range(4):
                    pool.wait_ge(s["nrm_ready"], l * 4 + u + 1)
                    pool.tensor_tensor(unit(uu, u), xc4[:, 8 * u:8 * u + 8],
                                       bias_now.rearrange("p (a d) -> p a d", a=1).broadcast_to([P, 8, D]), ALU.add)\
                        .then_inc(s["uu_ready"], 1)
                pool.wait_ge(s["rec_ready"], l + 1)
                pool.tensor_tensor(by_chunk(m4[:, 1]), xa[:, 0], every_chunk(lax[:, 3]), ALU.mult)\
                    .then_inc(s["pm_ready"], 1)
                if not last:
                    for u in range(POOL_UNITS):
                        centre(l, u)
            step(0)
            with pool.Fori(1, NL - 1) as l:
                step(l)
            step(NL - 1, True)
            pool.wait_ge(s["us_out"], 1)
            pool.memset(wg32, 0.0).then_inc(s["zk_ready"], 1)
            pool.memset(b2d, 0.0).then_inc(s["zk_ready"], 1)

        @block.scalar
        def _(act):
            A = act.activation
            act.wait_ge(s["row_in"], ROW_IN)
            A(dtc, ldt, ACT.Exp).then_inc(s["row_act"], 1)
            A(row[:, 4], row[:, 0], ACT.Exp).then_inc(s["row_act"], 1)
            act.wait_ge(s["row_dve"], 1)
            A(row[:, 8], row[:, 5], ACT.Tanh, scale=0.5).then_inc(s["row_act"], 1)
            A(row[:, 9], row[:, 5], ACT.Exp).then_inc(s["row_act"], 1)
            A(row[:, 10], row[:, 5], ACT.Exp, scale=128.0).then_inc(s["row_act"], 1)
            act.wait_ge(s["row_dve"], 2)
            A(row[:, 16:21], row[:, 11:16], ACT.Sin, scale=TWO_PI).then_inc(s["row_act"], 1)
            def decay(i, c):
                hs = slice(c * HCH, (c + 1) * HCH)
                act.wait_ge(s["arg_ready"], i * 4 + c + 1)
                A(pe_t[:, hs, :], pe_t[:, hs, :], ACT.Exp).then_inc(s["exp_done"], 1)

            def sines(i, c):
                hs = slice(c * HCH, (c + 1) * HCH)
                act.wait_ge(s["phase_ready"], i * 4 + c + 1)
                A(ph_t[:, hs, :], ph_t[:, hs, :], ACT.Sin, scale=TWO_PI, bias=n3pi).then_inc(s["sin_done"], 1)

            for c in range(CHUNKS):
                sines(0, c)
            for c in range(CHUNKS):
                decay(0, c)

            def context_out(i):
                act.wait_ge(s["c3_ps"], i)
                if not isinstance(i, int) or i > 1:
                    act.wait_ge(s["ctx_stored"], (i - 1) * 32)
                for j in range(2):
                    A(crow[64 * j:64 * j + 1, :], ps[64 * j:64 * j + 1, 2, :], ACT.Copy).then_inc(s["ctx_row"], 1)

            def step(i, last=False):
                def table_out(c):
                    if past(i):
                        act.wait_ge(v_stored[c], i * 16)
                    for g in (4 * c + 1, 4 * c + 3):
                        act.wait_ge(s["v_ps"], i * 16 + g + 1)
                        h = 4 * (g % 8)
                        A(vout[c // 2][:, h:h + 4, :].rearrange("p h t -> p (h t)"), ps[:, 6, :], ACT.Copy)\
                            .then_inc(s["v_out_act"], 1)

                def ahead(what, *chunks):
                    if not last:
                        for c in chunks:
                            what(i + 1, c)

                table_out(0)
                table_out(1)
                if past(i):
                    context_out(i)
                for j in range(2):
                    act.wait_ge(s["c1_ps"], i * 2 + j + 1)
                    act.wait_ge(s["zk_ready"], 2)
                    if past(i):
                        act.wait_ge(s["c2_ps"], i)
                    A(h1[:, 2 + 512 * j:514 + 512 * j], ps[:, j, :], ACT.Gelu, bias=b1c).then_inc(s["h1_ready"], 1)
                table_out(2)
                table_out(3)
                ahead(sines, 0)
                ahead(sines, 1)
                ahead(sines, 2)
                ahead(sines, 3)
                ahead(decay, 0)
                ahead(decay, 1)
                ahead(decay, 2)
                ahead(decay, 3)
                act.wait_ge(s["c2_ps"], i + 1)
                act.wait_ge(s["mask_ready"], 1)
                if past(i):
                    act.wait_ge(s["ctx_row"], i * 2)
                for j in range(2):
                    A(h2[:, 1 + 512 * j:513 + 512 * j], ps[64 * j:64 * j + 64, 2, :], ACT.Gelu,
                      bias=b2c[64 * j:64 * j + 64]).then_inc(s["h2_ready"], 1)
            step(0)
            step(1)
            with act.Fori(2, NL - 1) as i:
                step(i)
            step(NL - 1, True)
            context_out(NL)
            act.wait_ge(s["small_in"], 1)
            act.wait_ge(s["ctx_in"], 16 * B)
            A(post[:, 2, :, 0], ctxp[:, :], ACT.Sigmoid, bias=b3c).then_inc(s["small_out"], 1)
            A(post[:, 3, :, 0], amp[:, :, 66], ACT.Sigmoid).then_inc(s["small_out"], 1)
            def gauss(g):
                p, b, st, k = g % 2, g // 4, 2 * (g % 4), g // 2
                act.wait_ge(par["xq_ready"][p], k + 1)
                act.wait_ge(par["field_ps"][p], k)
                for j in range(2):
                    for sc in range(SC):
                        ins = A(eb[p][:, j, sc], xq[:, p, j], ACT.Exp,
                                scale=prb[:, b % 2, st + j, 9 + sc:10 + sc])
                ins.then_inc(par["e_done"][p], 1)

            def wave(g):
                p, k = g % 2, g // 2
                act.wait_ge(par["ph_ready"][p], k + 1)
                A(qb[p], qb[p], ACT.Sin, scale=TWO_PI, bias=n3pi).then_inc(par["s_done"][p], 1)

            def field_out(b):
                act.wait_ge(s["acc_ps"], b + 1)
                act.wait_ge(s["htr_ps"], b)
                A(accs[:, :], ps[:, b % 2, :], ACT.Copy).then_inc(s["acc_out"], 1)

            for g in range(FIELD_GROUPS):
                (gauss if g % 2 == 0 else wave)(g)
                (wave if g % 2 == 0 else gauss)(g)
                if g % 4 == 0 and g:
                    field_out(g // 4 - 1)
            field_out(B - 1)

            def sqrt(k):
                act.wait_ge(s["ln_var"], k)
                A(lnw[:, 3], lnw[:, 2], ACT.Sqrt).then_inc(s["ln_sd"], 1)

            def square(n, x, out):
                act.wait_ge(s["cen_ready"], n + 1)
                A(out, x, ACT.Square).then_inc(s["sq_out"], 1)

            for b in range(B):
                square(b, xc[:, 8 * b:8 * b + 8], sq[:, 8 * b:8 * b + 8])
            sqrt(1)
            act.wait_ge(s["ln_var"], 2)
            A(lnw[:, 3], lnw[:, 2], ACT.Sqrt).then_inc(s["ln_sd"], 1)
            for j in range(2):
                act.wait_ge(s["att_ps"], 3 + j)
                A(mnt[:, 1, 512 * j:512 * j + 512], ps[:, 2 + j, :], ACT.Copy).then_inc(s["mnt_out"], 1)
            act.wait_ge(s["w_in"], ATT_IN)
            for u in range(16):
                if u == 8:
                    act.wait_ge(s["small_in"], 2)
                    A(att.rearrange("p a b c d e -> p (a b c d e)"), amx.rearrange("p a b -> p (a b)"), ACT.Exp)\
                        .then_inc(s["small_out"], 1)
                act.wait_ge(s["gate_ps"], u + 1)
                g, b, j = u % 2, u // 4, (u // 2) % 2
                A(gt[:, g, b, 512 * j:512 * j + 512], ps[:, 5 + u % 3, :], ACT.Sigmoid, bias=bgc[:, g:g + 1])\
                    .then_inc(s["gate_out"], 1)
            for b in range(B):
                act.wait_ge(s["o_ps"], b + 1)
                if b >= 2:
                    act.wait_ge(s["ot_ps"], b - 1)
                A(ob[:, b % 2], ps[:, 2 + b % 2, :], ACT.Identity, bias=boc).then_inc(s["o_out"], 1)
                if b:
                    square(B + b - 1, xc[:, 8 * b - 8:8 * b], sq[:, 8 * b - 8:8 * b])
            square(2 * B - 1, xc[:, 24:32], sq[:, 24:32])
            sqrt(3)
            for k in range(4):
                act.wait_ge(s["x_ps"], 2 * k + 2)
                A(x96[0:64, 8 * k + 4:8 * k + 8, :], ps[0:64, 1, :], ACT.Copy).then_inc(s["x_out"], 1)
            act.wait_ge(s["lg_ps"], 3)
            A(lgt0[:, 1], ps[:, 3, :], ACT.Copy).then_inc(s["lgt_out"], 1)
            for n in range(38):
                if n < 32 and n % 2 == 0:
                    g = (n // 2) % 4
                    act.wait_ge(s["hx_ps"], n + 1)
                    if n >= 8:
                        act.wait_ge(s["f0_ps"], (n - 8) // 2 + 1)
                    A(hr[:, n % 8, :], ps[:, n % 4, :], ACT.Relu, bias=b1x[:, g:g + 1]).then_inc(s["hm_ready"], 1)
                if n % 8 == 4 and n >= 12:
                    k = (n - 12) // 8
                    act.wait_ge(s["f0_ps"], 4 * k + 4)
                    if k:
                        act.wait_ge(s["f0t_ps"], k)
                    A(f0, ps[:, 4 + k % 2, :], ACT.Relu).then_inc(s["f0_out"], 1)
                    if k:
                        square(2 * B + k - 1, xc4[:, 8 * k - 8:8 * k], sq4[:, 8 * k - 8:8 * k])
            square(3 * B - 1, xc4[:, 24:32], sq4[:, 24:32])
            sqrt(4)

            def squares(l, u):
                if u < POOL_UNITS:
                    act.wait_ge(s["cen_pool"], l * POOL_UNITS + u + 1)
                else:
                    act.wait_ge(s["cen_ready"], 12 + l * (4 - POOL_UNITS) + u - POOL_UNITS + 1)
                A(sq4[:, 8 * u:8 * u + 8], xc4[:, 8 * u:8 * u + 8], ACT.Square).then_inc(s["sq_out"], 1)

            def step(l, last=False):
                act.wait_ge(s["ln_var"], l + 5)
                A(lnw[:, 3], lnw[:, 2], ACT.Sqrt).then_inc(s["ln_sd"], 1)
                for k in range(4):
                    act.wait_ge(s["xc_ps"], l * 4 + k + 1)
                    A(x4[:, 4 * k:4 * k + 4].rearrange("p g n -> p (g n)"), ps[:, k, :], ACT.Copy)\
                        .then_inc(s["x4_out"], 1)
                for k in range(4):
                    act.wait_ge(s["xm_ps"], l * 4 + k + 1)
                    hp, hh = k // 2, 16 * (k % 2)
                    src = ps[64:128, k, :].rearrange("p (h c) -> p h c", h=16)[:, :, 0:28]
                    A(xa[64 * hp:64 * hp + 64, 1, :, hh:hh + 16, :], src.rearrange("p h (i b) -> p i h b", i=7),
                      ACT.Copy).then_inc(s["xa_out"], 1)
                for k in range(4):
                    act.wait_ge(s["y_ps"], l * 4 + k + 1)
                    A(yg[:, 4 * k:4 * k + 4, :], ps[:, 4 + k, :].rearrange("p (g t) -> p g t", g=4),
                      ACT.Gelu_apprx_tanh).then_inc(s["yg_ready"], 1)
                for k in (0, 2):
                    act.wait_ge(s["t2_ps"], l * 4 + k + 1)
                    A(yt[:, 512 * k:512 * k + 512], ps[:, 4 + k, :], ACT.Copy).then_inc(s["yt_out_a"], 1)

                def gate(u):
                    act.wait_ge(s["z_ps"], l * 4 + u + 1)
                    A(sg[:, u], ps[:, 4 + u, :], ACT.Sigmoid, bias=bcur[:, 1:2]).then_inc(s["sig_done"], 1)

                gate(0)
                gate(1)
                gate(2)
                if not last:
                    squares(l, 0)
                gate(3)
                if not last:
                    for u in range(1, 4):
                        squares(l, u)
            step(0)
            with act.Fori(1, NL - 1) as l:
                step(l)
            step(NL - 1, True)
            for k in range(4):
                square(CEN_LATE + k, xc4[:, 8 * k:8 * k + 8], sq4[:, 8 * k:8 * k + 8])
            sqrt(9)
            for k in range(4):
                act.wait_ge(s["x_ps"], 8 + 2 * k + 2)
                A(x65[0:64, 8 * k + 4:8 * k + 8, :], ps[0:64, 1, :], ACT.Copy).then_inc(s["x_out"], 1)
            act.wait_ge(s["gates_ps"], 2)
            A(lgt1[:, 1], ps[:, 4, :], ACT.Copy).then_inc(s["lgt_out"], 1)
            def hidden(n):
                act.wait_ge(s["hh_ps"], n + 1)
                if n >= 8:
                    act.wait_ge(s["w2_ps"], (n - 8) // 2 + 1)
                e = (n // 2) % E1
                A(h8[:, n % 8, :], ps[:, n % 3, :], ACT.Relu, bias=b1e[:, e:e + 1]).then_inc(s["hid_out"], 1)

            act.wait_ge(s["s_in"], S4_IN + 16 * 7)
            for n in range(6):
                hidden(n)
            act.wait_ge(s["small_in"], 3)
            A(lnw[:, 5], lnw[:, 4], ACT.Exp).then_inc(s["small_out"], 1)
            hidden(6)
            hidden(7)
            for c in range(0, 8, 2):
                act.wait_ge(s["ct_ps"], c + 1)
                A(cmtp[:, 512 * c:512 * c + 512], ps[0:24, 3, :], ACT.Copy).then_inc(s["ct_out_a"], 1)
            for n in range(8, 69):
                if n < 64:
                    hidden(n)
                if n % 16 == 4 and n > 16:
                    k = n // 16 - 1
                    act.wait_ge(s["w2_ps"], 8 * k + 8)
                    if k >= 2:
                        act.wait_ge(s["ft_ps"], k - 1)
                    A(fx[:, k % 2], ps[:, 5 + k % 2, :], ACT.Copy).then_inc(s["fx_out"], 1)

        @block.tensor
        def _(pe):
            def mm(out, lhsT, rhs, start=True, stop=True):
                return pe.matmul(out, lhsT, rhs, start=start, stop=stop)

            pe.wait_ge(s["const_in"], 16)
            pe.wait_ge(s["w_in"], W_IN)
            w1v = w1r.rearrange("o (c k) -> o k c", k=7)
            w2v = w2r.rearrange("o (c k) -> o k c", k=5)
            for j in range(3):
                for r in range(2):
                    mm(ps[64 * r:64 * r + 64, 0, P * j:P * j + P], w1v[:, 2 * j + r], ident)
            mm(ps[0:64, 0, 3 * P:4 * P], w1v[:, 6], ident).then_inc(s["wt_ps"], 1)
            for k in range(5):
                ins = mm(ps[:, 1, D * k:D * k + D], w2v[:, k], ident[0:64, 0:64])
            ins.then_inc(s["wt_ps"], 1)
            for q in range(7):
                if q in (0, 2):
                    pe.wait_ge(s["tin_ready"], q // 2 + 1)
                for r in range(2):
                    k = 2 * q + r
                    ins = pe.transpose(ps[:, 2 + k // 4, P * (k % 4):P * (k % 4) + P],
                                       tin[:, q, r].rearrange("p a n -> p (a n)"), ident)
                if q in (1, 6):
                    ins.then_inc(s["rt_ps"], 1)
            pe.wait_ge(s["wt_out"], 2)
            pe.wait_ge(s["rt_out"], 2)
            def third_conv(i):
                pe.wait_ge(s["h2_ready"], i * 2)
                pe.nop().then_inc(s["wait_taken"], 1)
                for k in range(3):
                    for j in range(2):
                        ins = mm(ps[64 * j:64 * j + 1, 2, :], w3t[:, k:k + 1], h2[:, k + 512 * j:k + 512 * j + 512],
                                 k == 0, k == 2)
                ins.then_inc(s["c3_ps"], 1)

            def step(i):
                pe.wait_ge(s["coef_ready"], i + 1)
                for c in range(CHUNKS):
                    pe.wait_ge(s["p_ready"], i * 4 + c + 1)
                    for g in range(4):
                        gg = 4 * c + g
                        if past(i) or gg >= 2:
                            pe.wait_ge(s["v_out_act"] if gg % 2 else s["v_out_dve"], i * 8 + gg // 2)
                        for q in range(4):
                            ins = pe.transpose(ps[:, 5 + gg % 2, P * q:P * q + P], pe_t[:, 4 * gg + q, :], ident)
                        ins.then_inc(s["v_ps"], 1)
                    if past(i) or c:
                        pe.wait_ge(s["k_out"], i * 4 + c)
                    for g in range(4):
                        for q in range(4):
                            h = HCH * c + 4 * g + q
                            ins = mm(ps[32 * q:32 * q + 32, 7, P * g:P * g + P], coef[:, h:h + 32], pe_t[:, h, :])
                    ins.then_inc(s["chunk_used"], 1)
                    if c < 2:
                        pe.wait_ge(s["oh_ready"], i + 1)
                        if past(i):
                            pe.wait_ge(s["h1_ready"], i * 2)
                        for k in range(3):
                            mm(ps[:, c, :], w1t[:, k], oh[:, 2 * k + 512 * c:2 * k + 512 * c + 512], k == 0, False)
                        mm(ps[:, c, :], w1t[0:64, 3], oh[0:64, 6 + 512 * c:518 + 512 * c], False, True)\
                            .then_inc(s["c1_ps"], 1)
                    if c == 1 and past(i):
                        third_conv(i)
                    if c == 2:
                        if past(i):
                            pe.wait_ge(s["amp_out"], i * 2)
                        for t in range(NT):
                            ins = mm(ps[:, 3 + t // 4, 68 * (t % 4):68 * (t % 4) + 68],
                                     oh[0:64, 3 + P * t:3 + P * t + P], el)
                        ins.then_inc(s["gat_ps"], 1)
                pe.wait_ge(s["h1_ready"], i * 2 + 2)
                if past(i):
                    pe.wait_ge(s["ctx_row"], i * 2)
                for k in range(5):
                    for j in range(2):
                        ins = mm(ps[64 * j:64 * j + 64, 2, :], w2t[:, k], h1[:, k + 512 * j:k + 512 * j + 512],
                                 k == 0, k == 4)
                ins.then_inc(s["c2_ps"], 1)
            step(0)
            with pe.Fori(1, NL) as i:
                step(i)
            third_conv(NL)
            def turn_out(b):
                pe.wait_ge(s["acc_out"], b + 1)
                pe.wait_ge(s["ht_out"], b)
                for c in range(4):
                    ins = pe.transpose(ps[:, 2, P * c:P * c + P], accs[:, P * c:P * c + P], ident)
                ins.then_inc(s["htr_ps"], 1)

            for g in range(FIELD_GROUPS):
                p, b, k = g % 2, g // 4, g // 2
                pe.wait_ge(par["aw_ready"][p], k + 1)
                if g % 4 == 0 and b > 1:
                    pe.wait_ge(s["acc_out"], b - 1)
                for j in range(2):
                    pe.wait_ge(par["mul_pool" if j else "mul_dve"][p], k + 1)
                    for sc in range(SC):
                        for hf in range(2):
                            ins = mm(ps[64 * hf:64 * hf + 64, b % 2, :], ampw[:, p, j, sc],
                                     eb[p][:, j, sc, 512 * hf:512 * hf + 512],
                                     g % 4 == 0 and j == 0 and sc == 0, g % 4 == 3 and j == 1 and sc == SC - 1)
                ins.then_inc(par["field_ps"][p], 1)
                if g % 4 == 3:
                    pe.wait_ge(par["field_ps"][p], k + 1)
                    pe.nop().then_inc(s["acc_ps"], 1)
                if g % 4 == 0 and g:
                    turn_out(b - 1)
            turn_out(B - 1)
            for bp in range(2):
                pe.wait_ge(s["ln_out"], bp + 1)
                for i in range(NT):
                    ins = pe.transpose(ps[:, 2 * bp + i // 4, P * (i % 4):P * (i % 4) + P],
                                       mn[:, i, 2 * bp:2 * bp + 2, :].rearrange("p b d -> p (b d)"), ident)
                    if i % 4 == 3:
                        ins.then_inc(s["att_ps"], 1)
            for sp_ in range(2):
                for i in range(NT):
                    ins = mm(ps[:, 4, 256 * sp_:256 * sp_ + 256],
                             mn[:, i, 2 * sp_:2 * sp_ + 2, :].rearrange("p b d -> p (b d)"),
                             mn[:, i].rearrange("p b d -> p (b d)"), i == 0, i == NT - 1)
            ins.then_inc(s["att_ps"], 1)
            pe.wait_ge(s["att_dve"], 1)
            pe.wait_ge(s["w_in"], ATT_IN)
            pe.wait_ge(s["mnt_out"], 4)
            for tp in range(2):
                for sp_ in range(2):
                    for t2 in range(2):
                        ins = mm(ps[:, 2 * t2 + tp, 256 * sp_:256 * sp_ + 256],
                                 gr[64 * t2:64 * t2 + 64, tp, 128 * sp_:128 * sp_ + 128],
                                 wqkvg[64 * t2:64 * t2 + 64, 1])
            ins.then_inc(s["att_ps"], 1)
            for u in range(16):
                if u == 6:
                    pe.wait_ge(s["att_dve"], 2)
                    r2f = r2.rearrange("p a h -> p (a h)")
                    mm(ps[:, 4, 0:64], cst[:, C_LO:C_LO + P], r2f)
                    mm(ps[:, 4, 64:128], cst[:, C_HI:C_HI + P], r2f).then_inc(s["att_ps"], 1)
                g, b, j = u % 2, u // 4, (u // 2) % 2
                rows = slice(64 * (b % 2), 64 * (b % 2) + 64)
                if u >= 3:
                    pe.wait_ge(s["gate_out"], u - 2)
                mm(ps[:, 5 + u % 3, :], wqkvg[rows, 3, P * g:P * g + P], mnt[rows, b // 2, 512 * j:512 * j + 512])\
                    .then_inc(s["gate_ps"], 1)
            pe.wait_ge(s["att_dve"], 3)
            for n in range(20):
                if n < 16:
                    g, b, j = n % 2, n // 4, (n // 2) % 2
                    if n >= 2:
                        pe.wait_ge(s["og_ready"], n - 1)
                    for tp in range(2):
                        ins = mm(ps[:, n % 2, :], wvs[:, b // 2, b % 2, tp, P * g:P * g + P],
                                 mnt[:, tp, 512 * j:512 * j + 512], tp == 0, tp == 1)
                    ins.then_inc(s["pv_ps"], 1)
                if n % 4 == 1 and n >= 5:
                    b = (n - 5) // 4
                    pe.wait_ge(s["og_ready"], 4 * b + 4)
                    if b >= 2:
                        pe.wait_ge(s["o_out"], b - 1)
                    for g in range(2):
                        for j in range(2):
                            ins = mm(ps[64 * j:64 * j + 64, 2 + b % 2, :], wo[:, g], gt[:, g, b, 512 * j:512 * j + 512],
                                     g == 0, g == 1)
                    ins.then_inc(s["o_ps"], 1)
                if n % 4 == 3 and n >= 7:
                    b = (n - 7) // 4
                    pe.wait_ge(s["o_out"], b + 1)
                    if b >= 2:
                        pe.wait_ge(s["ht_att"], b - 1)
                    for c in range(4):
                        ins = pe.transpose(ps[:, 4 + b % 2, P * c:P * c + P], ob[:, b % 2, P * c:P * c + P], ident)
                    ins.then_inc(s["ot_ps"], 1)
            pe.wait_ge(s["row_in"], MIX0_IN)
            pe.transpose(ps[0:64, 7, 0:E0], rwr, ident[0:32, 0:32]).then_inc(s["lg_ps"], 1)
            pe.wait_ge(s["ln_out"], 3)
            for k in range(8):
                if k >= 2:
                    pe.wait_ge(s["x_out"] if k % 2 else s["rw_out"], k // 2 if k % 2 else k // 2 + 1)
                for t in range(4):
                    ins = pe.transpose(ps[0:64, k % 2, P * t:P * t + P], xn[:, 4 * k + t], ident)
                ins.then_inc(s["x_ps"], 1)
            pe.wait_ge(s["rw_out"], 5)
            pe.wait_ge(s["x_out"], 4)
            for c in range(8):
                ins = mm(ps[32 * (c % 4):32 * (c % 4) + 32, 2 + c // 4, :], rwt,
                         x96[0:64, 4 * c:4 * c + 4, :].rearrange("p t q -> p (t q)"))
                if c % 4 == 3:
                    ins.then_inc(s["lg_ps"], 1)
            pe.wait_ge(s["lgt_out"], 2)
            for r in range(2):
                for b in range(B):
                    ins = pe.transpose(ps[:, 4 + r, P * b:P * b + P], lgt0[:, r, P * b:P * b + P], ident)
            ins.then_inc(s["lg_ps"], 1)
            for k in range(8):
                pe.wait_ge(s["oh0_ready"], 1)
                pe.wait_ge(s["oht_out"], 2 * max(k - 1, 0))
                for t in range(4):
                    ins = pe.transpose(ps[0:32, k % 2, P * t:P * t + P], o2[:, 4 * k + t], ident)
                ins.then_inc(s["oht_ps"], 1)
            pe.wait_ge(s["oht_out"], 16)
            pe.wait_ge(s["mask_ready"], 2)
            for n in range(39):
                if n < 32:
                    k, g, j = n // 8, (n // 2) % 4, n % 2
                    c = 2 * k + j
                    if n >= 4:
                        pe.wait_ge(s["hm_used"] if n % 2 else s["hm_ready"], (n - 4) // 2 + 1)
                    mm(ps[:, n % 4, :], w1x[:, g], x96[0:96, 4 * c:4 * c + 4, :].rearrange("p t q -> p (t q)"))\
                        .then_inc(s["hx_ps"], 1)
                for u in (n - 7, n - 5) if n % 4 == 3 and n >= 7 else ():
                    k, g = u // 8, (u // 2) % 4
                    pe.wait_ge(s["hm_ready"], u // 2 + 1)
                    pe.wait_ge(s["hm_used"], u // 2 + 1)
                    if g == 0 and k >= 2:
                        pe.wait_ge(s["f0_out"], k - 1)
                    for j in range(2):
                        ins = mm(ps[64 * j:64 * j + 64, 4 + k % 2, :], w2x[:, g], hr[:, (u + j) % 8, :], g == 0, False)
                    if g == 3:
                        for j in range(2):
                            c = 2 * k + j
                            ins = mm(ps[64 * j:64 * j + 64, 4 + k % 2, :], b2x,
                                     oht[:, 4 * c:4 * c + 4, :].rearrange("p t q -> p (t q)"), False, True)
                    ins.then_inc(s["f0_ps"], 1)
                if n % 8 == 6 and n >= 14:
                    k = (n - 14) // 8
                    pe.wait_ge(s["f0_out"], k + 1)
                    if k >= 2:
                        pe.wait_ge(s["ht_ffn"], k - 1)
                    for b in range(B):
                        ins = pe.transpose(ps[:, 6 + k % 2, P * b:P * b + P], f0[:, P * b:P * b + P], ident)
                    ins.then_inc(s["f0t_ps"], 1)
            pe.wait_ge(s["s_in"], S4_IN)
            for l in range(NL):
                ins = pe.transpose(ps[:, 0, P * l:P * l + P], wor[:, l].rearrange("p r d -> p (r d)"), ident)
            ins.then_inc(s["lt_ps"], 1)
            pe.wait_ge(s["lt_out"], 1)
            pe.wait_ge(s["ln_out"], 4)
            mm(ps[:, 0, 0:32], turn, lnw[:, 5]).then_inc(s["turn_ps"], 1)
            for k in range(4):
                ins = mm(ps[:, 4 + k, :], turn, uu[:, 8 * k:8 * k + 8, :].rearrange("p t d -> p (t d)"))
                ins.then_inc(s["turn_ps"], 1)
            def step(l):
                pe.wait_ge(s["uu_ready"], l * 4 + 4)
                pe.wait_ge(s["vt_in"], l * 16 + 16)
                for g in range(16):
                    for q in range(4):
                        ins = mm(ps[32 * q:32 * q + 32, g // 4, P * (g % 4):P * (g % 4) + P], uu[:, :, 4 * g + q],
                                 vt[:, 4 * g + q, :])
                    if g % 4 == 3:
                        ins.then_inc(s["xc_ps"], 1)
                for k in range(4):
                    pe.wait_ge(s["x4_out"], l * 4 + k + 1)
                    for g in range(4):
                        ins = pe.transpose(ps[:, k, P * g:P * g + P], x4[:, 4 * k + g, :], ident)
                    ins.then_inc(s["xm_ps"], 1)
                pe.wait_ge(s["t0_in"], l * 16 + 16)
                for g in range(16):
                    for q in range(4):
                        pe.matmul(ps[32 * q:32 * q + 32, 4 + g // 4, P * (g % 4):P * (g % 4) + P], uu[:, :, 4 * g + q],
                                  back(t0[:, 4 * g + q, :]), start=g % 4 == 0, stop=False, skip_group_check=True)
                pe.wait_ge(s["pt_in"], l * 16 + 16)
                for g in range(16):
                    if g % 8 == 0:
                        pe.wait_ge(s["st_ready"], l * 2 + g // 8 + 1)
                    for q in range(4):
                        ins = pe.matmul(ps[32 * q:32 * q + 32, 4 + g // 4, P * (g % 4):P * (g % 4) + P],
                                        sbt[:, 4 * g + q, :], back(pt[:, 4 * g + q, :]), start=False,
                                        stop=True, skip_group_check=True)
                    if g % 4 == 3:
                        ins.then_inc(s["y_ps"], 1)
                for k in range(4):
                    pe.wait_ge(s["yg_ready"], l * 4 + k + 1)
                    for g in range(4):
                        ins = pe.transpose(ps[:, k, P * g:P * g + P], yg[:, 4 * k + g, :], ident)
                    ins.then_inc(s["t1_ps"], 1)
                pe.wait_ge(s["yy_out"], l * 4 + 4)
                for k in range(4):
                    for g in range(4):
                        c = 2 * (4 * k + g)
                        ins = pe.transpose(ps[:, 4 + k, P * g:P * g + P], yy[:, c:c + 2, :].rearrange("p c h -> p (c h)"),
                                           ident)
                    ins.then_inc(s["t2_ps"], 1)

                def z(u):
                    jp, c2 = u // 2, u % 2
                    rows = slice(64 * c2, 64 * c2 + 64)
                    for half in (1, 0):
                        for jj in range(2):
                            k = 2 * jp + jj
                            ins = mm(ps[64 * jj:64 * jj + 64, 4 * half + u, :], w4l[rows, 64 * half:64 * half + 64],
                                     yt[rows, 512 * k:512 * k + 512])
                    ins.then_inc(s["z_ps"], 1)

                def turned_back(u):
                    pe.wait_ge(s["gl_ready"], l * 4 + u + 1)
                    for g in range(4):
                        ins = pe.transpose(ps[:, u, P * g:P * g + P], gl[:, u, P * g:P * g + P], ident)
                    ins.then_inc(s["gt_ps"], 1)

                pe.wait_ge(s["yt_out_a"], l * 2 + 2)
                pe.wait_ge(s["yt_out_d"], l * 2 + 2)
                pe.nop().then_inc(s["wait_taken"], 1)
                z(0)
                z(1)
                turned_back(0)
                z(2)
                turned_back(1)
                z(3)
                turned_back(2)
                turned_back(3)
            step(0)
            with pe.Fori(1, NL) as l:
                step(l)
            for k in range(4):
                pe.wait_ge(s["us_out"], 1)
                mm(ps[:, k, :], turn, us[:, 8 * k:8 * k + 8, :].rearrange("p t d -> p (t d)"))\
                    .then_inc(s["turn_ps"], 1)
            pe.wait_ge(s["ln_out"], 5)
            pe.wait_ge(s["us_out"], 1)
            for k in range(8):
                if k >= 2:
                    pe.wait_ge(s["x_out"] if k % 2 else s["rw_out"], 4 + k // 2 if k % 2 else 5 + k // 2)
                for t in range(4):
                    ins = pe.transpose(ps[0:64, k % 2, P * t:P * t + P], xn1[:, 4 * k + t], ident)
                ins.then_inc(s["x_ps"], 1)
            pe.wait_ge(s["rw_out"], 9)
            pe.wait_ge(s["x_out"], 8)
            pe.wait_ge(s["mask_ready"], 4)
            pe.wait_ge(s["s_in"], S4_IN + 16 * 7)
            for c in range(8):
                ins = mm(ps[32 * (c % 4):32 * (c % 4) + 32, 3 + c // 4, :], wg32,
                         x65[0:65, 4 * c:4 * c + 4, :].rearrange("p t q -> p (t q)"))
                if c % 4 == 3:
                    ins.then_inc(s["gates_ps"], 1)
            pe.wait_ge(s["lgt_out"], 4)
            for r in range(2):
                for b in range(B):
                    ins = pe.transpose(ps[:, 5 + r, P * b:P * b + P], lgt1[:, r, P * b:P * b + P], ident)
            ins.then_inc(s["gates_ps"], 1)
            def hidden(n):
                e, c = (n // 2) % E1, 2 * (n // 16) + n % 2
                if n >= 3:
                    pe.wait_ge(s["hid_out"], n - 2)
                mm(ps[:, n % 3, :], w1e[:, e], x65[0:64, 4 * c:4 * c + 4, :].rearrange("p t q -> p (t q)"))\
                    .then_inc(s["hh_ps"], 1)

            for n in range(8):
                hidden(n)
            pe.wait_ge(s["parts_ready"], 1)
            for c in range(8):
                if c >= 2:
                    pe.wait_ge(s["ct_out_d"] if c % 2 else s["ct_out_a"], c // 2)
                for b in range(B):
                    ins = pe.transpose(ps[0:24, 3 + c % 2, P * b:P * b + P],
                                       cm24[:, 4 * c + b].rearrange("p q e -> p (q e)"), ident)
                ins.then_inc(s["ct_ps"], 1)
            pe.wait_ge(s["pos_in"], 16 + 256)
            for r in range(2):
                ins = pe.transpose(ps[:, 7, P * r:P * r + P],
                                   cmb[:, 16 * r:16 * r + 16, :].rearrange("p t e -> p (t e)"), ident)
            ins.then_inc(s["gates_ps"], 1)
            pe.wait_ge(s["cmt_out"], 1)
            pe.wait_ge(s["ct_out_d"], 4)
            for r in range(2):
                for q in range(2):
                    ins = mm(ps[:, [5, 6, 7, 4][2 * r + q], :], cmt[:, r],
                             b2d[:, 8 * q:8 * q + 8, :].rearrange("p t d -> p (t d)"))
            ins.then_inc(s["gates_ps"], 1)
            pe.wait_ge(s["ct_out_a"], 4)
            for n in range(72):
                if n < 64:
                    k, e, j = n // 16, (n // 2) % E1, n % 2
                    c = 2 * k + j
                    if n >= 8:
                        hidden(n)
                    if n == 1:
                        pe.wait_ge(s["cmt_out"], 2)
                    if n >= 2:
                        pe.wait_ge(s["hw_out"], n - 1)
                    mm(ps[:, 3 + n % 2, :], sel[:, e], cmtp[:, 512 * c:512 * c + 512]).then_inc(s["bc_ps"], 1)
                for u in (n - 7, n - 5) if n % 4 == 3 and 7 <= n < 68 else ():
                    k, e = u // 16, (u // 2) % E1
                    pe.wait_ge(s["hw_out"], u + 2)
                    if e == 0 and k >= 2:
                        pe.wait_ge(s["fx_out"], k - 1)
                    for j in range(2):
                        ins = mm(ps[64 * j:64 * j + 64, 5 + k % 2, :], w2e[:, e], h8[:, (u + j) % 8, :],
                                 e == 0, e == E1 - 1)
                    ins.then_inc(s["w2_ps"], 1)
                if n % 16 == 7 and n > 16:
                    k = n // 16 - 1
                    pe.wait_ge(s["fx_out"], k + 1)
                    if k:
                        pe.wait_ge(s["out_ready"], k)
                    for b in range(B):
                        ins = pe.transpose(ps[:, 7, P * b:P * b + P], fx[:, k % 2, P * b:P * b + P], ident)
                    ins.then_inc(s["ft_ps"], 1)

        @block.vector
        def _(v):
            TT, TS, TC = v.tensor_tensor, v.tensor_scalar, v.tensor_copy

            def bc(ap, n):
                return ap.rearrange("p (k a) -> p k a", a=1).broadcast_to([ap.shape[0], ap.shape[1], n])

            def bcr(ap, n):
                return ap.rearrange("p (a k) -> p a k", a=1).broadcast_to([ap.shape[0], n, ap.shape[1]])

            od = Order(v, s["d_order"])
            od(v.memset(xb, -1))
            v.memset(h2, 0.0).then_inc(s["mask_ready"], 1)
            R = lambda j: row[:, j].rearrange("p q n -> p (q n)")
            v.wait_ge(s["row_act"], 2)
            for q in range(2):
                od(TS(row[:, 5, q], row[:, 4, q], dtc[:, q:q + 1], -1.0, ALU.mult, ALU.mult))
                od(TS(row[:, 6, q], row[:, 1, q], dtc[:, q:q + 1], 1.0 / 6.283185307179586, ALU.mult, ALU.mult))
            v.nop().then_inc(s["row_dve"], 1)

            def whole(dst, src, tmp):
                od(TS(tmp, src, ROUND, ROUND, ALU.add, ALU.subtract))
                od(TT(dst, src, tmp, ALU.subtract))

            whole(R(7), R(6), R(21))
            for r in range(2):
                od(TC(tin[:, 0, :, r], row[:, 5]))
                od(TS(tin[:, 1, :, r], row[:, 7], 2.0 ** MANT, None, ALU.mult))
            v.nop().then_inc(s["tin_ready"], 1)
            od(TC(R(11), R(7)))
            od(TS(R(22), R(7), 0.25, None, ALU.add))
            whole(R(12), R(22), R(21))
            od(TS(R(13), R(7), 0.5, None, ALU.mult))
            od(TS(R(22), R(7), 128.0, None, ALU.mult))
            whole(R(14), R(22), R(21))
            od(TS(R(22), R(14), 0.25, None, ALU.add))
            whole(R(15), R(22), R(21))
            v.nop().then_inc(s["row_dve"], 1)
            v.wait_ge(s["rt_ps"], 1)
            for q in range(2):
                od(TC(rt[:, q].rearrange("p l h -> p (l h)"), ps[:, 2, 256 * q:256 * q + 256]))
            v.nop().then_inc(s["rt_out"], 1)
            v.wait_ge(s["row_act"], 6)
            od(TS(R(21), R(8), -1.0, 1.0, ALU.mult, ALU.add))
            od(v.reciprocal(R(22), R(21)))
            od(TT(R(21), R(8), R(22), ALU.mult))
            od(TS(R(21), R(21), 2.0, None, ALU.mult))
            od(TT(R(21), R(21), R(17), ALU.mult))
            od(TT(R(22), R(18), R(18), ALU.mult))
            od(TS(R(22), R(22), -2.0, None, ALU.mult))
            od(TT(R(21), R(21), R(22), ALU.add))
            od(TT(R(22), R(9), R(16), ALU.mult))
            od(TT(R(23), R(4), R(4), ALU.mult))
            od(TT(R(24), R(1), R(1), ALU.mult))
            od(TT(R(23), R(23), R(24), ALU.add))
            od(v.reciprocal(R(23), R(23)))
            od(TT(R(24), R(22), R(1), ALU.mult))
            od(TT(R(25), R(21), R(4), ALU.mult))
            od(TT(R(24), R(24), R(25), ALU.subtract))
            od(TT(R(24), R(24), R(23), ALU.mult))
            od(TT(R(25), R(22), R(4), ALU.mult))
            od(TT(R(21), R(21), R(1), ALU.mult))
            od(TT(R(25), R(25), R(21), ALU.add))
            od(TT(R(25), R(25), R(23), ALU.mult))
            od(TS(R(25), R(25), -1.0, None, ALU.mult))
            od(TT(R(21), R(2), R(24), ALU.mult))
            od(TT(R(22), R(3), R(25), ALU.mult))
            od(TT(R(21), R(21), R(22), ALU.subtract))
            od(TT(R(22), R(2), R(25), ALU.mult))
            od(TT(R(23), R(3), R(24), ALU.mult))
            od(TT(R(22), R(22), R(23), ALU.add))
            od(TS(tin[:, 2, :, 0], row[:, 21], 2.0, None, ALU.mult))
            od(TS(tin[:, 2, :, 1], row[:, 22], -2.0, None, ALU.mult))
            od(TT(R(23), R(9), R(17), ALU.mult))
            od(TT(R(24), R(9), R(16), ALU.mult))
            od(TT(R(25), R(21), R(23), ALU.mult))
            od(TT(R(11), R(22), R(24), ALU.mult))
            od(TT(R(25), R(25), R(11), ALU.subtract))
            od(TT(R(21), R(21), R(24), ALU.mult))
            od(TT(R(22), R(22), R(23), ALU.mult))
            od(TT(R(21), R(21), R(22), ALU.add))
            for r in range(2):
                od(TT(tin[:, 3, :, r], row[:, 10], row[:, 20], ALU.mult))
                od(TT(tin[:, 4, :, r], row[:, 10], row[:, 19], ALU.mult))
                od(TS(tin[:, 5, :, r], row[:, 25], 2.0, None, ALU.mult))
                od(TS(tin[:, 6, :, r], row[:, 21], 2.0, None, ALU.mult))
            v.nop().then_inc(s["tin_ready"], 1)
            v.wait_ge(s["wt_ps"], 2)
            TC(w1t[:, 0:3].rearrange("p a b -> p (a b)"), ps[:, 0, 0:384])
            TC(w1t[0:64, 3], ps[0:64, 0, 384:512]).then_inc(s["wt_out"], 1)
            TC(w2t.rearrange("p a b -> p (a b)"), ps[:, 1, 0:320]).then_inc(s["wt_out"], 1)
            v.wait_ge(s["rt_ps"], 2)
            od(TC(rt[:, 2].rearrange("p l h -> p (l h)"), ps[:, 3, 0:256]))
            for q in range(4):
                k = 3 + q
                src = ps[:, 2 + k // 2, 256 * (k % 2):256 * (k % 2) + 256].rearrange("p (l h) -> p l h", l=NL)
                for hf in range(2):
                    od(TC(la[64 * hf:64 * hf + 64, q], src[64 * hf:64 * hf + 64, :, 32 * hf:32 * hf + 32]))
            v.nop().then_inc(s["rt_out"], 1)
            def phases(i, c, order):
                v.wait_ge(s["turned_ready"], i * 4 + c + 1)
                w = ph_i[:, c * HCH * P:(c + 1) * HCH * P]
                order(TS(w, ph_f[:, c * HCH * P:(c + 1) * HCH * P], cst[:, C_PH:C_PH + 1], None, ALU.add))
                TS(w, w, (1 << MANT) - 1, ONE_BITS, ALU.bitwise_and, ALU.bitwise_or).then_inc(s["phase_ready"], 1)

            od(v.memset(coef, 0.0))
            for c in range(CHUNKS):
                phases(0, c, od)

            def step(i, last=False):
                ot = Order(v, s["f_order"], i * 16)

                def table_out(c):
                    if past(i):
                        v.wait_ge(v_stored[c], i * 16)
                    for g in (4 * c, 4 * c + 2):
                        v.wait_ge(s["v_ps"], i * 16 + g + 1)
                        h = 4 * (g % 8)
                        TC(vout[c // 2][:, h:h + 4, :].rearrange("p h t -> p (h t)"), ps[:, 5, :])\
                            .then_inc(s["v_out_dve"], 1)
                    v.wait_ge(s["chunk_used"], i * 4 + c + 1)
                    if past(i) or c >= 2:
                        v.wait_ge(par["k_stored"][c % 2], i * 128 + 64 * (c // 2))
                    ot(TC(kst[:, c % 2].rearrange("p g t -> p (g t)"), ps[:, 7, :]))
                    first = kst[:, c % 2, :, 0]
                    TT(first, first, skip[:, bass.ds(i, 1), 4 * c:4 * c + 4].rearrange("p a g -> p (a g)"), ALU.add)\
                        .then_inc(s["k_out"], 1)

                if past(i):
                    v.wait_ge(s["chunk_used"], i * 4)
                TC(coef[:, 0:D], rt[:, 2, bass.ds(i, 1), :].rearrange("p a h -> p (a h)")).then_inc(s["coef_ready"], 1)
                v.wait_ge(s["x_in"], i * 32 + 32)
                if past(i):
                    v.wait_ge(s["gat_ps"], i)
                TS(oh, xb, cst[:, C_PC:C_PC + 1], None, ALU.is_equal).then_inc(s["oh_ready"], 1)
                def product(c):
                    hs = slice(c * HCH, (c + 1) * HCH)
                    v.wait_ge(s["exp_done"], i * 4 + c + 1)
                    v.wait_ge(s["sin_done"], i * 4 + c + 1)
                    TT(pe_t[:, hs, :], pe_t[:, hs, :], ph_t[:, hs, :], ALU.mult).then_inc(s["p_ready"], 1)

                product(0)
                product(1)
                product(2)
                table_out(0)
                product(3)
                table_out(1)
                if not last:
                    phases(i + 1, 0, ot)
                table_out(2)
                if not last:
                    phases(i + 1, 1, ot)
                table_out(3)
                if not last:
                    phases(i + 1, 2, ot)
                if not last:
                    phases(i + 1, 3, ot)
                v.wait_ge(s["gat_ps"], i + 1)
                for j in range(2):
                    TC(amp[:, bass.ds(i * 8 + 4 * j, 4), :], ps[:, 3 + j, 0:272].rearrange("p (t c) -> p t c", t=4))\
                        .then_inc(s["amp_out"], 1)
                v.wait_ge(s["k_out"], i * 4 + 4)
                v.nop().then_inc(s["f_order"], 16 - ot.n)
            step(0)
            with v.Fori(1, NL - 1) as i:
                step(i)
            step(NL - 1, True)
            v.wait_ge(s["amp_out"], 2 * B)
            v.nop().then_inc(s["small_in"], 1)
            lp = lambda j: amp[:, :, 64 + j]
            prf = prm[:, :, :, :].rearrange("p b t c -> p (b t) c")
            od(TS(post[:, 0, :, 0], lp(0), 0.05, None, ALU.mult))
            for b in range(B):
                od(TT(prf[:, 8 * b:8 * b + 8, 0], post[:, 0, 8 * b:8 * b + 8, 0], cst[:, C_BP:C_BP + NT], ALU.add))
            od(TS(post[:, 10, :, 0], lp(1), -1.0, None, ALU.mult))
            od(TT(post[:, 1, :, 0], post[:, 10, :, 0], lp(1), ALU.max))
            od(TT(post[:, 4], bc(post[:, 1, :, 0], SC), bcr(msc, 32), ALU.mult))
            od(TS(post[:, 4], post[:, 4], 1e-5, None, ALU.add))
            od(v.reciprocal(post[:, 5], post[:, 4]))
            od(TS(prf[:, :, 1:5], post[:, 5], 2.0 ** MANT, None, ALU.mult))
            od(TT(post[:, 6], post[:, 5], post[:, 5], ALU.mult))
            od(TS(prf[:, :, 9:13], post[:, 6], -0.5, None, ALU.mult))
            od(TS(post[:, 7, :, 0], lp(3), 0.5, 0.75, ALU.mult, ALU.add))
            od(TS(post[:, 8, :, 0], post[:, 7, :, 0], ROUND, ROUND, ALU.add, ALU.subtract))
            od(TT(post[:, 7, :, 0], post[:, 7, :, 0], post[:, 8, :, 0], ALU.subtract))
            od(TS(post[:, 7, :, 0], post[:, 7, :, 0], 2.0 ** MANT, None, ALU.mult))
            od(TC(prf[:, :, 5:9], bc(post[:, 7, :, 0], SC)))
            od(TT(swc, swc, swc, ALU.mult))
            v.wait_ge(s["small_out"], 2)
            od(TT(post[:, 9, :, 0], post[:, 2, :, 0], post[:, 3, :, 0], ALU.mult))
            od(TT(prf[:, :, 13:17], bc(post[:, 9, :, 0], SC), bcr(swc, 32), ALU.mult))
            for c in range(CHUNKS):
                v.wait_ge(p_stored[c], 16 * NL)
                v.wait_ge(v_stored[c], 16 * NL)
            for j in range(2):
                v.wait_ge(par["k_stored"][j], 64 * 2 * NL)
            v.wait_ge(s["zk_stored"], 16 * NL)
            v.wait_ge(s["pos_in"], 16)
            om = Order(v, s["m_order"])

            def front(g):
                p, b, st, k = g % 2, g // 4, 2 * (g % 4), g // 2
                if g % 4 == 0:
                    v.wait_ge(par["e_done"][1], max(2 * b - 2, 0))
                    v.wait_ge(par["aw_ready"][1], max(2 * b - 2, 0))
                    TC(prb[:, b % 2], prm[:, b])\
                        .then_inc(s["prb_ready"], 1)
                    v.wait_ge(s["prb_ready"], b + 1)
                v.wait_ge(par["mul_dve"][p], k)
                v.wait_ge(par["ph_ready"][p], k)
                v.wait_ge(par["xq_ready"][p], k)
                for j in range(2):
                    ins = TS(xd[:, p, j], pos[:, b, :],
                             prb[:, b % 2, st + j, 0:1], None, ALU.subtract)
                ins.then_inc(par["xd_ready"][p], 1)
                v.wait_ge(par["xd_ready"][p], k + 1)
                v.wait_ge(par["mul_pool"][p], k)
                for j in range(2):
                    for sc in range(SC):
                        w = (4 * j + sc) * L
                        ins = TS(qi[p][:, w:w + L], xd[:, p, j], prb[:, b % 2, st + j, 1 + sc:2 + sc],
                                 prb[:, b % 2, st + j, 5 + sc:6 + sc], ALU.mult, ALU.add)
                om(ins)
                TS(qi[p], qi[p], (1 << MANT) - 1, ONE_BITS, ALU.bitwise_and, ALU.bitwise_or)\
                    .then_inc(par["ph_ready"][p], 1)

            def product(g):
                p, k = g % 2, g // 2
                v.wait_ge(par["e_done"][p], k + 1)
                v.wait_ge(par["s_done"][p], k + 1)
                TT(eb[p][:, 0], eb[p][:, 0], qb[p][:, 0], ALU.mult).then_inc(par["mul_dve"][p], 1)

            def field_out(b):
                v.wait_ge(s["htr_ps"], b + 1)
                for hf in range(2):
                    dst = ht[:, 4 * hf:4 * hf + 4, b, :]
                    src = ps[:, 2, :].rearrange("p (c f d) -> p c f d", c=4, f=2)[:, :, hf]
                    ins = TC(dst, src)
                ins.then_inc(s["ht_out"], 1)

            front(0)
            for g in range(1, FIELD_GROUPS):
                front(g)
                product(g - 1)
                if g % 4 == 2 and g > 4:
                    field_out(g // 4 - 1)
            product(FIELD_GROUPS - 1)

            def centred(x, k, out):
                w = lnw[:, 0, 8 * k:8 * k + 8]
                od(v.reduce_sum(w, x, axis=AX.X))
                od(TS(w, w, -1.0 / D, None, ALU.mult))
                TT(out[:, 8 * k:8 * k + 8], x, bc(w, D), ALU.add).then_inc(s["cen_ready"], 1)

            def square_sums(n, sq_):
                for k in range(4):
                    v.wait_ge(s["sq_out"], n + k + 1)
                    od(v.reduce_sum(lnw[:, 1, 8 * k:8 * k + 8], sq_[:, 8 * k:8 * k + 8], axis=AX.X))

            def rstd(k):
                TS(lnw[:, 2], lnw[:, 1], 1.0 / D, EPS, ALU.mult, ALU.add).then_inc(s["ln_var"], 1)
                v.wait_ge(s["ln_sd"], k)
                od(v.reciprocal(lnw[:, 4], lnw[:, 3]))

            flat = lambda t: t.rearrange("p i b d -> p (i b) d")
            htf = flat(ht[:, :, :, :])
            v.wait_ge(par["field_ps"][0], FIELD_GROUPS // 2)
            for b in range(B):
                if b == B - 1:
                    field_out(b)
                v.wait_ge(s["ht_out"], b + 1)
                centred(ht[:, :, b, :], b, xc)
            square_sums(0, sq)
            rstd(1)
            od(TT(lnw[:, 5], lnw[:, 4], lnw[:, 4], ALU.mult))
            od(TT(lnw[:, 1], lnw[:, 1], lnw[:, 5], ALU.mult))
            od(TC(lnw[:, 5], lnw[:, 4]))
            rstd(2)
            od(TT(lnw[:, 4], lnw[:, 4], lnw[:, 5], ALU.mult))
            v.wait_ge(s["w_in"], ATT_IN)
            v.wait_ge(par["field_ps"][1], FIELD_GROUPS // 2)
            for b in range(B):
                w = xc[:, 8 * b:8 * b + 8]
                od(TT(w, w, bc(lnw[:, 4, 8 * b:8 * b + 8], D), ALU.mult))
                od(TT(w, w, bcr(gbc[:, 0], 8), ALU.mult))
                ins = TT(mn[:, :, b, :], w, bcr(gbc[:, 1], 8), ALU.add)
                if b % 2:
                    ins.then_inc(s["ln_out"], 1)
            for j in range(2):
                v.wait_ge(s["att_ps"], 1 + j)
                TC(mnt[:, 0, 512 * j:512 * j + 512], ps[:, j, :]).then_inc(s["mnt_out"], 1)
            v.wait_ge(s["att_ps"], 5)
            TC(gr.rearrange("p a b -> p (a b)"), ps[:, 4, :]).then_inc(s["att_dve"], 1)
            v.wait_ge(s["att_ps"], 6)
            for k in range(4):
                od(TT(rr[:, 2 * k:2 * k + 2], ps[:, k, :].rearrange("p (a c) -> p a c", a=2),
                      bcr(wqkvg[:, 0], 2), ALU.mult))
            v.reduce_sum(r2.rearrange("p a h -> p (a h)"), rr.rearrange("p a (h c) -> p (a h) c", c=CH), axis=AX.X)\
                .then_inc(s["att_dve"], 1)
            v.wait_ge(s["att_ps"], 7)
            sc_att = 1.0 / (CH ** 0.5) / (L ** 0.5)
            lgt = rr.rearrange("p a c -> p (a c)")[:, 0:128]
            od(TS(lgt, ps[:, 4, 0:128], sc_att, None, ALU.mult))
            by_t = lambda x: x.rearrange("p (s t k) -> p s k t", s=2, t=4)
            mx = rr.rearrange("p a c -> p (a c)")[:, 128:160]
            od(v.reduce_max(mx.rearrange("p (s k) -> p s k", s=2), by_t(lgt), axis=AX.X))
            amf = amx.rearrange("p a b -> p (a b)")
            for s2 in range(2):
                ins = TT(amf[:, 64 * s2:64 * s2 + 64].rearrange("p (t k) -> p t k", t=4),
                         lgt[:, 64 * s2:64 * s2 + 64].rearrange("p (t k) -> p t k", t=4),
                         bcr(mx[:, 16 * s2:16 * s2 + 16], 4), ALU.subtract)
            ins.then_inc(s["small_in"], 1)
            v.wait_ge(s["small_out"], 3)
            atf = att.rearrange("p a b c d e -> p (a b c d e)")
            od(v.reduce_sum(mx.rearrange("p (s k) -> p s k", s=2), by_t(atf), axis=AX.X))
            od(v.reciprocal(mx, mx))
            for s2 in range(2):
                w = atf[:, 64 * s2:64 * s2 + 64].rearrange("p (t k) -> p t k", t=4)
                od(TT(w, w, bcr(mx[:, 16 * s2:16 * s2 + 16], 4), ALU.mult))
            for t2 in range(2):
                rows = slice(64 * t2, 64 * t2 + 64)
                for sp_ in range(2):
                    for s2 in range(2):
                        for tp in range(2):
                            ins = TT(wvs[rows, sp_, s2, tp].rearrange("p (h c) -> p h c", h=NH),
                                     wqkvg[rows, 2].rearrange("p (h c) -> p h c", h=NH),
                                     bc(att[rows, s2, t2, tp, sp_], CH), ALU.mult)
            ins.then_inc(s["att_dve"], 1)
            for n in range(20):
                if n < 16:
                    g, b, j = n % 2, n // 4, (n // 2) % 2
                    w = gt[:, g, b, 512 * j:512 * j + 512]
                    v.wait_ge(s["gate_out"], n + 1)
                    v.wait_ge(s["pv_ps"], n + 1)
                    TT(w, ps[:, n % 2, :], w, ALU.mult).then_inc(s["og_ready"], 1)
                if n % 4 == 3 and n >= 7:
                    b = (n - 7) // 4
                    v.wait_ge(s["ot_ps"], b + 1)
                    for hf in range(2):
                        w = ht[:, 4 * hf:4 * hf + 4, b, :]
                        ins = TT(w, w, ps[:, 4 + b % 2, :].rearrange("p (c f d) -> p c f d", c=4, f=2)[:, :, hf],
                                 ALU.add)
                    ins.then_inc(s["ht_att"], 1)
                    v.wait_ge(s["ht_att"], b + 1)
                    centred(ht[:, :, b, :], b, xc)
            v.wait_ge(s["row_in"], MIX0_IN)
            for g in range(4):
                ins = TC(w1x[64:96, g].rearrange("p (e h) -> p e h", e=8),
                         bc(cst[64:96, C_BIG + 8 * g:C_BIG + 8 * g + 8], H0))
            ins.then_inc(s["mask_ready"], 1)
            v.wait_ge(s["lg_ps"], 1)
            TC(rwt, ps[0:64, 7, 0:E0]).then_inc(s["rw_out"], 1)
            square_sums(B, sq)
            rstd(3)
            for b in range(B):
                ins = TT(xn.rearrange("p (i b) d -> p i b d", b=B)[:, :, b, :], xc[:, 8 * b:8 * b + 8],
                         bc(lnw[:, 4, 8 * b:8 * b + 8], D), ALU.mult)
            ins.then_inc(s["ln_out"], 1)
            for k in range(4):
                v.wait_ge(s["x_ps"], 2 * k + 1)
                TC(x96[0:64, 8 * k:8 * k + 4, :].rearrange("p t q -> p (t q)"), ps[0:64, 0, :])\
                    .then_inc(s["rw_out"], 1)
            v.wait_ge(s["lg_ps"], 2)
            TC(lgt0[:, 0], ps[:, 2, :]).then_inc(s["lgt_out"], 1)
            v.wait_ge(s["lg_ps"], 4)
            for r in range(2):
                ins = TT(lg[:, 16 * r:16 * r + 16].rearrange("p (c b) e -> p b c e", b=B),
                         ps[:, 4 + r, :].rearrange("p (b c e) -> p b c e", b=B, c=4),
                         rbb.rearrange("p (a c e) -> p a c e", a=1, c=1).broadcast_to([P, B, 4, E0]), ALU.add)
            od(ins)
            od(v.reduce_max(lnw[:, 0], lg, axis=AX.X))
            od(TT(o1, lg, bc(lnw[:, 0], E0), ALU.is_equal))
            od(TT(o1, o1, bcr(cst[:, C_DESC:C_DESC + E0], 32), ALU.mult))
            od(v.reduce_max(lnw[:, 1], o1, axis=AX.X))
            TT(o2, o1, bc(lnw[:, 1], E0), ALU.is_equal).then_inc(s["oh0_ready"], 1)
            for k in range(8):
                v.wait_ge(s["oht_ps"], k + 1)
                TC(oht[:, 4 * k:4 * k + 4].rearrange("p t q -> p (t q)"), ps[0:32, k % 2, :])\
                    .then_inc(s["oht_out"], 1)
                TS(x96[64:96, 4 * k:4 * k + 4].rearrange("p t q -> p (t q)"), ps[0:32, k % 2, :], -1.0, None,
                   ALU.add).then_inc(s["oht_out"], 1)
            for n in range(40):
                if n < 32 and n % 2:
                    g = (n // 2) % 4
                    v.wait_ge(s["hx_ps"], n + 1)
                    if n >= 8:
                        v.wait_ge(s["f0_ps"], (n - 8) // 2 + 1)
                    TS(hr[:, n % 8, :], ps[:, n % 4, :], b1x[:, g:g + 1], 0.0, ALU.add, ALU.max)\
                        .then_inc(s["hm_used"], 1)
                if n % 8 == 7 and n >= 15:
                    k = (n - 15) // 8
                    v.wait_ge(s["f0t_ps"], k + 1)
                    w = ht[:, 2 * k:2 * k + 2].rearrange("p i b d -> p b i d")
                    TT(w, w, ps[:, 6 + k % 2, :].rearrange("p (b i d) -> p b i d", b=B, i=2), ALU.add)\
                        .then_inc(s["ht_ffn"], 1)
                    v.wait_ge(s["ht_ffn"], k + 1)
                    centred(htf[:, 8 * k:8 * k + 8], k, xc4)
            v.wait_ge(s["lt_ps"], 1)
            TC(wo4.rearrange("p l o -> p (l o)"), ps[:, 0, :]).then_inc(s["lt_out"], 1)
            v.wait_ge(s["lt_out"], 1)
            v.wait_ge(s["ht_ffn"], 4)
            v.wait_ge(s["s_in"], S4_IN)
            square_sums(2 * B, sq4)
            rstd(4)
            od(TT(lnw[:, 5], lnw[:, 4], lnw[:, 4], ALU.mult))
            od(TT(lnw[:, 5], lnw[:, 1], lnw[:, 5], ALU.mult))
            TT(uu, xc4, bc(lnw[:, 4], D), ALU.mult).then_inc(s["ln_out"], 1)
            od(v.memset(sbt, 0.0))
            v.wait_ge(s["turn_ps"], 1)
            od(TC(lnw[:, 1].rearrange("p (jp c x) -> p jp x c", jp=2, c=2),
                  ps[:, 0, 0:32].rearrange("p (jp x c) -> p jp x c", jp=2, c=2)))
            for k in range(4):
                v.wait_ge(s["turn_ps"], k + 2)
                od(TC(us[:, 8 * k:8 * k + 8, :].rearrange("p t d -> p (t d)"), ps[:, 4 + k, :]))

            def stats(u, order):
                w = lnw[:, 0, 8 * u:8 * u + 8]
                order(v.reduce_sum(w, unit(us, u), axis=AX.X))
                if u < POOL_UNITS:
                    TS(w, w, -1.0 / D, None, ALU.mult).then_inc(s["mean_ready"], 1)
                else:
                    order(TS(w, w, -1.0 / D, None, ALU.mult))
                    TT(xc4[:, 8 * u:8 * u + 8], unit(us, u), bc(w, D), ALU.add).then_inc(s["cen_ready"], 1)

            def squared(l, u, order):
                v.wait_ge(s["sq_out"], 12 + l * 4 + u + 1)
                order(v.reduce_sum(lnw[:, 1, 8 * u:8 * u + 8], sq4[:, 8 * u:8 * u + 8], axis=AX.X))

            def step(l, last=False):
                O = Order(v, s["s_order"], l * 128)
                TS(lnw[:, 2], lnw[:, 1], 1.0 / D, EPS, ALU.mult, ALU.add).then_inc(s["ln_var"], 1)
                O(TC(bias_now, lsb[:, bass.ds(l, 1), 1, :].rearrange("p a d -> p (a d)")))
                v.wait_ge(s["ln_sd"], l + 5)
                O(v.reciprocal(lnw[:, 4], lnw[:, 3]))

                def scale(u):
                    w = xc4[:, 8 * u:8 * u + 8]
                    v.wait_ge(s["nrm_part"], l * 4 + u + 1)
                    TT(w, w, lsb[:, bass.ds(l, 1), 0, :].broadcast_to([P, 8, D]), ALU.mult).then_inc(s["nrm_ready"], 1)

                for u in range(4):
                    w = xc4[:, 8 * u:8 * u + 8]
                    TT(w, w if past(l) else unit(us, u), bc(lnw[:, 4, 8 * u:8 * u + 8], D), ALU.mult)\
                        .then_inc(s["nrm_part"], 1)
                    if u:
                        scale(u - 1)
                scale(3)
                TC(w4l[:, :], wo4[:, bass.ds(l, 1), :].rearrange("p a o -> p (a o)"))
                TC(bcur, bo[:, bass.ds(l, 1), :].rearrange("p a z -> p (a z)"))
                for q in range(4):
                    ins = TC(lax[:, q].rearrange("p (h b) -> p h b", b=B),
                             bc(la[:, q, bass.ds(l, 1), :].rearrange("p a h -> p (a h)"), B))
                O(ins)
                for k in range(4):
                    v.wait_ge(s["xm_ps"], l * 4 + k + 1)
                    hp, hh = k // 2, 16 * (k % 2)
                    src = ps[0:64, k, :].rearrange("p (h c) -> p h c", h=16)[:, :, 0:28]
                    ins = TC(xa[64 * hp:64 * hp + 64, 0, :, hh:hh + 16, :], src.rearrange("p h (i b) -> p i h b", i=7))
                O(ins)
                v.wait_ge(s["xa_out"], l * 4 + 4)
                for i in range(1, 7):
                    last_s = xa[:, :, i - 1].rearrange("p r h b -> p r (h b)")
                    xi = xa[:, :, i].rearrange("p r h b -> p r (h b)")
                    TT(m4[:, 0:2, 0:128], last_s, bcr(lax[:, 0], 2), ALU.mult)
                    O(TT(m4[:, 2:4, 0:128], last_s, bcr(lax[:, 1], 2), ALU.mult))
                    O(TT(xi, xi, m4[:, 0:2, 0:128], ALU.add))
                    TT(xi[:, 0], xi[:, 0], m4[:, 3, 0:128], ALU.subtract)
                    O(TT(xi[:, 1], xi[:, 1], m4[:, 2, 0:128], ALU.add))
                v.nop().then_inc(s["rec_ready"], 1)
                for ri, gi in ((0, 0), (1, 1), (1, 0)):
                    ins = TT(by_chunk(m4[:, 2 * ri + gi]), xa[:, ri], every_chunk(lax[:, 2 + gi]), ALU.mult)
                O(ins)
                m = lambda rows, k: m4[rows, k].rearrange("p (h c) -> p h c", c=28)
                halves = [(slice(64 * hp, 64 * hp + 64), slice(32 * hp, 32 * hp + 32)) for hp in range(2)]
                v.wait_ge(s["pm_ready"], l + 1)
                for rows, hs in halves:
                    TT(sbt[0:64, hs, 4:32], m(rows, 0), m(rows, 3), ALU.subtract)
                    v.scalar_tensor_tensor(sbt[64:128, hs, 4:32], m(rows, 1), -1.0, m(rows, 2), ALU.mult,
                                           ALU.subtract).then_inc(s["st_ready"], 1)
                for k in range(4):
                    v.wait_ge(s["t1_ps"], l * 4 + k + 1)
                    TC(yy[:, :, 16 * k:16 * k + 16].rearrange("p c h -> p h c"),
                       ps[:, k, :].rearrange("p (h c) -> p h c", h=16)).then_inc(s["yy_out"], 1)
                for k in (1, 3):
                    v.wait_ge(s["t2_ps"], l * 4 + k + 1)
                    TC(yt[:, 512 * k:512 * k + 512], ps[:, 4 + k, :]).then_inc(s["yt_out_d"], 1)

                def gated(u):
                    v.wait_ge(s["sig_done"], l * 4 + u + 1)
                    v.scalar_tensor_tensor(gl[:, u], ps[:, u, :], bcur[:, 0:1], sg[:, u], ALU.add, ALU.mult)\
                        .then_inc(s["gl_ready"], 1)

                def residual(u):
                    jp, c2 = u // 2, u % 2
                    v.wait_ge(s["gt_ps"], l * 4 + u + 1)
                    w = us[:, 16 * jp:16 * jp + 16].rearrange("p (jj g c) o -> p g jj c o", jj=2, c=2)[:, :, :, c2, :]
                    O(TT(w, w, ps[:, u, :].rearrange("p (g jj o) -> p g jj o", g=4, jj=2), ALU.add))
                    if not last:
                        stats(u, O)

                gated(0)
                gated(1)
                residual(0)
                gated(2)
                residual(1)
                if not last:
                    squared(l, 0, O)
                gated(3)
                residual(2)
                residual(3)
                if not last:
                    for u in range(1, 4):
                        squared(l, u, O)
                else:
                    v.nop().then_inc(s["us_out"], 1)
                assert O.n <= 128
                v.nop().then_inc(s["s_order"], 128 - O.n)
            step(0)
            with v.Fori(1, NL - 1) as l:
                step(l)
            step(NL - 1, True)
            for k in range(4):
                v.wait_ge(s["turn_ps"], 6 + k)
                w = htf[:, 8 * k:8 * k + 8]
                od(TT(w, w, ps[:, k, :].rearrange("p (t d) -> p t d", t=8), ALU.add))
                centred(w, k, xc4)
            square_sums(SQ_LATE, sq4)
            rstd(9)
            TT(xn1, xc4, bc(lnw[:, 4], D), ALU.mult).then_inc(s["ln_out"], 1)
            v.wait_ge(s["s_in"], S4_IN + 16 * 7)
            TC(sel.rearrange("p e q -> p (e q)").rearrange("p (e q) -> p e q", e=E1), bc(selr, P))
            TT(wg32[64:65, 0:E1], bgx[64:65, 0], bgx[64:65, 1], ALU.add).then_inc(s["mask_ready"], 1)
            v.memset(x65[64:65].rearrange("p t q -> p (t q)"), 1.0).then_inc(s["mask_ready"], 1)
            for k in range(4):
                v.wait_ge(s["x_ps"], 8 + 2 * k + 1)
                TC(x65[0:64, 8 * k:8 * k + 4, :].rearrange("p t q -> p (t q)"), ps[0:64, 0, :])\
                    .then_inc(s["rw_out"], 1)
            v.wait_ge(s["gates_ps"], 1)
            TC(lgt1[:, 0], ps[:, 3, :]).then_inc(s["lgt_out"], 1)
            v.wait_ge(s["gates_ps"], 3)
            desc = bcr(cst[:, C_DESC + E0 - E1:C_DESC + E0], 32)

            def first_max(dst, src, mxc):
                od(v.reduce_max(mxc, src, axis=AX.X))
                od(TT(cm3, src, bc(mxc, E1), ALU.is_equal))
                od(TT(cm3, cm3, desc, ALU.mult))
                od(v.reduce_max(lnw[:, 3], cm3, axis=AX.X))
                od(TT(dst, cm3, bc(lnw[:, 3], E1), ALU.is_equal))

            for r in range(2):
                ins = TC(cm2[:, 16 * r:16 * r + 16].rearrange("p (c b) e -> p b c e", b=B),
                         ps[:, 5 + r, :].rearrange("p (b c e) -> p b c e", b=B, c=4)[:, :, :, 0:E1])
            od(ins)
            first_max(cmb, cm2, lnw[:, 0])
            od(TS(f1[:, :, 0:E1], cmb, -3.0e38, None, ALU.mult))
            od(TT(cm2, cm2, f1[:, :, 0:E1], ALU.add))
            first_max(f1[:, :, 8:16], cm2, lnw[:, 1])
            TT(lnw[:, 4], lnw[:, 1], lnw[:, 0], ALU.subtract).then_inc(s["small_in"], 1)
            v.wait_ge(s["small_out"], 4)
            od(TS(lnw[:, 0], lnw[:, 5], 1.0, None, ALU.add))
            od(v.reciprocal(lnw[:, 1], lnw[:, 0]))
            od(TT(lnw[:, 2], lnw[:, 5], lnw[:, 1], ALU.mult))
            od(TT(cmb, cmb, bc(lnw[:, 1], E1), ALU.mult))
            od(TT(f1[:, :, 8:16], f1[:, :, 8:16], bc(lnw[:, 2], E1), ALU.mult))
            od(TT(cmb, cmb, f1[:, :, 8:16], ALU.add))
            high = -65536
            cmi = cut(27168, 32 * E1, dt=I32).rearrange("p (t e) -> p t e", t=32)
            od(TS(cm24i[:, :, 0], cmi, high, None, ALU.bitwise_and))
            od(TT(cm2, cmb, cm24[:, :, 0], ALU.subtract))
            cm2i = cut(27424, 32 * E1, dt=I32).rearrange("p (t e) -> p t e", t=32)
            od(TS(cm24i[:, :, 1], cm2i, high, None, ALU.bitwise_and))
            TT(cm24[:, :, 2], cm2, cm24[:, :, 1], ALU.subtract).then_inc(s["parts_ready"], 1)
            for c in range(1, 8, 2):
                v.wait_ge(s["ct_ps"], c + 1)
                TC(cmtp[:, 512 * c:512 * c + 512], ps[0:24, 4, :]).then_inc(s["ct_out_d"], 1)
            v.wait_ge(s["gates_ps"], 4)
            TC(cmt.rearrange("p a b -> p (a b)"), ps[:, 7, 0:256]).then_inc(s["cmt_out"], 1)
            v.wait_ge(s["gates_ps"], 5)
            for k in range(4):
                w = htf[:, 8 * k:8 * k + 8]
                ins = TT(w, w, ps[:, [5, 6, 7, 4][k], :].rearrange("p (t d) -> p t d", t=8), ALU.add)
            ins.then_inc(s["cmt_out"], 1)
            v.wait_ge(s["cmt_out"], 2)
            for n in range(72):
                if n < 64:
                    v.wait_ge(s["hid_out"], n + 1)
                    v.wait_ge(s["bc_ps"], n + 1)
                    w = h8[:, n % 8, :]
                    TT(w, w, ps[:, 3 + n % 2, :], ALU.mult).then_inc(s["hw_out"], 1)
                if n % 16 == 7 and n > 16:
                    k = n // 16 - 1
                    v.wait_ge(s["ft_ps"], k + 1)
                    w = ht[:, 2 * k:2 * k + 2].rearrange("p i b d -> p b i d")
                    TT(w, w, ps[:, 7, :].rearrange("p (b i d) -> p b i d", b=B, i=2), ALU.add)\
                        .then_inc(s["out_ready"], 1)


def kernel(**inputs):
    import numpy as np
    from concourse import bacc
    from concourse.bass_utils import run_bass_kernel_spmd

    nc = bacc.Bacc("TRN2", target_bir_lowering=False, num_devices=1)
    c = np.zeros((P, C_SEL + E1), np.float32)
    c[:, C_ID:C_ID + P] = np.eye(P)
    c[:, C_T:C_T + P] = np.arange(P)
    c[:, C_BP:C_BP + NT] = (np.arange(L, dtype=np.float32) / np.float32(L - 1)).reshape(NT, P).T
    c[:, C_PC] = np.arange(P) % 64
    c[:, C_DESC:C_DESC + E0] = E0 - np.arange(E0)
    c[:, C_PH] = np.where(np.arange(P) < 64, 0.75, 0.5) * 2.0 ** MANT
    c[:64, C_LO:C_LO + P] = 1.0
    c[64:, C_HI:C_HI + P] = 1.0
    c[64:96, C_BIG:C_BIG + E0] = np.eye(E0) * BIG
    c[:, C_J:C_J + P] = np.eye(P)[::-1]
    c[:, C_SEL:C_SEL + E1] = np.tile(np.eye(E1), (P // E1, 1))
    c[:, C_N3PI] = -9.424777
    arrays = {n: np.ascontiguousarray(x) for n, x in inputs.items()}
    arrays["shape_constants"] = c
    aps = {n: nc.dram_tensor("in_" + n, x.shape, mybir.dt.from_np(x.dtype), kind="ExternalInput").ap()
           for n, x in arrays.items()}
    aps["out"] = nc.dram_tensor("out_0", (B, L, D), F32, kind="ExternalOutput").ap()
    tower_kernel(nc, aps)
    r = run_bass_kernel_spmd(nc, [{"in_" + n: x for n, x in arrays.items()}], core_ids=[0])
    return r.results[0]["out_0"]
```
